# Optimizing a Trainium2 kernel written in Bass

```python
import numpy as np
import jax
import jax.numpy as jnp

def _softmax(x, axis=-1):
    return jax.nn.softmax(x, axis=axis)

def _gelu(x):
    return jax.nn.gelu(x, approximate=True)

def _silu(x):
    return jax.nn.silu(x)

def _sigmoid(x):
    return jax.nn.sigmoid(x)

def _layernorm(x, axis=-1, eps=1e-05):
    m = jnp.mean(x, axis=axis, keepdims=True)
    v = jnp.var(x, axis=axis, keepdims=True)
    return (x - m) / jnp.sqrt(v + eps)

def _scatter_add(tgt, idx, src, axis=0):
    return tgt.at[idx].add(src)

def _segment_sum(src, seg, n):
    return jax.ops.segment_sum(src, seg, n)
kernel_name = 'mk_conv_seq_d4_conv_nchw512_r4_0f64cb'

def setup_inputs(seed: int=0):
    np.random.seed(seed)
    _w = jnp.asarray

    def _rec_inputs():
        import jax
        import jax.numpy as jnp
        _gk = jax.random.key(seed)
        x = -0.0002928 + 1 * jax.random.normal(jax.random.fold_in(_gk, 1), (8, 128, 32, 32), jnp.float32)
        return x
    x = _rec_inputs()

    def _L0_conv_setup():
        import jax, jax.numpy as jnp
        import numpy as np
        NUM_HEADS = 8
        NUM_GROUPS = 32
        EPS = 1e-05
        key = jax.random.key(seed)
        ks = jax.random.split(key, 7)
        B, C, Hs, Ws = (8, 128, 32, 32)
        x = jax.random.normal(ks[0], (B, C, Hs, Ws), jnp.float32)
        gn_w = 1.0 + 0.02 * jax.random.normal(ks[1], (C,), jnp.float32)
        gn_b = 0.02 * jax.random.normal(ks[2], (C,), jnp.float32)
        qkv_w = 0.02 * jax.random.normal(ks[3], (3 * C, C), jnp.float32)
        qkv_b = 0.02 * jax.random.normal(ks[4], (3 * C,), jnp.float32)
        proj_w = 0.02 * jax.random.normal(ks[5], (C, C), jnp.float32)
        proj_b = 0.02 * jax.random.normal(ks[6], (C,), jnp.float32)
        return {'x': x, 'gn_w': gn_w, 'gn_b': gn_b, 'qkv_w': qkv_w, 'qkv_b': qkv_b, 'proj_w': proj_w, 'proj_b': proj_b}
    _L0_conv_all = _L0_conv_setup()
    _L0_conv_in = {k: v for k, v in _L0_conv_all.items() if k in ('gn_w', 'gn_b', 'qkv_w', 'qkv_b', 'proj_w', 'proj_b')}
    del _L0_conv_all

    def _L1_conv_setup():
        import math
        import jax, jax.numpy as jnp
        import numpy as np
        NUM_GROUPS = 32
        NUM_HEADS = 8
        EPS = 1e-05

        def _group_norm(x, gamma, beta):
            b, c, T = x.shape
            g = NUM_GROUPS
            xg = x.reshape(b, g, c // g * T)
            mean = xg.mean(axis=-1, keepdims=True)
            var = xg.var(axis=-1, keepdims=True)
            xg = (xg - mean) * jax.lax.rsqrt(var + EPS)
            x = xg.reshape(b, c, T)
            return x * gamma[None, :, None] + beta[None, :, None]

        def _attention(qkv, n_heads):
            bs, width, T = qkv.shape
            ch = width // (3 * n_heads)
            qkv = qkv.reshape(bs * n_heads, 3 * ch, T)
            q, k, v = (qkv[:, :ch], qkv[:, ch:2 * ch], qkv[:, 2 * ch:])
            scale = 1.0 / math.sqrt(math.sqrt(ch))
            w = jnp.einsum('bct,bcs->bts', q * scale, k * scale)
            w = jax.nn.softmax(w.astype(jnp.float32), axis=-1).astype(qkv.dtype)
            a = jnp.einsum('bts,bcs->bct', w, v)
            return a.reshape(bs, n_heads * ch, T)
        key = jax.random.key(seed)
        ks = jax.random.split(key, 5)
        C = 128
        x = jax.random.normal(ks[0], (2, C, 16, 16), dtype=jnp.float32)
        gamma = jnp.ones((C,), dtype=jnp.float32)
        beta = jnp.zeros((C,), dtype=jnp.float32)
        w_qkv = jax.random.normal(ks[1], (3 * C, C), dtype=jnp.float32) / math.sqrt(C)
        b_qkv = jax.random.normal(ks[2], (3 * C,), dtype=jnp.float32) * 0.02
        w_proj = jax.random.normal(ks[3], (C, C), dtype=jnp.float32) / math.sqrt(C)
        b_proj = jax.random.normal(ks[4], (C,), dtype=jnp.float32) * 0.02
        return {'x': x, 'gamma': gamma, 'beta': beta, 'w_qkv': w_qkv, 'b_qkv': b_qkv, 'w_proj': w_proj, 'b_proj': b_proj}
    _L1_conv_all = _L1_conv_setup()
    _L1_conv_in = {k: v for k, v in _L1_conv_all.items() if k in ('gamma', 'beta', 'w_qkv', 'b_qkv', 'w_proj', 'b_proj')}
    del _L1_conv_all

    def _L2_conv_setup():
        import jax, jax.numpy as jnp
        import numpy as np
        GROUPS = 32
        EPS = 1e-06

        def group_norm(x, gamma, beta):
            b, c, h, w = x.shape
            xg = x.reshape(b, GROUPS, c // GROUPS, h, w)
            mu = jnp.mean(xg, axis=(2, 3, 4), keepdims=True)
            var = jnp.var(xg, axis=(2, 3, 4), keepdims=True)
            xn = ((xg - mu) * jax.lax.rsqrt(var + EPS)).reshape(b, c, h, w)
            return xn * gamma[None, :, None, None] + beta[None, :, None, None]

        def conv1x1(x, w, b):
            return jnp.einsum('bchw,oc->bohw', x, w) + b[None, :, None, None]
        key = jax.random.key(seed)
        ks = jax.random.split(key, 5)
        B, C, H, W = (4, 128, 16, 16)
        s = 1.0 / np.sqrt(C)
        return {'x': jax.random.normal(ks[0], (B, C, H, W), jnp.float32), 'gn_gamma': jnp.ones((C,), jnp.float32), 'gn_beta': jnp.zeros((C,), jnp.float32), 'wq': jax.random.normal(ks[1], (C, C), jnp.float32) * s, 'bq': jnp.zeros((C,), jnp.float32), 'wk': jax.random.normal(ks[2], (C, C), jnp.float32) * s, 'bk': jnp.zeros((C,), jnp.float32), 'wv': jax.random.normal(ks[3], (C, C), jnp.float32) * s, 'bv': jnp.zeros((C,), jnp.float32), 'wp': jax.random.normal(ks[4], (C, C), jnp.float32) * s, 'bp': jnp.zeros((C,), jnp.float32)}
    _L2_conv_all = _L2_conv_setup()
    _L2_conv_in = {k: v for k, v in _L2_conv_all.items() if k in ('gn_gamma', 'gn_beta', 'wq', 'bq', 'wk', 'bk', 'wv', 'bv', 'wp', 'bp')}
    del _L2_conv_all

    def _L3_conv_setup():
        import jax, jax.numpy as jnp
        import numpy as np
        C = 128
        GROUPS = 32
        EPS = 1e-06

        def _group_norm(x, gamma, beta):
            B, Cc, H, W = x.shape
            xg = x.reshape(B, GROUPS, Cc // GROUPS, H, W)
            mean = jnp.mean(xg, axis=(2, 3, 4), keepdims=True)
            var = jnp.var(xg, axis=(2, 3, 4), keepdims=True)
            xn = (xg - mean) * jax.lax.rsqrt(var + EPS)
            xn = xn.reshape(B, Cc, H, W)
            return xn * gamma[None, :, None, None] + beta[None, :, None, None]
        key = jax.random.key(seed)
        ks = jax.random.split(key, 11)
        B, H, W = (2, 16, 16)
        x = jax.random.normal(ks[0], (B, C, H, W), dtype=jnp.float32)
        gamma = jnp.ones((C,), dtype=jnp.float32)
        beta = jnp.zeros((C,), dtype=jnp.float32)
        s = 1.0 / np.sqrt(C)
        wq = jax.random.normal(ks[1], (C, C), dtype=jnp.float32) * s
        bq = jax.random.normal(ks[2], (C,), dtype=jnp.float32) * 0.01
        wk = jax.random.normal(ks[3], (C, C), dtype=jnp.float32) * s
        bk = jax.random.normal(ks[4], (C,), dtype=jnp.float32) * 0.01
        wv = jax.random.normal(ks[5], (C, C), dtype=jnp.float32) * s
        bv = jax.random.normal(ks[6], (C,), dtype=jnp.float32) * 0.01
        wo = jax.random.normal(ks[7], (C, C), dtype=jnp.float32) * s
        bo = jax.random.normal(ks[8], (C,), dtype=jnp.float32) * 0.01
        return {'x': x, 'gamma': gamma, 'beta': beta, 'wq': wq, 'bq': bq, 'wk': wk, 'bk': bk, 'wv': wv, 'bv': bv, 'wo': wo, 'bo': bo}
    _L3_conv_all = _L3_conv_setup()
    _L3_conv_in = {k: v for k, v in _L3_conv_all.items() if k in ('gamma', 'beta', 'wq', 'bq', 'wk', 'bk', 'wv', 'bv', 'wo', 'bo')}
    del _L3_conv_all
    return {'x': x, 'L0_conv_gn_w': _L0_conv_in['gn_w'], 'L0_conv_gn_b': _L0_conv_in['gn_b'], 'L0_conv_qkv_w': _L0_conv_in['qkv_w'], 'L0_conv_qkv_b': _L0_conv_in['qkv_b'], 'L0_conv_proj_w': _L0_conv_in['proj_w'], 'L0_conv_proj_b': _L0_conv_in['proj_b'], 'L1_conv_gamma': _L1_conv_in['gamma'], 'L1_conv_beta': _L1_conv_in['beta'], 'L1_conv_w_qkv': _L1_conv_in['w_qkv'], 'L1_conv_b_qkv': _L1_conv_in['b_qkv'], 'L1_conv_w_proj': _L1_conv_in['w_proj'], 'L1_conv_b_proj': _L1_conv_in['b_proj'], 'L2_conv_gn_gamma': _L2_conv_in['gn_gamma'], 'L2_conv_gn_beta': _L2_conv_in['gn_beta'], 'L2_conv_wq': _L2_conv_in['wq'], 'L2_conv_bq': _L2_conv_in['bq'], 'L2_conv_wk': _L2_conv_in['wk'], 'L2_conv_bk': _L2_conv_in['bk'], 'L2_conv_wv': _L2_conv_in['wv'], 'L2_conv_bv': _L2_conv_in['bv'], 'L2_conv_wp': _L2_conv_in['wp'], 'L2_conv_bp': _L2_conv_in['bp'], 'L3_conv_gamma': _L3_conv_in['gamma'], 'L3_conv_beta': _L3_conv_in['beta'], 'L3_conv_wq': _L3_conv_in['wq'], 'L3_conv_bq': _L3_conv_in['bq'], 'L3_conv_wk': _L3_conv_in['wk'], 'L3_conv_bk': _L3_conv_in['bk'], 'L3_conv_wv': _L3_conv_in['wv'], 'L3_conv_bv': _L3_conv_in['bv'], 'L3_conv_wo': _L3_conv_in['wo'], 'L3_conv_bo': _L3_conv_in['bo']}

def reference(x, L0_conv_gn_w, L0_conv_gn_b, L0_conv_qkv_w, L0_conv_qkv_b, L0_conv_proj_w, L0_conv_proj_b, L1_conv_gamma, L1_conv_beta, L1_conv_w_qkv, L1_conv_b_qkv, L1_conv_w_proj, L1_conv_b_proj, L2_conv_gn_gamma, L2_conv_gn_beta, L2_conv_wq, L2_conv_bq, L2_conv_wk, L2_conv_bk, L2_conv_wv, L2_conv_bv, L2_conv_wp, L2_conv_bp, L3_conv_gamma, L3_conv_beta, L3_conv_wq, L3_conv_bq, L3_conv_wk, L3_conv_bk, L3_conv_wv, L3_conv_bv, L3_conv_wo, L3_conv_bo):
    import jax
    import jax.numpy as jnp

    def _L0_conv_ref(x, gn_w, gn_b, qkv_w, qkv_b, proj_w, proj_b):
        import jax, jax.numpy as jnp
        import numpy as np
        NUM_HEADS = 8
        NUM_GROUPS = 32
        EPS = 1e-05
        B, C = (x.shape[0], x.shape[1])
        T = int(np.prod(x.shape[2:]))
        xr = x.reshape(B, C, T)
        g = xr.reshape(B, NUM_GROUPS, -1)
        mu = g.mean(axis=-1, keepdims=True)
        var = g.var(axis=-1, keepdims=True)
        h = ((g - mu) * jax.lax.rsqrt(var + EPS)).reshape(B, C, T)
        h = h * gn_w[:, None] + gn_b[:, None]
        qkv = jnp.einsum('oc,bct->bot', qkv_w, h) + qkv_b[:, None]
        ch = C // NUM_HEADS
        qkv = qkv.reshape(B * NUM_HEADS, 3 * ch, T)
        q, k, v = (qkv[:, :ch], qkv[:, ch:2 * ch], qkv[:, 2 * ch:])
        scale = 1.0 / jnp.sqrt(jnp.sqrt(jnp.asarray(ch, q.dtype)))
        w = jnp.einsum('bct,bcs->bts', q * scale, k * scale)
        w = jax.nn.softmax(w.astype(jnp.float32), axis=-1).astype(q.dtype)
        a = jnp.einsum('bts,bcs->bct', w, v).reshape(B, C, T)
        out = jnp.einsum('oc,bct->bot', proj_w, a) + proj_b[:, None]
        return (xr + out).reshape(x.shape)

    def _L1_conv_ref(x, gamma, beta, w_qkv, b_qkv, w_proj, b_proj):
        import math
        import jax, jax.numpy as jnp
        import numpy as np
        NUM_GROUPS = 32
        NUM_HEADS = 8
        EPS = 1e-05

        def _group_norm(x, gamma, beta):
            b, c, T = x.shape
            g = NUM_GROUPS
            xg = x.reshape(b, g, c // g * T)
            mean = xg.mean(axis=-1, keepdims=True)
            var = xg.var(axis=-1, keepdims=True)
            xg = (xg - mean) * jax.lax.rsqrt(var + EPS)
            x = xg.reshape(b, c, T)
            return x * gamma[None, :, None] + beta[None, :, None]

        def _attention(qkv, n_heads):
            bs, width, T = qkv.shape
            ch = width // (3 * n_heads)
            qkv = qkv.reshape(bs * n_heads, 3 * ch, T)
            q, k, v = (qkv[:, :ch], qkv[:, ch:2 * ch], qkv[:, 2 * ch:])
            scale = 1.0 / math.sqrt(math.sqrt(ch))
            w = jnp.einsum('bct,bcs->bts', q * scale, k * scale)
            w = jax.nn.softmax(w.astype(jnp.float32), axis=-1).astype(qkv.dtype)
            a = jnp.einsum('bts,bcs->bct', w, v)
            return a.reshape(bs, n_heads * ch, T)
        b, c = x.shape[:2]
        spatial = x.shape[2:]
        xf = x.reshape(b, c, -1)
        h = _group_norm(xf, gamma, beta)
        qkv = jnp.einsum('oc,bct->bot', w_qkv, h) + b_qkv[None, :, None]
        h = _attention(qkv, NUM_HEADS)
        h = jnp.einsum('oc,bct->bot', w_proj, h) + b_proj[None, :, None]
        return (xf + h).reshape(b, c, *spatial)

    def _L2_conv_ref(x, gn_gamma, gn_beta, wq, bq, wk, bk, wv, bv, wp, bp):
        import jax, jax.numpy as jnp
        import numpy as np
        GROUPS = 32
        EPS = 1e-06

        def group_norm(x, gamma, beta):
            b, c, h, w = x.shape
            xg = x.reshape(b, GROUPS, c // GROUPS, h, w)
            mu = jnp.mean(xg, axis=(2, 3, 4), keepdims=True)
            var = jnp.var(xg, axis=(2, 3, 4), keepdims=True)
            xn = ((xg - mu) * jax.lax.rsqrt(var + EPS)).reshape(b, c, h, w)
            return xn * gamma[None, :, None, None] + beta[None, :, None, None]

        def conv1x1(x, w, b):
            return jnp.einsum('bchw,oc->bohw', x, w) + b[None, :, None, None]
        b, c, h, w = x.shape
        h_ = group_norm(x, gn_gamma, gn_beta)
        q = conv1x1(h_, wq, bq).reshape(b, c, h * w)
        k = conv1x1(h_, wk, bk).reshape(b, c, h * w)
        v = conv1x1(h_, wv, bv).reshape(b, c, h * w)
        scale = jnp.asarray(c, x.dtype) ** (-0.5)
        scores = jnp.einsum('bci,bcj->bij', q, k) * scale
        attn = jax.nn.softmax(scores, axis=-1)
        out = jnp.einsum('bcj,bij->bci', v, attn).reshape(b, c, h, w)
        out = conv1x1(out, wp, bp)
        return x + out

    def _L3_conv_ref(x, gamma, beta, wq, bq, wk, bk, wv, bv, wo, bo):
        import jax, jax.numpy as jnp
        import numpy as np
        C = 128
        GROUPS = 32
        EPS = 1e-06

        def _group_norm(x, gamma, beta):
            B, Cc, H, W = x.shape
            xg = x.reshape(B, GROUPS, Cc // GROUPS, H, W)
            mean = jnp.mean(xg, axis=(2, 3, 4), keepdims=True)
            var = jnp.var(xg, axis=(2, 3, 4), keepdims=True)
            xn = (xg - mean) * jax.lax.rsqrt(var + EPS)
            xn = xn.reshape(B, Cc, H, W)
            return xn * gamma[None, :, None, None] + beta[None, :, None, None]
        B, Cc, H, W = x.shape
        N = H * W
        h = _group_norm(x, gamma, beta).reshape(B, Cc, N)
        q = jnp.einsum('oc,bcn->bon', wq, h) + bq[None, :, None]
        k = jnp.einsum('oc,bcn->bon', wk, h) + bk[None, :, None]
        v = jnp.einsum('oc,bcn->bon', wv, h) + bv[None, :, None]
        scale = Cc ** (-0.5)
        attn = jnp.einsum('bcn,bcm->bnm', q, k) * scale
        attn = jax.nn.softmax(attn, axis=-1)
        out = jnp.einsum('bcm,bnm->bcn', v, attn)
        proj = jnp.einsum('oc,bcn->bon', wo, out) + bo[None, :, None]
        return x + proj.reshape(B, Cc, H, W)

    def _gn(v, G=32, eps=1e-05):
        B_, C_, H_, W_ = v.shape
        g = v.reshape(B_, G, C_ // G, H_, W_)
        m = jnp.mean(g, axis=(2, 3, 4), keepdims=True)
        s = jnp.var(g, axis=(2, 3, 4), keepdims=True)
        return ((g - m) / jnp.sqrt(s + eps)).reshape(v.shape)

    def _ln_c(v, eps=1e-06):
        m = jnp.mean(v, axis=1, keepdims=True)
        s = jnp.var(v, axis=1, keepdims=True)
        return (v - m) / jnp.sqrt(s + eps)

    def _ln_t(v, eps=1e-05):
        m = jnp.mean(v, axis=-1, keepdims=True)
        s = jnp.var(v, axis=-1, keepdims=True)
        return (v - m) / jnp.sqrt(s + eps)

    def _to_tokens(v):
        B_, C_, H_, W_ = v.shape
        return v.reshape(B_, C_, H_ * W_).transpose(0, 2, 1)

    def _from_tokens(t, like):
        B_, C_, H_, W_ = like.shape
        return t.transpose(0, 2, 1).reshape(B_, C_, H_, W_)
    x = _L0_conv_ref(x, L0_conv_gn_w, L0_conv_gn_b, L0_conv_qkv_w, L0_conv_qkv_b, L0_conv_proj_w, L0_conv_proj_b)
    x = _L1_conv_ref(x, L1_conv_gamma, L1_conv_beta, L1_conv_w_qkv, L1_conv_b_qkv, L1_conv_w_proj, L1_conv_b_proj)
    x = _L2_conv_ref(x, L2_conv_gn_gamma, L2_conv_gn_beta, L2_conv_wq, L2_conv_bq, L2_conv_wk, L2_conv_bk, L2_conv_wv, L2_conv_bv, L2_conv_wp, L2_conv_bp)
    x = _L3_conv_ref(x, L3_conv_gamma, L3_conv_beta, L3_conv_wq, L3_conv_bq, L3_conv_wk, L3_conv_bk, L3_conv_wv, L3_conv_bv, L3_conv_wo, L3_conv_bo)
    return x

_drawn_inputs = setup_inputs


def setup_inputs(seed=0):
    import zlib

    import numpy as np

    out = dict(_drawn_inputs(seed))
    spreads = {'L1_conv_gamma': (1.0, 0.6),
     'L1_conv_beta': (0.0, 0.8),
     'L2_conv_gn_gamma': (1.0, 0.6),
     'L2_conv_gn_beta': (0.0, 0.8),
     'L2_conv_bq': (0.0, 2.0),
     'L2_conv_bk': (0.0, 2.0),
     'L2_conv_bv': (0.0, 0.8),
     'L2_conv_bp': (0.0, 0.8),
     'L3_conv_gamma': (1.0, 0.6),
     'L3_conv_beta': (0.0, 0.8)}
    factors = {'L0_conv_gn_w': 8.0,
     'L0_conv_gn_b': 8.0,
     'L0_conv_qkv_w': 8.0,
     'L0_conv_qkv_b': 5.279,
     'L0_conv_proj_w': 4.956,
     'L3_conv_bq': 64.0,
     'L3_conv_bk': 200.0,
     'L3_conv_bv': 44.024,
     'L3_conv_bo': 200.0,
     'L0_conv_proj_b': 8.0,
     'L1_conv_w_qkv': 4.703,
     'L1_conv_b_qkv': 8.0,
     'L1_conv_w_proj': 4.559,
     'L1_conv_b_proj': 8.0,
     'L2_conv_wq': 6.159,
     'L2_conv_wk': 5.484,
     'L2_conv_wv': 4.471,
     'L2_conv_wp': 4.067,
     'L3_conv_wq': 5.61,
     'L3_conv_wk': 5.428,
     'L3_conv_wv': 4.472,
     'L3_conv_wo': 4.05}
    for name, (base, spread) in spreads.items():
        noise = np.random.default_rng([zlib.crc32(name.encode()), seed]).standard_normal(out[name].shape)
        drawn = base * np.exp(spread * noise) if base else spread * noise
        out[name] = jnp.asarray(drawn.astype(out[name].dtype))
    for name, factor in factors.items():
        out[name] = (out[name] * factor).astype(out[name].dtype)
    return out
```

```python
from contextlib import ExitStack

import concourse.bass as bass
from concourse import mybir

ALU = mybir.AluOpType
ACT = mybir.ActivationFunctionType
AX = mybir.AxisListType
F32 = mybir.dt.float32
BF16 = mybir.dt.bfloat16

P = 128
T = 1024
B = 8
HALF = 512
TILES = T // P
GROUP = 4
HEADS = 8
CH = P // HEADS
QUAD = 4
TERMS = 6
KS = TERMS * CH
KM = KS + 3

W_Q, W_K, W_V, W_GAMMA, W_BETA, W_BQ, W_BK = 0, P, 2 * P, 3 * P, 3 * P + 1, 3 * P + 2, 3 * P + 3
NG = 3 * P + 4
W_P, W_BP = NG, NG + P
NO = P + 1


def set_up_constants(nc, pool, gmat, ident, ready):
    nc.gpsimd.memset(gmat[:, :], 1.0 / GROUP).then_inc(ready, 1)
    pool.wait_ge(ready, 1)
    blocks = gmat[:, :].rearrange("p (g r) -> p g r", r=GROUP)
    nc.gpsimd.affine_select(out=blocks, in_=blocks, compare_op=ALU.is_ge, fill=0.0, base=0,
                            pattern=[[-GROUP, P // GROUP], [0, GROUP]], channel_multiplier=1).then_inc(ready, 1)
    pool.wait_ge(ready, 2)
    nc.gpsimd.affine_select(out=blocks, in_=blocks, compare_op=ALU.is_ge, fill=0.0, base=GROUP - 1,
                            pattern=[[GROUP, P // GROUP], [0, GROUP]], channel_multiplier=-1).then_inc(ready, 1)
    nc.gpsimd.memset(ident[:, :], 0.0).then_inc(ready, 1)
    pool.wait_ge(ready, 4)
    nc.gpsimd.affine_select(out=ident[:, :], in_=ident[:, :], compare_op=ALU.not_equal, fill=1.0, base=0,
                            pattern=[[-1, P]], channel_multiplier=1).then_inc(ready, 1)


class Own:

    def __init__(self, eng, sem):
        self.eng, self.sem, self.n = eng, sem, 0

    def mark(self, instruction):
        instruction.then_inc(self.sem, 1)
        self.n += 1

    def wait(self):
        self.eng.wait_ge(self.sem, self.n)

    def done(self, instruction):
        self.mark(instruction)
        self.wait()

    def drain(self):
        self.eng.sem_inc(self.sem, -self.n)
        self.n = 0


def many_heads(nc, ctx0, x, w, bv, out):
    EPS = 1e-5
    GROUPS = 2 * TILES
    UNITS = QUAD * TILES
    MH = UNITS // 2
    AVG, MAX1, K0, K1, Q0, Q1, V0, V1, MAX0, O0, O1 = 0, 1, 3, 4, 5, 6, 8, 9, 12, 14, 15
    PAIRS = 2 * B // 2
    CONSTS = 13

    ctx = ExitStack()
    with ctx:
        def sb(name, shape, dt=F32):
            return ctx.enter_context(nc.sbuf_tensor("h_" + name, shape, dt))

        def psum(name, shape):
            return ctx.enter_context(nc.psum_tensor("h_" + name, shape, F32))

        def sem(name):
            return ctx0.enter_context(nc.semaphore("h_" + name))

        qrep = [sb(f"qrep{i}", [P, 2, HEADS, HALF], BF16) for i in range(2)]
        krep = [sb(f"krep{i}", [P, HEADS, T], BF16) for i in range(2)]
        vT = [sb(f"vT{i}", [P, TILES, HEADS, 32]) for i in range(2)]
        probs = [sb(f"probs{i}", [P, QUAD, HALF]) for i in range(2)]
        den_dram = nc.dram_tensor("den_dram", (HEADS, T), F32).ap()
        rden_dram = nc.dram_tensor("rden_dram", (HEADS, T), F32).ap()
        x_in = sb("x_in", [P, T])
        x_res = sb("x_res", [P, T])
        wg = sb("wg", [P, NG])
        wo = sb("wo", [P, NO])
        bvb = sb("bvb", [P, P])
        h = sb("h", [P, T])
        full = {"q": sb("qf", [P, T]), "k": sb("kf", [P, T])}
        parts = {"q": sb("qp", [P, 3, T], BF16), "k": sb("kp", [P, 3, T], BF16)}
        rest = sb("rest", [P, T])
        av = [sb(f"av{i}", [P, T]) for i in range(2)]
        num = sb("num", [P, T])
        den = sb("den", [P, HEADS * T // P])
        rden = sb("rden", [P, HEADS * T // P])
        rrep = sb("rrep", [P, T])
        attn = sb("attn", [P, T])
        y = sb("y", [P, T])
        nmax = sb("nmax", [P, UNITS])
        nrest = sb("nrest", [P, MH])
        nparts = [sb(f"nparts{i}", [P, 3, MH], BF16) for i in range(2)]
        mrow = [sb(f"mrow{i}", [3 * MH, P], BF16) for i in range(2)]
        gmat = sb("gmat", [P, P])
        ident = sb("ident", [P, P], BF16)
        bst = sb("bst", [P, 2, 6])
        mv = sb("mv", [P, 2])
        st2 = sb("st2", [P, 2])
        gs = sb("gs", [P, 2])
        co = sb("co", [P, 6])
        exponent = sb("exponent", [P, 1])

        s_ps = [psum(f"s{i}", [P, 2, HALF]) for i in range(2)]
        st_ps = [psum(f"st{i}", [P, HALF]) for i in range(2)]
        pv_ps = psum("pv", [P, HALF])
        misc = psum("misc", [P, HALF])
        misc_bf = misc[:, :].bitcast(BF16)

        consts = sem("consts")
        max_done = sem("max_done")
        scores_ready = sem("scores_ready")
        st_ready = sem("st_ready")
        exp_done = sem("exp_done")
        pv_done = sem("pv_done")
        pv_free = sem("pv_free")
        misc_act = sem("misc_act")
        misc_dve = sem("misc_dve")
        misc_for_act = sem("misc_for_act")
        misc_for_dve = sem("misc_for_dve")
        stats_ready = sem("stats_ready")
        coef_ready = sem("coef_ready")
        scale_ready = sem("scale_ready")
        h_ready = sem("h_ready")
        evacuated = sem("evacuated")
        parts_ready = sem("parts_ready")
        parts_free = sem("parts_free")
        rep_ready = sem("rep_ready")
        nmax_ready = sem("nmax_ready")
        nparts_ready = sem("nparts_ready")
        mrow_dma = sem("mrow_dma")
        av_ready = sem("av_ready")
        av_free = sem("av_free")
        o_in = sem("o_in")
        den_ready = sem("den_ready")
        rden_ready = sem("rden_ready")
        attn_ready = sem("attn_ready")
        y_ready = sem("y_ready")
        g_in = sem("g_in")
        rep_dma, load_dma, av_dma, den_dma, copy_dma, store_dma = (
            sem(n) for n in ("rep_dma", "load_dma", "av_dma", "den_dma", "copy_dma", "store_dma"))
        act_own, dve_own, pool_own = sem("act_own"), sem("dve_own"), sem("pool_own")

        block = ctx.enter_context(nc.Block())

        @block.sync
        def _(sp):
            def load_g(row, layer):
                sp.dma_start(x_in[:, :], row).then_inc(load_dma, 16)
                sp.dma_start(wg[:, :], w[layer, :, 0:NG]).then_inc(load_dma, 16)
                sp.dma_start(bvb[:, :], bv[layer, :, :].to_broadcast([P, P])).then_inc(load_dma, 16)

            def replicate(par, u):
                sp.wait_ge(parts_ready, 2 * u + 1)
                for term, part in enumerate((0, 1, 2, 0, 1, 0)):
                    sp.dma_start(krep[par][term * CH:(term + 1) * CH, :, :], parts["k"][:, part, :]).then_inc(rep_dma, 16)
                sp.wait_ge(parts_ready, 2 * u + 2)
                for term, part in enumerate((0, 0, 0, 1, 1, 2)):
                    for th in range(2):
                        sp.dma_start(qrep[par][term * CH:(term + 1) * CH, th, :, :],
                                     parts["q"][:, part, th * HALF:(th + 1) * HALF]).then_inc(rep_dma, 16)
                sp.wait_ge(rep_dma, 16 * 3 * TERMS)
                sp.sem_inc(rep_dma, -16 * 3 * TERMS)
                sp.sem_inc(rep_ready, 1)
                sp.sem_inc(parts_free, 1)

            def gather(quad):
                sp.dma_start(den_dram[quad * QUAD:(quad + 1) * QUAD, :], av[quad][CH:P:32, :]).then_inc(av_dma, 16)
                for j in range(QUAD):
                    to = (quad * QUAD + j) * CH
                    sp.dma_start(num[to:to + CH, :], av[quad][32 * j:32 * j + CH, :]).then_inc(av_dma, 16)

            load_g(x[0, :, :], 0)
            sp.wait_ge(load_dma, 48)
            sp.sem_inc(load_dma, -48)
            sp.sem_inc(g_in, 1)
            for b in range(B):
                sp.dma_start(out[b, :, :], x[b, :, :]).then_inc(copy_dma, 16)
            replicate(0, 0)
            sp.sem_inc(parts_ready, -2)
            sp.wait_ge(av_ready, 1)
            sp.sem_inc(av_ready, -1)
            gather(0)
            sp.wait_ge(y_ready, 1)
            sp.sem_inc(y_ready, -1)
            load_g(x[1, :, :], 0)
            sp.wait_ge(load_dma, 48)
            sp.sem_inc(load_dma, -48)
            sp.wait_ge(copy_dma, 16 * B)
            sp.sem_inc(g_in, 1)

            def last_output(row):
                gather(1)
                sp.dma_start(x_res[:, :], row).then_inc(load_dma, 16)
                sp.wait_ge(av_dma, 16 * 2 * (QUAD + 1))
                sp.sem_inc(av_dma, -16 * 2 * (QUAD + 1))
                sp.sem_inc(av_free, 1)
                sp.dma_start(den[:, :], den_dram.rearrange("h (p t) -> (h p) t", p=CH)).then_inc(den_dma, 16)
                sp.wait_ge(den_dma, 16)
                sp.sem_inc(den_dma, -16)
                sp.sem_inc(den_ready, 1)

            def spread():
                sp.dma_start(rden_dram.rearrange("h (p t) -> (h p) t", p=CH), rden[:, :]).then_inc(den_dma, 16)
                sp.wait_ge(den_dma, 16)
                sp.dma_start(rrep[:, :], rden_dram.rearrange("h (a t) -> h a t", a=1).to_broadcast([HEADS, CH, T])).then_inc(den_dma, 16)
                sp.wait_ge(load_dma, 16)
                sp.sem_inc(load_dma, -16)
                sp.wait_ge(den_dma, 32)
                sp.sem_inc(den_dma, -32)
                sp.sem_inc(o_in, 1)

            with sp.Fori(0, PAIRS) as pair:
                for u in range(2):
                    i = 2 * pair + u
                    sp.wait_ge(av_ready, 2 * u + 1)
                    last_output(out[(i + B - 1) % B, :, :])
                    sp.wait_ge(rden_ready, u + 1)
                    spread()
                    replicate(1 - u, u)
                    sp.wait_ge(y_ready, 2 * (u + 1))
                    sp.dma_start(out[(i + B - 1) % B, :, :], y[:, :]).then_inc(store_dma, 16)
                    load_g(out[(i + 2) % B, :, :], (i + 2) // B)
                    sp.dma_start(wo[:, :], w[i // B, :, W_P:W_P + NO]).then_inc(load_dma, 16)
                    sp.wait_ge(store_dma, 16)
                    sp.sem_inc(store_dma, -16)
                    sp.wait_ge(load_dma, 64)
                    sp.sem_inc(load_dma, -64)
                    sp.sem_inc(g_in, 1)
                    sp.wait_ge(av_ready, 2 * u + 2)
                    gather(0)
                sp.sem_inc(parts_ready, -4)
                sp.sem_inc(av_ready, -4)
                sp.sem_inc(rden_ready, -2)
                sp.sem_inc(y_ready, -4)
            sp.wait_ge(av_ready, 1)
            last_output(out[B - 1, :, :])
            sp.wait_ge(rden_ready, 1)
            spread()
            sp.wait_ge(y_ready, 2)
            sp.dma_start(out[B - 1, :, :], y[:, :]).then_inc(store_dma, 16)
            sp.wait_ge(store_dma, 16)

        @block.gpsimd
        def _(pool):
            own = Own(pool, pool_own)
            set_up_constants(nc, pool, gmat, ident, consts)
            n = 5
            for i in range(2):
                for part, value in ((vT[i][:, :, :, CH:32], 1.0), (krep[i][KS:KM, :, :], 1.0), (av[i][:, :], 1.0)):
                    pool.wait_ge(consts, n)
                    nc.gpsimd.memset(part, value).then_inc(consts, 1)
                    n += 1
            pool.wait_ge(consts, n)
            nc.gpsimd.memset(wo[:, :], 0.0).then_inc(consts, 1)
            pool.wait_ge(consts, n + 1)
            nc.gpsimd.memset(exponent[:, :], -0.5).then_inc(consts, 1)
            pool.wait_ge(consts, CONSTS)

            def split(n, which):
                pool.wait_ge(evacuated, n)
                tt, whole, (lead, middle, last) = nc.gpsimd.tensor_tensor, full[which][:, :], (parts[which][:, p, :] for p in range(3))
                own.done(tt(middle, whole, lead, ALU.subtract))
                own.done(tt(rest[:, :], whole, lead, ALU.subtract))
                own.done(tt(last, rest[:, :], middle, ALU.subtract))
                pool.sem_inc(parts_ready, 1)

            def stage_g(u):
                pool.wait_ge(coef_ready, u + 1)
                tt = nc.gpsimd.tensor_tensor
                own.done(tt(co[:, 4:5], co[:, 1:2], exponent[:, :], ALU.pow))
                own.done(tt(co[:, 2:3], co[:, 4:5], wg[:, W_GAMMA:W_GAMMA + 1], ALU.mult))
                own.done(tt(co[:, 5:6], gs[:, 0:1], co[:, 2:3], ALU.mult))
                tt(co[:, 3:4], wg[:, W_BETA:W_BETA + 1], co[:, 5:6], ALU.subtract).then_inc(scale_ready, 1)
                split(2 * u + 1, "k")
                split(2 * u + 2, "q")

            def normalise(n):
                pool.wait_ge(o_in, n)
                nc.gpsimd.tensor_tensor(attn[:, :], num[:, :], rrep[:, :], ALU.mult).then_inc(attn_ready, 1)

            def split_max(n, th):
                pool.wait_ge(nmax_ready, n)
                new, to = nmax[:, th * MH:(th + 1) * MH], nparts[th]
                own.done(nc.gpsimd.tensor_scalar(to[:, 0, :], new, 1.0, None, ALU.mult))
                own.done(nc.gpsimd.tensor_tensor(nrest[:, :], new, to[:, 0, :], ALU.subtract))
                own.done(nc.gpsimd.tensor_scalar(to[:, 1, :], nrest[:, :], 1.0, None, ALU.mult))
                own.done(nc.gpsimd.tensor_tensor(to[:, 2, :], nrest[:, :], to[:, 1, :], ALU.subtract))
                pool.sem_inc(nparts_ready, 1)

            pool.sem_inc(av_ready, 2)
            stage_g(0)
            pool.sem_inc(coef_ready, -1)
            pool.sem_inc(evacuated, -2)
            split_max(1, 0)
            pool.sem_inc(nmax_ready, -1)
            own.drain()
            with pool.Fori(0, PAIRS):
                for u in range(2):
                    split_max(4 * u + 1, 1)
                    stage_g(u)
                    normalise(u + 1)
                    split_max(4 * u + 2, 0)
                    split_max(4 * u + 3, 1)
                    split_max(4 * u + 4, 0)
                pool.sem_inc(coef_ready, -2)
                pool.sem_inc(evacuated, -4)
                pool.sem_inc(nmax_ready, -8)
                pool.sem_inc(o_in, -2)
                own.drain()
            normalise(1)

        @block.vector
        def _(dve):
            own = Own(dve, dve_own)

            def statistics(n):
                dve.wait_ge(g_in, n)
                for c in range(2):
                    own.mark(nc.vector.bn_stats(bst[:, c, :], x_in[:, c * HALF:(c + 1) * HALF]))
                own.wait()
                own.done(nc.vector.bn_aggr(mv[:, :], bst[:, :, :]))
                own.mark(nc.vector.tensor_copy(st2[:, 0:1], mv[:, 0:1]))
                nc.vector.scalar_tensor_tensor(out=st2[:, 1:2], in0=mv[:, 0:1], scalar=mv[:, 0:1], in1=mv[:, 1:2],
                                               op0=ALU.mult, op1=ALU.add).then_inc(stats_ready, 1)

            def coefficients(n):
                dve.wait_ge(misc_for_dve, n)
                own.done(nc.vector.tensor_copy(gs[:, :], misc[:, 0:2]))
                dve.sem_inc(misc_dve, 1)
                own.done(nc.vector.scalar_tensor_tensor(out=co[:, 0:1], in0=gs[:, 0:1], scalar=gs[:, 0:1],
                                                        in1=gs[:, 1:2], op0=ALU.mult, op1=ALU.subtract))
                nc.vector.tensor_scalar(co[:, 1:2], co[:, 0:1], -1.0, EPS, ALU.mult, ALU.add).then_inc(coef_ready, 1)

            def values(n, par, c, last=None):
                dve.wait_ge(misc_for_dve, n)
                nc.vector.tensor_tensor(
                    vT[par][:, 4 * c:4 * c + 4, :, 0:CH],
                    misc[:, :].rearrange("p (s h c) -> p s h c", s=4, h=HEADS),
                    bvb[:, :].rearrange("p (a h c) -> p a h c", a=1, h=HEADS).to_broadcast([P, 4, HEADS, CH]),
                    ALU.add).then_inc(misc_dve, 1)

            def invert(n):
                dve.wait_ge(den_ready, n)
                nc.vector.reciprocal(rden[:, :], den[:, :]).then_inc(rden_ready, 1)

            def output(n, c):
                dve.wait_ge(misc_for_dve, n)
                own.done(nc.vector.scalar_tensor_tensor(
                    out=y[:, c * HALF:(c + 1) * HALF], in0=misc[:, :], scalar=wo[:, P:P + 1],
                    in1=x_res[:, c * HALF:(c + 1) * HALF], op0=ALU.add, op1=ALU.add))
                if c == 0:
                    dve.sem_inc(misc_dve, 1)
                dve.sem_inc(y_ready, 1)

            def maximum(n, unit):
                dve.wait_ge(scores_ready, n + 1)
                reduce = nc.vector.tensor_reduce(nmax[:, unit:unit + 1], s_ps[n % 2][:, :, :], AX.XY, ALU.max, negate=True)
                if unit % MH != MH - 1:
                    reduce.then_inc(max_done, 1)
                else:
                    own.done(reduce)
                    dve.sem_inc(max_done, 1)
                    dve.sem_inc(nmax_ready, 1)

            statistics(1)
            coefficients(1)
            values(2, 0, 0)
            dve.wait_ge(misc_for_dve, 3)
            own.done(nc.vector.tensor_tensor(
                vT[0][:, 4:8, :, 0:CH], misc[:, :].rearrange("p (s h c) -> p s h c", s=4, h=HEADS),
                bvb[:, :].rearrange("p (a h c) -> p a h c", a=1, h=HEADS).to_broadcast([P, 4, HEADS, CH]), ALU.add))
            dve.sem_inc(misc_dve, 1)
            dve.sem_inc(y_ready, 1)
            dve.sem_inc(g_in, -1)
            dve.sem_inc(misc_for_dve, -3)
            for unit in range(UNITS):
                maximum(unit, unit)
            dve.sem_inc(scores_ready, -UNITS)
            own.drain()
            with dve.Fori(0, PAIRS):
                for s in range(4):
                    u = s // 2
                    for k in range(GROUPS):
                        if s % 2 == 0:
                            base = 5 * u
                            if k == 0:
                                statistics(u + 1)
                            if k == AVG + 1:
                                coefficients(base + 1)
                            if k == 5:
                                invert(u + 1)
                            if k == V0 + 1:
                                values(base + 2, 1 - u, 0)
                            if k == V1 + 1:
                                values(base + 3, 1 - u, 1)
                            if k == O0 + 1:
                                output(base + 4, 0)
                        for unit in (2 * k, 2 * k + 1):
                            maximum(UNITS * s + unit, unit)
                    if s % 2 == 0:
                        output(5 * u + 5, 1)
                dve.sem_inc(g_in, -2)
                dve.sem_inc(misc_for_dve, -10)
                dve.sem_inc(den_ready, -2)
                dve.sem_inc(scores_ready, -4 * UNITS)
                own.drain()
            invert(1)
            output(1, 0)
            output(2, 1)

        @block.scalar
        def _(act):
            own = Own(act, act_own)

            def evacuate(n, which, c, hold=False):
                act.wait_ge(misc_for_act, n)
                bias = wg[:, W_BQ:W_BQ + 1] if which == "q" else wg[:, W_BK:W_BK + 1]
                cols = slice(c * HALF, (c + 1) * HALF)
                own.mark(nc.scalar.activation(full[which][:, cols], misc[:, :], ACT.Identity, bias=bias))

            def leading(which, c):
                cols = slice(c * HALF, (c + 1) * HALF)
                own.mark(nc.scalar.copy(parts[which][:, 0, cols], full[which][:, cols]))

            def normalise(c):
                cols = slice(c * HALF, (c + 1) * HALF)
                nc.scalar.activation(h[:, cols], x_in[:, cols], ACT.Identity, bias=co[:, 3:4],
                                     scale=co[:, 2:3]).then_inc(h_ready, 1)

            def max_rows(n, th):
                act.wait_ge(misc_for_act, n)
                own.mark(nc.scalar.copy(mrow[th][:, :], misc_bf[0:3 * MH, 0:P]))

            def send_max_rows(step, th):
                own.wait()
                act.sem_inc(misc_act, 1)
                par, quad = step // 2 % 2, step % 2
                act.dma_start(qrep[par][KS:KM, th, quad * QUAD:(quad + 1) * QUAD, :],
                              mrow[th][:, :]).then_inc(mrow_dma, 16)

            def sums(n, quad, th):
                act.wait_ge(pv_done, n + 2)
                own.mark(nc.scalar.copy(av[quad][:, th * HALF:(th + 1) * HALF], pv_ps[:, :]))

            act.wait_ge(scale_ready, 1)
            act.sem_inc(scale_ready, -1)
            normalise(0)
            normalise(1)
            for n, (which, c) in enumerate((("k", 0), ("k", 1), ("q", 0), ("q", 1))):
                evacuate(n + 1, which, c)
                own.wait()
                act.sem_inc(misc_act, 1)
                leading(which, c)
                own.wait()
                if c == 1:
                    act.sem_inc(evacuated, 1)
            max_rows(5, 0)
            send_max_rows(0, 0)
            act.sem_inc(misc_for_act, -5)
            own.drain()
            act.sem_inc(pv_free, 1)
            act.wait_ge(consts, CONSTS)
            with act.Fori(0, PAIRS):
                for s in range(4):
                    u, quad = s // 2, s % 2
                    base = 8 * u + 6 * quad
                    order = [MAX1, MAX0] if quad else [MAX1, K0, K1, Q0, Q1, MAX0]
                    for k in range(GROUPS):
                        g = GROUPS * s + k
                        act.wait_ge(pv_done, g + 1)
                        for j in range(QUAD):
                            n = QUAD * g + j
                            act.wait_ge(st_ready, n + 1)
                            nc.scalar.activation(probs[g % 2][:, j, :], st_ps[j % 2][:, :], ACT.Exp,
                                                 scale=1.0 / CH ** 0.5).then_inc(exp_done, 1)
                            if j == 0 and k - 1 in order:
                                if k - 1 == MAX1:
                                    send_max_rows(s, 1)
                                elif k - 1 == MAX0:
                                    send_max_rows(s + 1, 0)
                                else:
                                    own.wait()
                                    act.sem_inc(misc_act, 1)
                            if j == 1 and k - 1 in (K0, K1, Q0, Q1) and quad == 0:
                                leading("k" if k - 1 in (K0, K1) else "q", (k - 1 - K0) % 2)
                            if j == 3 and k - 1 in (K1, Q1) and quad == 0:
                                own.wait()
                                act.sem_inc(evacuated, 1)
                            if j % 2 == 1 and k == K0 - 1 and quad == 0:
                                if j == 1:
                                    act.wait_ge(scale_ready, u + 1)
                                normalise(j // 2)
                            if j == 0 and k == TILES + 1:
                                if quad == 0:
                                    act.wait_ge(av_free, u + 1)
                                sums(g - 1, quad, 0)
                            if j == 1 and k == TILES + 1:
                                own.wait()
                                act.sem_inc(pv_free, 1)
                        if k in order:
                            n = base + order.index(k) + 1
                            if k in (MAX0, MAX1):
                                max_rows(n, 1 if k == MAX1 else 0)
                            else:
                                if k == K0:
                                    act.wait_ge(parts_free, u + 1)
                                evacuate(n, "k" if k in (K0, K1) else "q", (k - K0) % 2)
                    sums(GROUPS * (s + 1), quad, 1)
                    own.wait()
                    act.sem_inc(pv_free, 1)
                    act.sem_inc(av_ready, 1)
                act.sem_inc(misc_for_act, -16)
                act.sem_inc(pv_done, -4 * GROUPS)
                act.sem_inc(st_ready, -4 * GROUPS * QUAD)
                act.sem_inc(av_free, -2)
                act.sem_inc(scale_ready, -2)
                act.sem_inc(parts_free, -2)
                own.drain()

        @block.tensor
        def _(pe):
            def project(c, column, ready):
                nc.tensor.matmul(misc[:, :], wg[:, column:column + P], h[:, c * HALF:(c + 1) * HALF],
                                 start=True, stop=True).then_inc(ready, 1)

            def project_values(c):
                for n in range(4):
                    t = 4 * c + n
                    last = nc.tensor.matmul(misc[:, n * P:(n + 1) * P], h[:, t * P:(t + 1) * P],
                                            wg[:, W_V:W_V + P], start=True, stop=True)
                last.then_inc(misc_for_dve, 1)

            def project_output(c):
                nc.tensor.matmul(misc[:, :], wo[:, 0:P], attn[:, c * HALF:(c + 1) * HALF],
                                 start=True, stop=True).then_inc(misc_for_dve, 1)

            def average():
                nc.tensor.matmul(misc[:, 0:2], gmat[:, :], st2[:, :], start=True, stop=True).then_inc(misc_for_dve, 1)

            def transpose_max(th):
                nc.tensor.transpose(misc_bf[0:3 * MH, 0:P], nparts[th][:, :, :].rearrange("p a b -> p (a b)"),
                                    ident[:, :]).then_inc(misc_for_act, 1)

            def row_scores(n, par, quad, unit, halves=(0, 1)):
                th, head, tile = unit // MH, quad * QUAD + unit % MH // (TILES // 2), unit % (TILES // 2)
                for c in halves:
                    last = nc.tensor.matmul(s_ps[n % 2][:, c, :], qrep[par][0:KS, th, head, tile * P:(tile + 1) * P],
                                            krep[par][0:KS, head, c * HALF:(c + 1) * HALF], start=True, stop=True)
                if 1 in halves:
                    last.then_inc(scores_ready, 1)

            pe.sem_inc(pv_done, 2)
            pe.wait_ge(consts, CONSTS)
            pe.wait_ge(stats_ready, 1)
            average()
            pe.wait_ge(misc_dve, 1)
            pe.wait_ge(h_ready, 2)
            project(0, W_K, misc_for_act)
            pe.wait_ge(misc_act, 1)
            project(1, W_K, misc_for_act)
            pe.wait_ge(misc_act, 2)
            project(0, W_Q, misc_for_act)
            pe.wait_ge(misc_act, 3)
            project(1, W_Q, misc_for_act)
            pe.wait_ge(misc_act, 4)
            project_values(0)
            pe.wait_ge(misc_dve, 2)
            project_values(1)
            pe.wait_ge(misc_dve, 3)
            pe.wait_ge(rep_ready, 1)
            for unit in range(UNITS):
                if unit >= 2:
                    pe.wait_ge(max_done, unit - 1)
                row_scores(unit, 0, 0, unit)
            pe.wait_ge(nparts_ready, 1)
            transpose_max(0)
            pe.sem_inc(stats_ready, -1)
            pe.sem_inc(misc_dve, -3)
            pe.sem_inc(h_ready, -2)
            pe.sem_inc(misc_act, -4)
            pe.sem_inc(rep_ready, -1)
            pe.sem_inc(max_done, -(UNITS - 2))
            pe.sem_inc(nparts_ready, -1)

            with pe.Fori(0, PAIRS):
                for s in range(4):
                    u, quad = s // 2, s % 2
                    par = u
                    mpar, mquad = (s + 1) // 2 % 2, (s + 1) % 2
                    a, d = 8 * u, 4 * u
                    if quad == 1:
                        pe.wait_ge(rep_ready, u + 1)

                    def products(k):
                        g = GROUPS * s + k
                        pe.wait_ge(exp_done, QUAD * (g + 1))
                        if k % TILES == 0:
                            pe.wait_ge(pv_free, 2 * s + k // TILES + 1)
                        for j in range(QUAD):
                            last = nc.tensor.matmul(pv_ps[32 * j:32 * j + 32, :],
                                                    vT[par][:, k % TILES, quad * QUAD + j, :], probs[g % 2][:, j, :],
                                                    start=(k % TILES == 0), stop=(k % TILES == TILES - 1))
                        last.then_inc(pv_done, 1)

                    def in_shared_bank(k):
                        if k == MAX1:
                            if quad == 0:
                                pe.wait_ge(misc_dve, d + 1)
                            pe.wait_ge(nparts_ready, 2 * s + 1)
                            transpose_max(1)
                        elif k == MAX0:
                            if quad == 0:
                                pe.wait_ge(misc_dve, d + 3)
                            else:
                                pe.wait_ge(misc_act, a + 8)
                            pe.wait_ge(nparts_ready, 2 * s + 2)
                            transpose_max(0)
                        elif quad == 1:
                            pass
                        elif k == AVG:
                            pe.wait_ge(misc_act, a + 1)
                            pe.wait_ge(stats_ready, u + 1)
                            average()
                        elif k == K0:
                            pe.wait_ge(misc_act, a + 2)
                            pe.wait_ge(h_ready, 2 * (u + 1))
                            project(0, W_K, misc_for_act)
                        elif k == K1:
                            pe.wait_ge(misc_act, a + 3)
                            project(1, W_K, misc_for_act)
                        elif k == Q0:
                            pe.wait_ge(misc_act, a + 4)
                            project(0, W_Q, misc_for_act)
                        elif k == Q1:
                            pe.wait_ge(misc_act, a + 5)
                            project(1, W_Q, misc_for_act)
                        elif k == V0:
                            pe.wait_ge(misc_act, a + 6)
                            project_values(0)
                        elif k == V1:
                            pe.wait_ge(misc_dve, d + 2)
                            project_values(1)
                        elif k == O0:
                            pe.wait_ge(misc_act, a + 7)
                            pe.wait_ge(attn_ready, u + 1)
                            project_output(0)
                        elif k == O1:
                            pe.wait_ge(misc_dve, d + 4)
                            project_output(1)

                    def m_unit(unit, half):
                        if half == 0:
                            pe.wait_ge(max_done, UNITS * s + unit + 1)
                        row_scores(unit, mpar, mquad, unit, (half,))

                    m_unit(0, 0)
                    for k in range(GROUPS):
                        th, st = k // TILES, k % TILES
                        if st == 0:
                            pe.wait_ge(mrow_dma, 16 * (2 * s + th + 1))
                        for j in range(QUAD):
                            n = QUAD * (GROUPS * s + k) + j
                            head = quad * QUAD + j
                            if n >= 2:
                                pe.wait_ge(exp_done, n - 1)
                            nc.tensor.matmul(st_ps[j % 2][:, :], krep[par][0:KM, head, st * P:(st + 1) * P],
                                             qrep[par][0:KM, th, head, :],
                                             start=True, stop=True).then_inc(st_ready, 1)
                            if j == 0:
                                m_unit(2 * k, 1)
                                m_unit(2 * k + 1, 0)
                            if j == 1:
                                m_unit(2 * k + 1, 1)
                                in_shared_bank(k)
                            if j == 2 and k >= 1:
                                products(k - 1)
                            if j == 3 and k < GROUPS - 1:
                                m_unit(2 * k + 2, 0)
                    products(GROUPS - 1)
                pe.sem_inc(mrow_dma, -16 * 8)
                pe.sem_inc(rep_ready, -2)
                pe.sem_inc(exp_done, -4 * GROUPS * QUAD)
                pe.sem_inc(max_done, -4 * UNITS)
                pe.sem_inc(pv_free, -8)
                pe.sem_inc(stats_ready, -2)
                pe.sem_inc(misc_act, -16)
                pe.sem_inc(misc_dve, -8)
                pe.sem_inc(h_ready, -4)
                pe.sem_inc(nparts_ready, -8)
                pe.sem_inc(attn_ready, -2)
            pe.wait_ge(mrow_dma, 16)
            pe.wait_ge(misc_act, 1)
            pe.wait_ge(attn_ready, 1)
            project_output(0)
            pe.wait_ge(misc_dve, 1)
            project_output(1)


def one_head(nc, ctx0, w, bv, out, x=None):
    EPS = 1e-6
    SCALE = float(P) ** -0.5
    HT = TILES // 2
    PAIRS = 2 * B // 2
    BODY = 2 * TILES
    AVG, O0, K0, K1, Q0, Q1, V0, V1, O1 = (0, 0), (0, 1), (1, 1), (2, 0), (2, 1), (3, 0), (3, 1), (4, 0), (5, 0)
    x_first = out if x is None else x

    ctx = ExitStack()
    with ctx:
        def sb(name, shape, dt=F32):
            return ctx.enter_context(nc.sbuf_tensor("o_" + name, shape, dt))

        def psum(name, shape):
            return ctx.enter_context(nc.psum_tensor("o_" + name, shape, F32))

        def sem(name):
            return ctx0.enter_context(nc.semaphore("o_" + name))

        q = [sb(f"q{i}", [P, T]) for i in range(2)]
        k = [sb(f"k{i}", [P, T]) for i in range(2)]
        vT = [sb(f"vT{i}", [P, TILES, P]) for i in range(2)]
        probs = [sb(f"probs{i}", [P, T]) for i in range(2)]
        pT = [sb(f"pT{i}", [P, TILES, HALF]) for i in range(2)]
        x_in = sb("x_in", [P, T])
        x_res = sb("x_res", [P, T])
        wg = sb("wg", [P, NG])
        wo = sb("wo", [P, NO])
        bvb = sb("bvb", [P, P])
        h = sb("h", [P, T])
        attn = sb("attn", [P, T])
        y = sb("y", [P, T])
        gmat = sb("gmat", [P, P])
        ident_bf = sb("ident_bf", [P, P], BF16)
        ident = sb("ident", [P, P])
        bst = sb("bst", [P, 2, 6])
        mv = sb("mv", [P, 2])
        st2 = sb("st2", [P, 2])
        gs = sb("gs", [P, 2])
        co = sb("co", [P, 6])
        exponent = sb("exponent", [P, 1])
        nmax = sb("nmax", [P, 2])
        bias = sb("bias", [P, 2])
        rsum = sb("rsum", [P, 2])
        rinv = sb("rinv", [P, 2])

        s_ps = [psum(f"s{i}", [P, 2, HALF]) for i in range(2)]
        t_ps = [psum(f"t{i}", [P, HT, P]) for i in range(2)]
        pv_ps = psum("pv", [P, HALF])
        misc = psum("misc", [P, HALF])

        consts = sem("consts")
        s_ready = sem("s_ready")
        bias_ready = sem("bias_ready")
        exp_ready = sem("exp_ready")
        p_ready = sem("p_ready")
        t_for_act = sem("t_for_act")
        t_for_dve = sem("t_for_dve")
        pt_act = sem("pt_act")
        pt_dve = sem("pt_dve")
        pv_ready = sem("pv_ready")
        attn_ready = sem("attn_ready")
        misc_act = sem("misc_act")
        misc_dve = sem("misc_dve")
        misc_for_act = sem("misc_for_act")
        misc_for_dve = sem("misc_for_dve")
        stats_ready = sem("stats_ready")
        coef_ready = sem("coef_ready")
        scale_ready = sem("scale_ready")
        h_ready = sem("h_ready")
        loaded = sem("loaded")
        y_ready = sem("y_ready")
        load_dma, store_dma = sem("load_dma"), sem("store_dma")
        act_own, dve_own, pool_own = sem("act_own"), sem("dve_own"), sem("pool_own")

        block = ctx.enter_context(nc.Block())

        @block.sync
        def _(sp):
            def load_g(row, layer):
                sp.dma_start(x_in[:, :], row).then_inc(load_dma, 16)
                sp.dma_start(wg[:, :], w[layer, :, 0:NG]).then_inc(load_dma, 16)
                sp.dma_start(bvb[:, :], bv[layer, :, :].to_broadcast([P, P])).then_inc(load_dma, 16)

            def landed(n):
                sp.wait_ge(load_dma, 16 * n)
                sp.sem_inc(load_dma, -16 * n)
                sp.sem_inc(loaded, 1)

            load_g(x_first[0, :, :], 2)
            landed(3)
            sp.wait_ge(y_ready, 1)
            sp.sem_inc(y_ready, -1)
            load_g(x_first[1, :, :], 2)
            sp.dma_start(x_res[:, :], x_first[B - 1, :, :]).then_inc(load_dma, 16)
            landed(4)
            with sp.Fori(0, PAIRS) as pair:
                for u in range(2):
                    i = 2 * pair + u
                    sp.wait_ge(y_ready, 2 * (u + 1))
                    sp.dma_start(out[(i + B - 1) % B, :, :], y[:, :]).then_inc(store_dma, 16)
                    load_g(out[(i + 2) % B, :, :], ((i + 2) // B + 2) % 4)
                    sp.dma_start(x_res[:, :], out[i % B, :, :]).then_inc(load_dma, 16)
                    sp.dma_start(wo[:, :], w[i // B + 2, :, W_P:W_P + NO]).then_inc(load_dma, 16)
                    sp.wait_ge(store_dma, 16)
                    sp.sem_inc(store_dma, -16)
                    landed(5)
                sp.sem_inc(y_ready, -4)
            sp.wait_ge(y_ready, 2)
            sp.dma_start(out[B - 1, :, :], y[:, :]).then_inc(store_dma, 16)
            sp.wait_ge(store_dma, 16)

        @block.gpsimd
        def _(pool):
            own = Own(pool, pool_own)
            set_up_constants(nc, pool, gmat, ident_bf, consts)
            n = 5
            for part, value in ((exponent[:, :], -0.5), (wo[:, :], 0.0), (attn[:, :], 0.0), (vT[1][:, :, :], 0.0),
                                (pT[1][:, :, :], 0.0)):
                pool.wait_ge(consts, n)
                nc.gpsimd.memset(part, value).then_inc(consts, 1)
                n += 1
            pool.wait_ge(consts, n)
            nc.gpsimd.tensor_scalar(ident[:, :], ident_bf[:, :], 1.0, None, ALU.mult).then_inc(consts, 1)

            def stage_g(u):
                pool.wait_ge(coef_ready, u + 1)
                tt = nc.gpsimd.tensor_tensor
                own.done(tt(co[:, 4:5], co[:, 1:2], exponent[:, :], ALU.pow))
                own.done(tt(co[:, 2:3], co[:, 4:5], wg[:, W_GAMMA:W_GAMMA + 1], ALU.mult))
                own.done(tt(co[:, 5:6], gs[:, 0:1], co[:, 2:3], ALU.mult))
                tt(co[:, 3:4], wg[:, W_BETA:W_BETA + 1], co[:, 5:6], ALU.subtract).then_inc(scale_ready, 1)

            stage_g(0)
            pool.sem_inc(coef_ready, -1)
            own.drain()
            with pool.Fori(0, PAIRS):
                stage_g(0)
                stage_g(1)
                pool.sem_inc(coef_ready, -2)
                own.drain()

        @block.vector
        def _(dve):
            own = Own(dve, dve_own)

            def statistics(n):
                dve.wait_ge(loaded, n)
                for c in range(2):
                    own.mark(nc.vector.bn_stats(bst[:, c, :], x_in[:, c * HALF:(c + 1) * HALF]))
                own.wait()
                own.done(nc.vector.bn_aggr(mv[:, :], bst[:, :, :]))
                own.done(nc.vector.tensor_copy(st2[:, 0:1], mv[:, 0:1]))
                nc.vector.scalar_tensor_tensor(out=st2[:, 1:2], in0=mv[:, 0:1], scalar=mv[:, 0:1], in1=mv[:, 1:2],
                                               op0=ALU.mult, op1=ALU.add).then_inc(stats_ready, 1)

            def coefficients(n):
                dve.wait_ge(misc_for_dve, n)
                own.done(nc.vector.tensor_copy(gs[:, :], misc[:, 0:2]))
                dve.sem_inc(misc_dve, 1)
                own.done(nc.vector.scalar_tensor_tensor(out=co[:, 0:1], in0=gs[:, 0:1], scalar=gs[:, 0:1],
                                                        in1=gs[:, 1:2], op0=ALU.mult, op1=ALU.subtract))
                nc.vector.tensor_scalar(co[:, 1:2], co[:, 0:1], -1.0, EPS, ALU.mult, ALU.add).then_inc(coef_ready, 1)

            def values(n, par, c):
                dve.wait_ge(misc_for_dve, n)
                return nc.vector.tensor_tensor(
                    vT[par][:, 4 * c:4 * c + 4, :], misc[:, :].rearrange("p (s c) -> p s c", s=4),
                    bvb[:, :].rearrange("p (a c) -> p a c", a=1).to_broadcast([P, 4, P]), ALU.add)

            def output(n, c):
                dve.wait_ge(misc_for_dve, n)
                own.done(nc.vector.scalar_tensor_tensor(
                    out=y[:, c * HALF:(c + 1) * HALF], in0=misc[:, :], scalar=wo[:, P:P + 1],
                    in1=x_res[:, c * HALF:(c + 1) * HALF], op0=ALU.add, op1=ALU.add))
                dve.sem_inc(misc_dve, 1)
                dve.sem_inc(y_ready, 1)

            def maximum(n, tile):
                dve.wait_ge(s_ready, n)
                b = tile % 2
                own.done(nc.vector.tensor_reduce(nmax[:, b:b + 1], s_ps[b][:, :, :], AX.XY, ALU.max, negate=True))
                nc.vector.tensor_scalar(bias[:, b:b + 1], nmax[:, b:b + 1], SCALE, None, ALU.mult).then_inc(bias_ready, 1)

            def divide(n, tile):
                dve.wait_ge(exp_ready, n)
                b = tile % 2
                own.done(nc.vector.reciprocal(rinv[:, b:b + 1], rsum[:, b:b + 1]))
                nc.vector.tensor_scalar(probs[b][:, :], probs[b][:, :], rinv[:, b:b + 1], None,
                                        ALU.mult).then_inc(p_ready, 1)

            statistics(1)
            coefficients(1)
            values(2, 0, 0).then_inc(misc_dve, 1)
            dve.wait_ge(misc_for_dve, 3)
            own.done(values(3, 0, 1))
            dve.sem_inc(misc_dve, 1)
            dve.sem_inc(y_ready, 1)
            dve.sem_inc(loaded, -1)
            dve.sem_inc(misc_for_dve, -3)
            maximum(1, 0)
            divide(1, 0)
            dve.sem_inc(s_ready, -1)
            dve.sem_inc(exp_ready, -1)
            own.drain()
            with dve.Fori(0, PAIRS):
                for m in range(BODY):
                    u, tile = m // TILES, m % TILES
                    base = 5 * u
                    if tile == 0:
                        statistics(u + 1)
                    maximum(m + 1, m + 1)
                    if tile == AVG[0]:
                        coefficients(base + 1)
                        output(base + 2, 0)
                    if tile == V0[0]:
                        values(base + 3, 1 - u, 0).then_inc(misc_dve, 1)
                    if tile == V1[0]:
                        values(base + 4, 1 - u, 1).then_inc(misc_dve, 1)
                    if tile == O1[0]:
                        output(base + 5, 1)
                    dve.wait_ge(t_for_dve, m + 1)
                    nc.vector.tensor_copy(pT[m // HT % 2][:, HT:TILES, m % HT * P:(m % HT + 1) * P],
                                          t_ps[1][:, :, :]).then_inc(pt_dve, 1)
                    divide(m + 1, m + 1)
                dve.sem_inc(loaded, -2)
                dve.sem_inc(misc_for_dve, -10)
                dve.sem_inc(s_ready, -BODY)
                dve.sem_inc(exp_ready, -BODY)
                dve.sem_inc(t_for_dve, -BODY)
                own.drain()
            dve.wait_ge(loaded, 1)
            dve.sem_inc(stats_ready, 1)
            output(1, 0)
            output(2, 1)

        @block.scalar
        def _(act):
            def normalise(c):
                cols = slice(c * HALF, (c + 1) * HALF)
                nc.scalar.activation(h[:, cols], x_in[:, cols], ACT.Identity, bias=co[:, 3:4],
                                     scale=co[:, 2:3]).then_inc(h_ready, 1)

            def evacuate(n, to, c, column):
                act.wait_ge(misc_for_act, n)
                nc.scalar.activation(to[:, c * HALF:(c + 1) * HALF], misc[:, :], ACT.Identity,
                                     bias=wg[:, column:column + 1]).then_inc(misc_act, 1)

            def exponentials(n, tile):
                act.wait_ge(bias_ready, n)
                b = tile % 2
                nc.scalar.activation(probs[b][:, :], s_ps[b][:, :, :], ACT.Exp, bias=bias[:, b:b + 1], scale=SCALE,
                                     accum_out=rsum[:, b:b + 1]).then_inc(exp_ready, 1)

            def products(n, c):
                act.wait_ge(pv_ready, n)
                nc.scalar.copy(attn[:, c * HALF:(c + 1) * HALF], pv_ps[:, :]).then_inc(attn_ready, 1)

            act.wait_ge(scale_ready, 1)
            act.sem_inc(scale_ready, -1)
            normalise(0)
            normalise(1)
            evacuate(1, k[0], 0, W_BK)
            evacuate(2, k[0], 1, W_BK)
            evacuate(3, q[0], 0, W_BQ)
            evacuate(4, q[0], 1, W_BQ)
            act.sem_inc(misc_for_act, -4)
            exponentials(1, 0)
            act.sem_inc(bias_ready, -1)
            act.wait_ge(consts, 11)
            with act.Fori(0, PAIRS):
                for m in range(BODY):
                    u, tile = m // TILES, m % TILES
                    base = 4 * u
                    exponentials(m + 1, m + 1)
                    if tile == K1[0]:
                        evacuate(base + 2, k[1 - u], 1, W_BK)
                    if tile == Q1[0]:
                        evacuate(base + 4, q[1 - u], 1, W_BQ)
                    if tile % HT == HT - 1:
                        products(m // HT + 1, 1 if tile < HT else 0)
                    if tile == K0[0]:
                        evacuate(base + 1, k[1 - u], 0, W_BK)
                    if tile == Q0[0]:
                        evacuate(base + 3, q[1 - u], 0, W_BQ)
                    act.wait_ge(t_for_act, m + 1)
                    nc.scalar.copy(pT[m // HT % 2][:, 0:HT, m % HT * P:(m % HT + 1) * P],
                                   t_ps[0][:, :, :]).then_inc(pt_act, 1)
                    if tile == AVG[0]:
                        act.wait_ge(scale_ready, u + 1)
                        normalise(0)
                        normalise(1)
                act.sem_inc(bias_ready, -BODY)
                act.sem_inc(misc_for_act, -8)
                act.sem_inc(pv_ready, -4)
                act.sem_inc(t_for_act, -BODY)
                act.sem_inc(scale_ready, -2)
            products(1, 1)

        @block.tensor
        def _(pe):
            def project(c, column):
                nc.tensor.matmul(misc[:, :], wg[:, column:column + P], h[:, c * HALF:(c + 1) * HALF],
                                 start=True, stop=True).then_inc(misc_for_act, 1)

            def project_values(c):
                for n in range(4):
                    t = 4 * c + n
                    last = nc.tensor.matmul(misc[:, n * P:(n + 1) * P], h[:, t * P:(t + 1) * P],
                                            wg[:, W_V:W_V + P], start=True, stop=True)
                last.then_inc(misc_for_dve, 1)

            def project_output(c):
                nc.tensor.matmul(misc[:, :], wo[:, 0:P], attn[:, c * HALF:(c + 1) * HALF],
                                 start=True, stop=True).then_inc(misc_for_dve, 1)

            def average():
                nc.tensor.matmul(misc[:, 0:2], gmat[:, :], st2[:, :], start=True, stop=True).then_inc(misc_for_dve, 1)

            def scores(par, n):
                tile = n % TILES
                for c in range(2):
                    last = nc.tensor.matmul(s_ps[n % 2][:, c, :], q[par][:, tile * P:(tile + 1) * P],
                                            k[par][:, c * HALF:(c + 1) * HALF], start=True, stop=True)
                last.then_inc(s_ready, 1)

            def products(half, quarter):
                for st in (2 * quarter, 2 * quarter + 1):
                    last = nc.tensor.matmul(pv_ps[:, :], vT[half // 2 % 2][:, st, :], pT[half % 2][:, st, :],
                                            start=(st == 0), stop=(st == TILES - 1))
                if quarter == 3:
                    last.then_inc(pv_ready, 1)

            pe.sem_inc(pt_act, 1)
            pe.sem_inc(pt_dve, 1)
            pe.sem_inc(attn_ready, 1)
            pe.wait_ge(consts, 11)
            pe.wait_ge(stats_ready, 1)
            average()
            pe.wait_ge(misc_dve, 1)
            pe.wait_ge(h_ready, 2)
            project(0, W_K)
            pe.wait_ge(misc_act, 1)
            project(1, W_K)
            pe.wait_ge(misc_act, 2)
            project(0, W_Q)
            pe.wait_ge(misc_act, 3)
            project(1, W_Q)
            pe.wait_ge(misc_act, 4)
            scores(0, 0)
            project_values(0)
            pe.wait_ge(misc_dve, 2)
            project_values(1)
            pe.sem_inc(stats_ready, -1)
            pe.sem_inc(misc_dve, -2)
            pe.sem_inc(h_ready, -2)
            pe.sem_inc(misc_act, -4)
            with pe.Fori(0, PAIRS):
                for m in range(BODY):
                    u, tile = m // TILES, m % TILES
                    a, d = 4 * u, 5 * u

                    def in_shared_bank(slot):
                        if slot == AVG:
                            pe.wait_ge(misc_dve, d + 1)
                            pe.wait_ge(stats_ready, u + 1)
                            average()
                        elif slot == O0:
                            pe.wait_ge(misc_dve, d + 2)
                            project_output(0)
                        elif slot == K0:
                            pe.wait_ge(misc_dve, d + 3)
                            pe.wait_ge(h_ready, 2 * (u + 1))
                            project(0, W_K)
                        elif slot == K1:
                            pe.wait_ge(misc_act, a + 1)
                            project(1, W_K)
                        elif slot == Q0:
                            pe.wait_ge(misc_act, a + 2)
                            project(0, W_Q)
                        elif slot == Q1:
                            pe.wait_ge(misc_act, a + 3)
                            project(1, W_Q)
                        elif slot == V0:
                            pe.wait_ge(misc_act, a + 4)
                            project_values(0)
                        elif slot == V1:
                            pe.wait_ge(misc_dve, d + 4)
                            project_values(1)
                        elif slot == O1:
                            pe.wait_ge(misc_dve, d + 5)
                            project_output(1)

                    scores((m + 1) // TILES % 2, m + 1)
                    in_shared_bank((tile, 0))
                    if m % HT == 0:
                        pe.wait_ge(pt_act, m + 1)
                        pe.wait_ge(pt_dve, m + 1)
                        pe.wait_ge(attn_ready, m // HT + 1)
                    products((m // HT + 3) % 4, m % HT)
                    in_shared_bank((tile, 1))
                    pe.wait_ge(p_ready, m + 1)
                    for bank, taken in ((0, pt_act), (1, pt_dve)):
                        pe.wait_ge(taken, m + 1)
                        for n in range(HT):
                            st = bank * HT + n
                            last = nc.tensor.transpose(t_ps[bank][:, n, :], probs[m % 2][:, st * P:(st + 1) * P], ident[:, :])
                        last.then_inc(t_for_dve if bank else t_for_act, 1)
                pe.sem_inc(pt_act, -BODY)
                pe.sem_inc(pt_dve, -BODY)
                pe.sem_inc(attn_ready, -4)
                pe.sem_inc(p_ready, -BODY)
                pe.sem_inc(stats_ready, -2)
                pe.sem_inc(misc_dve, -10)
                pe.sem_inc(misc_act, -8)
                pe.sem_inc(h_ready, -4)
            pe.wait_ge(pt_act, 1)
            pe.wait_ge(pt_dve, 1)
            pe.wait_ge(attn_ready, 1)
            for quarter in range(4):
                products(3, quarter)
            pe.wait_ge(misc_dve, 1)
            pe.wait_ge(stats_ready, 1)
            project_output(0)
            pe.wait_ge(misc_dve, 2)
            pe.wait_ge(attn_ready, 2)
            project_output(1)


def layout(inputs):
    import numpy as np

    def column(a):
        return np.asarray(a).reshape(P, 1)

    stack, rows = [], []
    for gamma, beta, qkv_w, qkv_b, proj_w, proj_b in (
        ("L0_conv_gn_w", "L0_conv_gn_b", "L0_conv_qkv_w", "L0_conv_qkv_b", "L0_conv_proj_w", "L0_conv_proj_b"),
        ("L1_conv_gamma", "L1_conv_beta", "L1_conv_w_qkv", "L1_conv_b_qkv", "L1_conv_w_proj", "L1_conv_b_proj"),
    ):
        wqkv = np.asarray(inputs[qkv_w]).reshape(HEADS, 3, CH, P)
        bqkv = np.asarray(inputs[qkv_b]).reshape(HEADS, 3, CH)
        wq, wk = (wqkv[:, n].transpose(2, 1, 0).reshape(P, P) for n in (0, 1))
        wv = wqkv[:, 2].transpose(2, 0, 1).reshape(P, P)
        bq, bk = (bqkv[:, n].transpose(1, 0).reshape(P, 1) for n in (0, 1))
        stack.append(np.concatenate([wq, wk, wv, column(inputs[gamma]), column(inputs[beta]), bq, bk,
                                     np.asarray(inputs[proj_w]).T, column(inputs[proj_b])], axis=1))
        rows.append(bqkv[:, 2].reshape(1, P))
    for names in (
        ("L2_conv_wq", "L2_conv_wk", "L2_conv_wv", "L2_conv_gn_gamma", "L2_conv_gn_beta", "L2_conv_bq", "L2_conv_bk",
         "L2_conv_wp", "L2_conv_bp", "L2_conv_bv"),
        ("L3_conv_wq", "L3_conv_wk", "L3_conv_wv", "L3_conv_gamma", "L3_conv_beta", "L3_conv_bq", "L3_conv_bk",
         "L3_conv_wo", "L3_conv_bo", "L3_conv_bv"),
    ):
        a = [np.asarray(inputs[n]) for n in names]
        stack.append(np.concatenate([m.T if m.ndim == 2 else column(m) for m in a[:-1]], axis=1))
        rows.append(a[-1].reshape(1, P))
    return np.stack(stack), np.stack(rows)


def program(nc, x, w, bv, out):
    with ExitStack() as ctx:
        many_heads(nc, ctx, x, w, bv, out)
        one_head(nc, ctx, w, bv, out)


def kernel(**inputs):
    import numpy as np
    import concourse.bacc as bacc
    from concourse.bass_utils import run_bass_kernel_spmd

    x = np.ascontiguousarray(np.asarray(inputs["x"]).reshape(B, P, T))
    w, bv = layout(inputs)
    arrays = {"x_dram": x, "w_dram": w, "bv_dram": bv}
    nc = bacc.Bacc("TRN2", target_bir_lowering=False, num_devices=1)
    args = [nc.dram_tensor(name, a.shape, F32, kind="ExternalInput").ap() for name, a in arrays.items()]
    out = nc.dram_tensor("out_dram", (B, P, T), F32, kind="ExternalOutput").ap()
    program(nc, *args, out)
    result = run_bass_kernel_spmd(nc, [arrays], core_ids=[0])
    return result.results[0]["out_dram"].reshape(np.asarray(inputs["x"]).shape)
```

```python
from contextlib import ExitStack

import concourse.bass as bass
from concourse import mybir

ALU = mybir.AluOpType
ACT = mybir.ActivationFunctionType
AX = mybir.AxisListType
F32 = mybir.dt.float32
BF16 = mybir.dt.bfloat16
F32R = mybir.dt.float32r

P = 128
T = 1024
B = 8
HALF = 512
TILES = T // P
GROUP = 4
HEADS = 8
CH = P // HEADS
QUAD = 4
TERMS = 6
KS = TERMS * CH
KM = KS + 3

W_Q, W_K, W_V, W_GAMMA, W_BETA, W_BQ, W_BK = 0, P, 2 * P, 3 * P, 3 * P + 1, 3 * P + 2, 3 * P + 3
NG = 3 * P + 4
W_P, W_BP = NG, NG + P
NO = P + 1


def set_up_constants(nc, pool, gmat, ident, ready):
    nc.gpsimd.memset(gmat[:, :], 1.0 / GROUP).then_inc(ready, 1)
    pool.wait_ge(ready, 1)
    blocks = gmat[:, :].rearrange("p (g r) -> p g r", r=GROUP)
    nc.gpsimd.affine_select(out=blocks, in_=blocks, compare_op=ALU.is_ge, fill=0.0, base=0,
                            pattern=[[-GROUP, P // GROUP], [0, GROUP]], channel_multiplier=1).then_inc(ready, 1)
    pool.wait_ge(ready, 2)
    nc.gpsimd.affine_select(out=blocks, in_=blocks, compare_op=ALU.is_ge, fill=0.0, base=GROUP - 1,
                            pattern=[[GROUP, P // GROUP], [0, GROUP]], channel_multiplier=-1).then_inc(ready, 1)
    nc.gpsimd.memset(ident[:, :], 0.0).then_inc(ready, 1)
    pool.wait_ge(ready, 4)
    nc.gpsimd.affine_select(out=ident[:, :], in_=ident[:, :], compare_op=ALU.not_equal, fill=1.0, base=0,
                            pattern=[[-1, P]], channel_multiplier=1).then_inc(ready, 1)


class Own:

    def __init__(self, eng, sem):
        self.eng, self.sem, self.n = eng, sem, 0

    def mark(self, instruction):
        instruction.then_inc(self.sem, 1)
        self.n += 1

    def wait(self):
        self.eng.wait_ge(self.sem, self.n)

    def done(self, instruction):
        self.mark(instruction)
        self.wait()

    def drain(self):
        self.eng.sem_inc(self.sem, -self.n)
        self.n = 0


def many_heads(nc, ctx0, x, w, bv, out):
    EPS = 1e-5
    GROUPS = 2 * TILES
    UNITS = QUAD * TILES
    MH = UNITS // 2
    AVG, MAX1, K0, K1, Q0, Q1, V0, V1, MAX0, O0, O1 = 0, 1, 3, 4, 5, 6, 8, 9, 12, 14, 15
    PAIRS = 2 * B // 2
    CONSTS = 13

    ctx = ExitStack()
    with ctx:
        def sb(name, shape, dt=F32):
            return ctx.enter_context(nc.sbuf_tensor("h_" + name, shape, dt))

        def psum(name, shape):
            return ctx.enter_context(nc.psum_tensor("h_" + name, shape, F32))

        def sem(name):
            return ctx0.enter_context(nc.semaphore("h_" + name))

        qrep = [sb(f"qrep{i}", [P, 2, HEADS, HALF], BF16) for i in range(2)]
        krep = [sb(f"krep{i}", [P, HEADS, T], BF16) for i in range(2)]
        vT = [sb(f"vT{i}", [P, TILES, HEADS, 32]) for i in range(2)]
        probs = [sb(f"probs{i}", [P, QUAD, HALF]) for i in range(2)]
        den_dram = nc.dram_tensor("den_dram", (HEADS, T), F32).ap()
        rden_dram = nc.dram_tensor("rden_dram", (HEADS, T), F32).ap()
        x_in = sb("x_in", [P, T])
        x_res = sb("x_res", [P, T])
        wg = sb("wg", [P, NG])
        wo = sb("wo", [P, NO])
        bvb = sb("bvb", [P, P])
        h = sb("h", [P, T])
        full = {"q": sb("qf", [P, T]), "k": sb("kf", [P, T])}
        parts = {"q": sb("qp", [P, 3, T], BF16), "k": sb("kp", [P, 3, T], BF16)}
        rest = sb("rest", [P, T])
        av = [sb(f"av{i}", [P, T]) for i in range(2)]
        num = sb("num", [P, T])
        den = sb("den", [P, HEADS * T // P])
        rden = sb("rden", [P, HEADS * T // P])
        rrep = sb("rrep", [P, T])
        attn = sb("attn", [P, T])
        y = sb("y", [P, T])
        nmax = sb("nmax", [P, UNITS])
        nrest = sb("nrest", [P, MH])
        nparts = [sb(f"nparts{i}", [P, 3, MH], BF16) for i in range(2)]
        mrow = [sb(f"mrow{i}", [3 * MH, P], BF16) for i in range(2)]
        gmat = sb("gmat", [P, P])
        ident = sb("ident", [P, P], BF16)
        bst = sb("bst", [P, 2, 6])
        mv = sb("mv", [P, 2])
        st2 = sb("st2", [P, 2])
        gs = sb("gs", [P, 2])
        co = sb("co", [P, 6])
        exponent = sb("exponent", [P, 1])

        s_ps = [psum(f"s{i}", [P, 2, HALF]) for i in range(2)]
        st_ps = [psum(f"st{i}", [P, HALF]) for i in range(2)]
        pv_ps = psum("pv", [P, HALF])
        misc = psum("misc", [P, HALF])
        misc_bf = misc[:, :].bitcast(BF16)

        consts = sem("consts")
        max_done = sem("max_done")
        scores_ready = sem("scores_ready")
        st_ready = sem("st_ready")
        exp_done = sem("exp_done")
        pv_done = sem("pv_done")
        pv_free = sem("pv_free")
        misc_act = sem("misc_act")
        misc_dve = sem("misc_dve")
        misc_for_act = sem("misc_for_act")
        misc_for_dve = sem("misc_for_dve")
        stats_ready = sem("stats_ready")
        coef_ready = sem("coef_ready")
        scale_ready = sem("scale_ready")
        h_ready = sem("h_ready")
        evacuated = sem("evacuated")
        parts_ready = sem("parts_ready")
        parts_free = sem("parts_free")
        rep_ready = sem("rep_ready")
        nmax_ready = sem("nmax_ready")
        nparts_ready = sem("nparts_ready")
        mrow_dma = sem("mrow_dma")
        av_ready = sem("av_ready")
        av_free = sem("av_free")
        o_in = sem("o_in")
        den_ready = sem("den_ready")
        rden_ready = sem("rden_ready")
        attn_ready = sem("attn_ready")
        y_ready = sem("y_ready")
        g_in = sem("g_in")
        rep_dma, load_dma, av_dma, den_dma, copy_dma, store_dma = (
            sem(n) for n in ("rep_dma", "load_dma", "av_dma", "den_dma", "copy_dma", "store_dma"))
        act_own, dve_own, pool_own = sem("act_own"), sem("dve_own"), sem("pool_own")

        block = ctx.enter_context(nc.Block())

        @block.sync
        def _(sp):
            def load_g(row, layer):
                sp.dma_start(x_in[:, :], row).then_inc(load_dma, 16)
                sp.dma_start(wg[:, :], w[layer, :, 0:NG]).then_inc(load_dma, 16)
                sp.dma_start(bvb[:, :], bv[layer, :, :].to_broadcast([P, P])).then_inc(load_dma, 16)

            def replicate(par, u):
                sp.wait_ge(parts_ready, 2 * u + 1)
                for term, part in enumerate((0, 1, 2, 0, 1, 0)):
                    sp.dma_start(krep[par][term * CH:(term + 1) * CH, :, :], parts["k"][:, part, :]).then_inc(rep_dma, 16)
                sp.wait_ge(parts_ready, 2 * u + 2)
                for term, part in enumerate((0, 0, 0, 1, 1, 2)):
                    for th in range(2):
                        sp.dma_start(qrep[par][term * CH:(term + 1) * CH, th, :, :],
                                     parts["q"][:, part, th * HALF:(th + 1) * HALF]).then_inc(rep_dma, 16)
                sp.wait_ge(rep_dma, 16 * 3 * TERMS)
                sp.sem_inc(rep_dma, -16 * 3 * TERMS)
                sp.sem_inc(rep_ready, 1)
                sp.sem_inc(parts_free, 1)

            def gather(quad):
                sp.dma_start(den_dram[quad * QUAD:(quad + 1) * QUAD, :], av[quad][CH:P:32, :]).then_inc(av_dma, 16)
                for j in range(QUAD):
                    to = (quad * QUAD + j) * CH
                    sp.dma_start(num[to:to + CH, :], av[quad][32 * j:32 * j + CH, :]).then_inc(av_dma, 16)

            load_g(x[0, :, :], 0)
            sp.wait_ge(load_dma, 48)
            sp.sem_inc(load_dma, -48)
            sp.sem_inc(g_in, 1)
            for b in range(B):
                sp.dma_start(out[b, :, :], x[b, :, :]).then_inc(copy_dma, 16)
            replicate(0, 0)
            sp.sem_inc(parts_ready, -2)
            sp.wait_ge(av_ready, 1)
            sp.sem_inc(av_ready, -1)
            gather(0)
            sp.wait_ge(y_ready, 1)
            sp.sem_inc(y_ready, -1)
            load_g(x[1, :, :], 0)
            sp.wait_ge(load_dma, 48)
            sp.sem_inc(load_dma, -48)
            sp.wait_ge(copy_dma, 16 * B)
            sp.sem_inc(g_in, 1)

            def last_output(row):
                gather(1)
                sp.dma_start(x_res[:, :], row).then_inc(load_dma, 16)
                sp.wait_ge(av_dma, 16 * 2 * (QUAD + 1))
                sp.sem_inc(av_dma, -16 * 2 * (QUAD + 1))
                sp.sem_inc(av_free, 1)
                sp.dma_start(den[:, :], den_dram.rearrange("h (p t) -> (h p) t", p=CH)).then_inc(den_dma, 16)
                sp.wait_ge(den_dma, 16)
                sp.sem_inc(den_dma, -16)
                sp.sem_inc(den_ready, 1)

            def spread():
                sp.dma_start(rden_dram.rearrange("h (p t) -> (h p) t", p=CH), rden[:, :]).then_inc(den_dma, 16)
                sp.wait_ge(den_dma, 16)
                sp.dma_start(rrep[:, :], rden_dram.rearrange("h (a t) -> h a t", a=1).to_broadcast([HEADS, CH, T])).then_inc(den_dma, 16)
                sp.wait_ge(load_dma, 16)
                sp.sem_inc(load_dma, -16)
                sp.wait_ge(den_dma, 32)
                sp.sem_inc(den_dma, -32)
                sp.sem_inc(o_in, 1)

            with sp.Fori(0, PAIRS) as pair:
                for u in range(2):
                    i = 2 * pair + u
                    sp.wait_ge(av_ready, 2 * u + 1)
                    last_output(out[(i + B - 1) % B, :, :])
                    sp.wait_ge(rden_ready, u + 1)
                    spread()
                    replicate(1 - u, u)
                    sp.wait_ge(y_ready, 2 * (u + 1))
                    sp.dma_start(out[(i + B - 1) % B, :, :], y[:, :]).then_inc(store_dma, 16)
                    load_g(out[(i + 2) % B, :, :], (i + 2) // B)
                    sp.dma_start(wo[:, :], w[i // B, :, W_P:W_P + NO]).then_inc(load_dma, 16)
                    sp.wait_ge(store_dma, 16)
                    sp.sem_inc(store_dma, -16)
                    sp.wait_ge(load_dma, 64)
                    sp.sem_inc(load_dma, -64)
                    sp.sem_inc(g_in, 1)
                    sp.wait_ge(av_ready, 2 * u + 2)
                    gather(0)
                sp.sem_inc(parts_ready, -4)
                sp.sem_inc(av_ready, -4)
                sp.sem_inc(rden_ready, -2)
                sp.sem_inc(y_ready, -4)
            sp.wait_ge(av_ready, 1)
            last_output(out[B - 1, :, :])
            sp.wait_ge(rden_ready, 1)
            spread()
            sp.wait_ge(y_ready, 2)
            sp.dma_start(out[B - 1, :, :], y[:, :]).then_inc(store_dma, 16)
            sp.wait_ge(store_dma, 16)

        @block.gpsimd
        def _(pool):
            own = Own(pool, pool_own)
            set_up_constants(nc, pool, gmat, ident, consts)
            n = 5
            for i in range(2):
                for part, value in ((vT[i][:, :, :, CH:32], 1.0), (krep[i][KS:KM, :, :], 1.0), (av[i][:, :], 1.0)):
                    pool.wait_ge(consts, n)
                    nc.gpsimd.memset(part, value).then_inc(consts, 1)
                    n += 1
            pool.wait_ge(consts, n)
            nc.gpsimd.memset(wo[:, :], 0.0).then_inc(consts, 1)
            pool.wait_ge(consts, n + 1)
            nc.gpsimd.memset(exponent[:, :], -0.5).then_inc(consts, 1)
            pool.wait_ge(consts, CONSTS)

            def split(n, which):
                pool.wait_ge(evacuated, n)
                tt, whole, (lead, middle, last) = nc.gpsimd.tensor_tensor, full[which][:, :], (parts[which][:, p, :] for p in range(3))
                own.done(tt(middle, whole, lead, ALU.subtract))
                own.done(tt(rest[:, :], whole, lead, ALU.subtract))
                own.done(tt(last, rest[:, :], middle, ALU.subtract))
                pool.sem_inc(parts_ready, 1)

            def stage_g(u):
                pool.wait_ge(coef_ready, u + 1)
                tt = nc.gpsimd.tensor_tensor
                own.done(tt(co[:, 4:5], co[:, 1:2], exponent[:, :], ALU.pow))
                own.done(tt(co[:, 2:3], co[:, 4:5], wg[:, W_GAMMA:W_GAMMA + 1], ALU.mult))
                own.done(tt(co[:, 5:6], gs[:, 0:1], co[:, 2:3], ALU.mult))
                tt(co[:, 3:4], wg[:, W_BETA:W_BETA + 1], co[:, 5:6], ALU.subtract).then_inc(scale_ready, 1)
                split(2 * u + 1, "k")
                split(2 * u + 2, "q")

            def normalise(n):
                pool.wait_ge(o_in, n)
                nc.gpsimd.tensor_tensor(attn[:, :], num[:, :], rrep[:, :], ALU.mult).then_inc(attn_ready, 1)

            def split_max(n, th):
                pool.wait_ge(nmax_ready, n)
                new, to = nmax[:, th * MH:(th + 1) * MH], nparts[th]
                own.done(nc.gpsimd.tensor_scalar(to[:, 0, :], new, 1.0, None, ALU.mult))
                own.done(nc.gpsimd.tensor_tensor(nrest[:, :], new, to[:, 0, :], ALU.subtract))
                own.done(nc.gpsimd.tensor_scalar(to[:, 1, :], nrest[:, :], 1.0, None, ALU.mult))
                own.done(nc.gpsimd.tensor_tensor(to[:, 2, :], nrest[:, :], to[:, 1, :], ALU.subtract))
                pool.sem_inc(nparts_ready, 1)

            pool.sem_inc(av_ready, 2)
            stage_g(0)
            pool.sem_inc(coef_ready, -1)
            pool.sem_inc(evacuated, -2)
            split_max(1, 0)
            pool.sem_inc(nmax_ready, -1)
            own.drain()
            with pool.Fori(0, PAIRS):
                for u in range(2):
                    split_max(4 * u + 1, 1)
                    stage_g(u)
                    normalise(u + 1)
                    split_max(4 * u + 2, 0)
                    split_max(4 * u + 3, 1)
                    split_max(4 * u + 4, 0)
                pool.sem_inc(coef_ready, -2)
                pool.sem_inc(evacuated, -4)
                pool.sem_inc(nmax_ready, -8)
                pool.sem_inc(o_in, -2)
                own.drain()
            normalise(1)

        @block.vector
        def _(dve):
            own = Own(dve, dve_own)

            def statistics(n):
                dve.wait_ge(g_in, n)
                for c in range(2):
                    own.mark(nc.vector.bn_stats(bst[:, c, :], x_in[:, c * HALF:(c + 1) * HALF]))
                own.wait()
                own.done(nc.vector.bn_aggr(mv[:, :], bst[:, :, :]))
                own.mark(nc.vector.tensor_copy(st2[:, 0:1], mv[:, 0:1]))
                nc.vector.scalar_tensor_tensor(out=st2[:, 1:2], in0=mv[:, 0:1], scalar=mv[:, 0:1], in1=mv[:, 1:2],
                                               op0=ALU.mult, op1=ALU.add).then_inc(stats_ready, 1)

            def coefficients(n):
                dve.wait_ge(misc_for_dve, n)
                own.done(nc.vector.tensor_copy(gs[:, :], misc[:, 0:2]))
                dve.sem_inc(misc_dve, 1)
                own.done(nc.vector.scalar_tensor_tensor(out=co[:, 0:1], in0=gs[:, 0:1], scalar=gs[:, 0:1],
                                                        in1=gs[:, 1:2], op0=ALU.mult, op1=ALU.subtract))
                nc.vector.tensor_scalar(co[:, 1:2], co[:, 0:1], -1.0, EPS, ALU.mult, ALU.add).then_inc(coef_ready, 1)

            def values(n, par, c, last=None):
                dve.wait_ge(misc_for_dve, n)
                nc.vector.tensor_tensor(
                    vT[par][:, 4 * c:4 * c + 4, :, 0:CH],
                    misc[:, :].rearrange("p (s h c) -> p s h c", s=4, h=HEADS),
                    bvb[:, :].rearrange("p (a h c) -> p a h c", a=1, h=HEADS).to_broadcast([P, 4, HEADS, CH]),
                    ALU.add).then_inc(misc_dve, 1)

            def invert(n):
                dve.wait_ge(den_ready, n)
                nc.vector.reciprocal(rden[:, :], den[:, :]).then_inc(rden_ready, 1)

            def output(n, c):
                dve.wait_ge(misc_for_dve, n)
                own.done(nc.vector.scalar_tensor_tensor(
                    out=y[:, c * HALF:(c + 1) * HALF], in0=misc[:, :], scalar=wo[:, P:P + 1],
                    in1=x_res[:, c * HALF:(c + 1) * HALF], op0=ALU.add, op1=ALU.add))
                if c == 0:
                    dve.sem_inc(misc_dve, 1)
                dve.sem_inc(y_ready, 1)

            def maximum(n, unit):
                dve.wait_ge(scores_ready, n + 1)
                reduce = nc.vector.tensor_reduce(nmax[:, unit:unit + 1], s_ps[n % 2][:, :, :], AX.XY, ALU.max, negate=True)
                if unit % MH != MH - 1:
                    reduce.then_inc(max_done, 1)
                else:
                    own.done(reduce)
                    dve.sem_inc(max_done, 1)
                    dve.sem_inc(nmax_ready, 1)

            statistics(1)
            coefficients(1)
            values(2, 0, 0)
            dve.wait_ge(misc_for_dve, 3)
            own.done(nc.vector.tensor_tensor(
                vT[0][:, 4:8, :, 0:CH], misc[:, :].rearrange("p (s h c) -> p s h c", s=4, h=HEADS),
                bvb[:, :].rearrange("p (a h c) -> p a h c", a=1, h=HEADS).to_broadcast([P, 4, HEADS, CH]), ALU.add))
            dve.sem_inc(misc_dve, 1)
            dve.sem_inc(y_ready, 1)
            dve.sem_inc(g_in, -1)
            dve.sem_inc(misc_for_dve, -3)
            for unit in range(UNITS):
                maximum(unit, unit)
            dve.sem_inc(scores_ready, -UNITS)
            own.drain()
            with dve.Fori(0, PAIRS):
                for s in range(4):
                    u = s // 2
                    for k in range(GROUPS):
                        if s % 2 == 0:
                            base = 5 * u
                            if k == 0:
                                statistics(u + 1)
                            if k == AVG + 1:
                                coefficients(base + 1)
                            if k == 5:
                                invert(u + 1)
                            if k == V0 + 1:
                                values(base + 2, 1 - u, 0)
                            if k == V1 + 1:
                                values(base + 3, 1 - u, 1)
                            if k == O0 + 1:
                                output(base + 4, 0)
                        for unit in (2 * k, 2 * k + 1):
                            maximum(UNITS * s + unit, unit)
                    if s % 2 == 0:
                        output(5 * u + 5, 1)
                dve.sem_inc(g_in, -2)
                dve.sem_inc(misc_for_dve, -10)
                dve.sem_inc(den_ready, -2)
                dve.sem_inc(scores_ready, -4 * UNITS)
                own.drain()
            invert(1)
            output(1, 0)
            output(2, 1)

        @block.scalar
        def _(act):
            own = Own(act, act_own)

            def evacuate(n, which, c, hold=False):
                act.wait_ge(misc_for_act, n)
                bias = wg[:, W_BQ:W_BQ + 1] if which == "q" else wg[:, W_BK:W_BK + 1]
                cols = slice(c * HALF, (c + 1) * HALF)
                own.mark(nc.scalar.activation(full[which][:, cols], misc[:, :], ACT.Identity, bias=bias))

            def leading(which, c):
                cols = slice(c * HALF, (c + 1) * HALF)
                own.mark(nc.scalar.copy(parts[which][:, 0, cols], full[which][:, cols]))

            def normalise(c):
                cols = slice(c * HALF, (c + 1) * HALF)
                nc.scalar.activation(h[:, cols], x_in[:, cols], ACT.Identity, bias=co[:, 3:4],
                                     scale=co[:, 2:3]).then_inc(h_ready, 1)

            def max_rows(n, th):
                act.wait_ge(misc_for_act, n)
                own.mark(nc.scalar.copy(mrow[th][:, :], misc_bf[0:3 * MH, 0:P]))

            def send_max_rows(step, th):
                own.wait()
                act.sem_inc(misc_act, 1)
                par, quad = step // 2 % 2, step % 2
                act.dma_start(qrep[par][KS:KM, th, quad * QUAD:(quad + 1) * QUAD, :],
                              mrow[th][:, :]).then_inc(mrow_dma, 16)

            def sums(n, quad, th):
                act.wait_ge(pv_done, n + 2)
                own.mark(nc.scalar.copy(av[quad][:, th * HALF:(th + 1) * HALF], pv_ps[:, :]))

            act.wait_ge(scale_ready, 1)
            act.sem_inc(scale_ready, -1)
            normalise(0)
            normalise(1)
            for n, (which, c) in enumerate((("k", 0), ("k", 1), ("q", 0), ("q", 1))):
                evacuate(n + 1, which, c)
                own.wait()
                act.sem_inc(misc_act, 1)
                leading(which, c)
                own.wait()
                if c == 1:
                    act.sem_inc(evacuated, 1)
            max_rows(5, 0)
            send_max_rows(0, 0)
            act.sem_inc(misc_for_act, -5)
            own.drain()
            act.sem_inc(pv_free, 1)
            act.wait_ge(consts, CONSTS)
            with act.Fori(0, PAIRS):
                for s in range(4):
                    u, quad = s // 2, s % 2
                    base = 8 * u + 6 * quad
                    order = [MAX1, MAX0] if quad else [MAX1, K0, K1, Q0, Q1, MAX0]
                    for k in range(GROUPS):
                        g = GROUPS * s + k
                        act.wait_ge(pv_done, g + 1)
                        for j in range(QUAD):
                            n = QUAD * g + j
                            act.wait_ge(st_ready, n + 1)
                            nc.scalar.activation(probs[g % 2][:, j, :], st_ps[j % 2][:, :], ACT.Exp,
                                                 scale=1.0 / CH ** 0.5).then_inc(exp_done, 1)
                            if j == 0 and k - 1 in order:
                                if k - 1 == MAX1:
                                    send_max_rows(s, 1)
                                elif k - 1 == MAX0:
                                    send_max_rows(s + 1, 0)
                                else:
                                    own.wait()
                                    act.sem_inc(misc_act, 1)
                            if j == 1 and k - 1 in (K0, K1, Q0, Q1) and quad == 0:
                                leading("k" if k - 1 in (K0, K1) else "q", (k - 1 - K0) % 2)
                            if j == 3 and k - 1 in (K1, Q1) and quad == 0:
                                own.wait()
                                act.sem_inc(evacuated, 1)
                            if j % 2 == 1 and k == K0 - 1 and quad == 0:
                                if j == 1:
                                    act.wait_ge(scale_ready, u + 1)
                                normalise(j // 2)
                            if j == 0 and k == TILES + 1:
                                if quad == 0:
                                    act.wait_ge(av_free, u + 1)
                                sums(g - 1, quad, 0)
                            if j == 1 and k == TILES + 1:
                                own.wait()
                                act.sem_inc(pv_free, 1)
                        if k in order:
                            n = base + order.index(k) + 1
                            if k in (MAX0, MAX1):
                                max_rows(n, 1 if k == MAX1 else 0)
                            else:
                                if k == K0:
                                    act.wait_ge(parts_free, u + 1)
                                evacuate(n, "k" if k in (K0, K1) else "q", (k - K0) % 2)
                    sums(GROUPS * (s + 1), quad, 1)
                    own.wait()
                    act.sem_inc(pv_free, 1)
                    act.sem_inc(av_ready, 1)
                act.sem_inc(misc_for_act, -16)
                act.sem_inc(pv_done, -4 * GROUPS)
                act.sem_inc(st_ready, -4 * GROUPS * QUAD)
                act.sem_inc(av_free, -2)
                act.sem_inc(scale_ready, -2)
                act.sem_inc(parts_free, -2)
                own.drain()

        @block.tensor
        def _(pe):
            def project(c, column, ready):
                nc.tensor.matmul(misc[:, :], wg[:, column:column + P], h[:, c * HALF:(c + 1) * HALF],
                                 start=True, stop=True).then_inc(ready, 1)

            def project_values(c):
                for n in range(4):
                    t = 4 * c + n
                    last = nc.tensor.matmul(misc[:, n * P:(n + 1) * P], h[:, t * P:(t + 1) * P],
                                            wg[:, W_V:W_V + P], start=True, stop=True)
                last.then_inc(misc_for_dve, 1)

            def project_output(c):
                nc.tensor.matmul(misc[:, :], wo[:, 0:P], attn[:, c * HALF:(c + 1) * HALF],
                                 start=True, stop=True).then_inc(misc_for_dve, 1)

            def average():
                nc.tensor.matmul(misc[:, 0:2], gmat[:, :], st2[:, :], start=True, stop=True).then_inc(misc_for_dve, 1)

            def transpose_max(th):
                nc.tensor.transpose(misc_bf[0:3 * MH, 0:P], nparts[th][:, :, :].rearrange("p a b -> p (a b)"),
                                    ident[:, :]).then_inc(misc_for_act, 1)

            def row_scores(n, par, quad, unit, halves=(0, 1)):
                th, head, tile = unit // MH, quad * QUAD + unit % MH // (TILES // 2), unit % (TILES // 2)
                for c in halves:
                    last = nc.tensor.matmul(s_ps[n % 2][:, c, :], qrep[par][0:KS, th, head, tile * P:(tile + 1) * P],
                                            krep[par][0:KS, head, c * HALF:(c + 1) * HALF], start=True, stop=True)
                if 1 in halves:
                    last.then_inc(scores_ready, 1)

            pe.sem_inc(pv_done, 2)
            pe.wait_ge(consts, CONSTS)
            pe.wait_ge(stats_ready, 1)
            average()
            pe.wait_ge(misc_dve, 1)
            pe.wait_ge(h_ready, 2)
            project(0, W_K, misc_for_act)
            pe.wait_ge(misc_act, 1)
            project(1, W_K, misc_for_act)
            pe.wait_ge(misc_act, 2)
            project(0, W_Q, misc_for_act)
            pe.wait_ge(misc_act, 3)
            project(1, W_Q, misc_for_act)
            pe.wait_ge(misc_act, 4)
            project_values(0)
            pe.wait_ge(misc_dve, 2)
            project_values(1)
            pe.wait_ge(misc_dve, 3)
            pe.wait_ge(rep_ready, 1)
            for unit in range(UNITS):
                if unit >= 2:
                    pe.wait_ge(max_done, unit - 1)
                row_scores(unit, 0, 0, unit)
            pe.wait_ge(nparts_ready, 1)
            transpose_max(0)
            pe.sem_inc(stats_ready, -1)
            pe.sem_inc(misc_dve, -3)
            pe.sem_inc(h_ready, -2)
            pe.sem_inc(misc_act, -4)
            pe.sem_inc(rep_ready, -1)
            pe.sem_inc(max_done, -(UNITS - 2))
            pe.sem_inc(nparts_ready, -1)

            with pe.Fori(0, PAIRS):
                for s in range(4):
                    u, quad = s // 2, s % 2
                    par = u
                    mpar, mquad = (s + 1) // 2 % 2, (s + 1) % 2
                    a, d = 8 * u, 4 * u
                    if quad == 1:
                        pe.wait_ge(rep_ready, u + 1)

                    def products(k):
                        g = GROUPS * s + k
                        pe.wait_ge(exp_done, QUAD * (g + 1))
                        if k % TILES == 0:
                            pe.wait_ge(pv_free, 2 * s + k // TILES + 1)
                        for j in range(QUAD):
                            last = nc.tensor.matmul(pv_ps[32 * j:32 * j + 32, :],
                                                    vT[par][:, k % TILES, quad * QUAD + j, :], probs[g % 2][:, j, :],
                                                    start=(k % TILES == 0), stop=(k % TILES == TILES - 1))
                        last.then_inc(pv_done, 1)

                    def in_shared_bank(k):
                        if k == MAX1:
                            if quad == 0:
                                pe.wait_ge(misc_dve, d + 1)
                            pe.wait_ge(nparts_ready, 2 * s + 1)
                            transpose_max(1)
                        elif k == MAX0:
                            if quad == 0:
                                pe.wait_ge(misc_dve, d + 3)
                            else:
                                pe.wait_ge(misc_act, a + 8)
                            pe.wait_ge(nparts_ready, 2 * s + 2)
                            transpose_max(0)
                        elif quad == 1:
                            pass
                        elif k == AVG:
                            pe.wait_ge(misc_act, a + 1)
                            pe.wait_ge(stats_ready, u + 1)
                            average()
                        elif k == K0:
                            pe.wait_ge(misc_act, a + 2)
                            pe.wait_ge(h_ready, 2 * (u + 1))
                            project(0, W_K, misc_for_act)
                        elif k == K1:
                            pe.wait_ge(misc_act, a + 3)
                            project(1, W_K, misc_for_act)
                        elif k == Q0:
                            pe.wait_ge(misc_act, a + 4)
                            project(0, W_Q, misc_for_act)
                        elif k == Q1:
                            pe.wait_ge(misc_act, a + 5)
                            project(1, W_Q, misc_for_act)
                        elif k == V0:
                            pe.wait_ge(misc_act, a + 6)
                            project_values(0)
                        elif k == V1:
                            pe.wait_ge(misc_dve, d + 2)
                            project_values(1)
                        elif k == O0:
                            pe.wait_ge(misc_act, a + 7)
                            pe.wait_ge(attn_ready, u + 1)
                            project_output(0)
                        elif k == O1:
                            pe.wait_ge(misc_dve, d + 4)
                            project_output(1)

                    def m_unit(unit, half):
                        if half == 0:
                            pe.wait_ge(max_done, UNITS * s + unit + 1)
                        row_scores(unit, mpar, mquad, unit, (half,))

                    m_unit(0, 0)
                    for k in range(GROUPS):
                        th, st = k // TILES, k % TILES
                        if st == 0:
                            pe.wait_ge(mrow_dma, 16 * (2 * s + th + 1))
                        for j in range(QUAD):
                            n = QUAD * (GROUPS * s + k) + j
                            head = quad * QUAD + j
                            if n >= 2:
                                pe.wait_ge(exp_done, n - 1)
                            nc.tensor.matmul(st_ps[j % 2][:, :], krep[par][0:KM, head, st * P:(st + 1) * P],
                                             qrep[par][0:KM, th, head, :],
                                             start=True, stop=True).then_inc(st_ready, 1)
                            if j == 0:
                                m_unit(2 * k, 1)
                                m_unit(2 * k + 1, 0)
                            if j == 1:
                                m_unit(2 * k + 1, 1)
                                in_shared_bank(k)
                            if j == 2 and k >= 1:
                                products(k - 1)
                            if j == 3 and k < GROUPS - 1:
                                m_unit(2 * k + 2, 0)
                    products(GROUPS - 1)
                pe.sem_inc(mrow_dma, -16 * 8)
                pe.sem_inc(rep_ready, -2)
                pe.sem_inc(exp_done, -4 * GROUPS * QUAD)
                pe.sem_inc(max_done, -4 * UNITS)
                pe.sem_inc(pv_free, -8)
                pe.sem_inc(stats_ready, -2)
                pe.sem_inc(misc_act, -16)
                pe.sem_inc(misc_dve, -8)
                pe.sem_inc(h_ready, -4)
                pe.sem_inc(nparts_ready, -8)
                pe.sem_inc(attn_ready, -2)
            pe.wait_ge(mrow_dma, 16)
            pe.wait_ge(misc_act, 1)
            pe.wait_ge(attn_ready, 1)
            project_output(0)
            pe.wait_ge(misc_dve, 1)
            project_output(1)


def one_head(nc, ctx0, w, bv, out):
    EPS = 1e-6
    SCALE = float(P) ** -0.5
    HT = TILES // 2
    PAIRS = 2 * B // 2
    BODY = 2 * TILES
    AVG, O0, K0, K1, Q0, V0, O1, Q1, V1 = (0, 1), (1, 0), (1, 2), (2, 2), (3, 2), (4, 1), (5, 1), (6, 2), (7, 1)
    HI, LO = 0, 1

    ctx = ExitStack()
    with ctx:
        def sb(name, shape, dt=F32):
            return ctx.enter_context(nc.sbuf_tensor("o_" + name, shape, dt))

        def psum(name, shape):
            return ctx.enter_context(nc.psum_tensor("o_" + name, shape, F32))

        def sem(name):
            return ctx0.enter_context(nc.semaphore("o_" + name))

        q = [sb(f"q{i}", [P, 2, T], F32R) for i in range(2)]
        k = [sb(f"k{i}", [P, 2, T], F32R) for i in range(2)]
        vT = [sb(f"vT{i}", [P, 2, TILES, P], F32R) for i in range(2)]
        full = {"q": sb("qf", [P, T]), "k": sb("kf", [P, T]), "v": sb("vf", [P, T])}
        probs = [sb(f"probs{i}", [P, T]) for i in range(2)]
        pT = [sb(f"pT{i}", [P, 2, TILES, HALF], F32R) for i in range(2)]
        x_in = sb("x_in", [P, T])
        x_res = sb("x_res", [P, T])
        wg = [sb(f"wg{i}", [P, NG]) for i in range(2)]
        bvb = [sb(f"bvb{i}", [P, P]) for i in range(2)]
        wo = sb("wo", [P, NO])
        h = sb("h", [P, T])
        attn = sb("attn", [P, T])
        y = sb("y", [P, T])
        gmat = sb("gmat", [P, P])
        ident_bf = sb("ident_bf", [P, P], BF16)
        ident = sb("ident", [P, P])
        bst = sb("bst", [P, 2, 6])
        mv = sb("mv", [P, 2])
        st2 = sb("st2", [P, 2])
        gs = sb("gs", [P, 2])
        co = sb("co", [P, 6])
        exponent = sb("exponent", [P, 1])
        nmax = sb("nmax", [P, 2])
        bias = sb("bias", [P, 2])
        rsum = sb("rsum", [P, 2])
        rinv = sb("rinv", [P, 2])

        s_ps = [psum(f"s{i}", [P, 2, HALF]) for i in range(2)]
        t_ps = [psum(f"t{i}", [P, HT, P]) for i in range(2)]
        pv_ps = psum("pv", [P, HALF])
        misc = psum("misc", [P, HALF])

        consts = sem("consts")
        CONSTS = 10
        zeros = sem("zeros")
        s_ready = sem("s_ready")
        bias_ready = sem("bias_ready")
        exp_ready = sem("exp_ready")
        rinv_ready = sem("rinv_ready")
        p_ready = sem("p_ready")
        t_ready = sem("t_ready")
        hi_ready = sem("hi_ready")
        t_free = sem("t_free")
        pv_ready = sem("pv_ready")
        attn_ready = sem("attn_ready")
        misc_act = sem("misc_act")
        misc_dve = sem("misc_dve")
        misc_for_act = sem("misc_for_act")
        misc_for_dve = sem("misc_for_dve")
        kq_full = sem("kq_full")
        v_full = sem("v_full")
        kq_parts = sem("kq_parts")
        v_parts = sem("v_parts")
        stats_ready = sem("stats_ready")
        coef_ready = sem("coef_ready")
        scale_ready = sem("scale_ready")
        h_ready = sem("h_ready")
        x_dma = sem("x_dma")
        w_dma = [sem(f"w_dma{i}") for i in range(2)]
        o_dma = sem("o_dma")
        x_used = sem("x_used")
        w_used = sem("w_used")
        y_ready = sem("y_ready")
        act_own, dve_own, pool_own = sem("act_own"), sem("dve_own"), sem("pool_own")

        block = ctx.enter_context(nc.Block())

        @block.sync
        def _(sp):
            def load_weights(par, layer):
                sp.dma_start(wg[par][:, :], w[layer, :, 0:NG]).then_inc(w_dma[par], 16)
                sp.dma_start(bvb[par][:, :], bv[layer, :, :].to_broadcast([P, P])).then_inc(w_dma[par], 16)

            sp.dma_start(x_in[:, :], out[0, :, :]).then_inc(x_dma, 16)
            load_weights(0, 2)
            load_weights(1, 2)
            sp.dma_start(x_res[:, :], out[B - 1, :, :]).then_inc(o_dma, 48)
            sp.wait_ge(x_used, 1)
            sp.sem_inc(x_used, -1)
            sp.dma_start(x_in[:, :], out[1, :, :]).then_inc(x_dma, 16)
            with sp.Fori(0, PAIRS) as pair:
                for u in range(2):
                    i = 2 * pair + u
                    sp.wait_ge(w_used, u + 1)
                    load_weights(u, ((i + 2) // B + 2) % 4)
                    sp.wait_ge(x_used, u + 1)
                    sp.dma_start(x_in[:, :], out[(i + 2) % B, :, :]).then_inc(x_dma, 16)
                    sp.wait_ge(y_ready, 2 * (u + 1))
                    sp.dma_start(out[(i + B - 1) % B, :, :], y[:, :]).then_inc(o_dma, 16)
                    sp.dma_start(x_res[:, :], out[i % B, :, :]).then_inc(o_dma, 16)
                    sp.dma_start(wo[:, :], w[i // B + 2, :, W_P:W_P + NO]).then_inc(o_dma, 16)
                sp.sem_inc(w_used, -2)
                sp.sem_inc(x_used, -2)
                sp.sem_inc(y_ready, -4)
            sp.wait_ge(y_ready, 2)
            sp.dma_start(out[B - 1, :, :], y[:, :]).then_inc(o_dma, 16)
            sp.wait_ge(o_dma, 16)

        @block.gpsimd
        def _(pool):
            own = Own(pool, pool_own)
            set_up_constants(nc, pool, gmat, ident_bf, consts)
            n = 5
            for part, value in ((exponent[:, :], -0.5), (wo[:, :], 0.0), (attn[:, :], 0.0), (vT[1][:, :, :, :].bitcast(F32), 0.0)):
                pool.wait_ge(consts, n)
                nc.gpsimd.memset(part, value).then_inc(consts, 1)
                n += 1
            pool.wait_ge(consts, n)
            nc.gpsimd.tensor_scalar(ident[:, :], ident_bf[:, :], 1.0, None, ALU.mult).then_inc(consts, 1)

            def coefficients(n, par):
                pool.wait_ge(w_dma[par], 32)
                pool.wait_ge(coef_ready, n)
                tt = nc.gpsimd.tensor_tensor
                own.done(tt(co[:, 4:5], co[:, 1:2], exponent[:, :], ALU.pow))
                own.done(tt(co[:, 2:3], co[:, 4:5], wg[par][:, W_GAMMA:W_GAMMA + 1], ALU.mult))
                own.done(tt(co[:, 5:6], gs[:, 0:1], co[:, 2:3], ALU.mult))
                tt(co[:, 3:4], wg[par][:, W_BETA:W_BETA + 1], co[:, 5:6], ALU.subtract).then_inc(scale_ready, 1)

            def split(source, hi, lo, ready):
                own.done(nc.gpsimd.tensor_copy(hi, source))
                nc.gpsimd.tensor_tensor(lo, source, hi.bitcast(F32), ALU.subtract).then_inc(ready, 1)

            def split_kq(n, operand, name, c):
                pool.wait_ge(kq_full, n)
                cols = slice(c * HALF, (c + 1) * HALF)
                split(full[name][:, cols], operand[:, HI, cols], operand[:, LO, cols], kq_parts)

            def split_v(n, par, c):
                pool.wait_ge(v_full, n)
                tiles = slice(c * HT, (c + 1) * HT)
                split(full["v"][:, c * HALF:(c + 1) * HALF].rearrange("p (s c) -> p s c", s=HT),
                      vT[par][:, HI, tiles, :], vT[par][:, LO, tiles, :], v_parts)

            def stage_g(u, par):
                coefficients(u + 1, par)
                split_kq(4 * u + 1, k[par], "k", 0)
                split_kq(4 * u + 2, k[par], "k", 1)
                split_kq(4 * u + 3, q[par], "q", 0)
                split_v(2 * u + 1, par, 0)
                split_kq(4 * u + 4, q[par], "q", 1)
                split_v(2 * u + 2, par, 1)

            stage_g(0, 0)
            pool.sem_inc(w_dma[0], -32)
            pool.sem_inc(coef_ready, -1)
            pool.sem_inc(kq_full, -4)
            pool.sem_inc(v_full, -2)
            own.drain()
            with pool.Fori(0, PAIRS):
                stage_g(0, 1)
                stage_g(1, 0)
                pool.sem_inc(w_dma[0], -32)
                pool.sem_inc(w_dma[1], -32)
                pool.sem_inc(coef_ready, -2)
                pool.sem_inc(kq_full, -8)
                pool.sem_inc(v_full, -4)
                own.drain()

        @block.vector
        def _(dve):
            own = Own(dve, dve_own)

            def statistics(n):
                dve.wait_ge(x_dma, 16 * n)
                for c in range(2):
                    own.mark(nc.vector.bn_stats(bst[:, c, :], x_in[:, c * HALF:(c + 1) * HALF]))
                own.wait()
                own.done(nc.vector.bn_aggr(mv[:, :], bst[:, :, :]))
                own.done(nc.vector.tensor_copy(st2[:, 0:1], mv[:, 0:1]))
                nc.vector.scalar_tensor_tensor(out=st2[:, 1:2], in0=mv[:, 0:1], scalar=mv[:, 0:1], in1=mv[:, 1:2],
                                               op0=ALU.mult, op1=ALU.add).then_inc(stats_ready, 1)

            def coefficients(n):
                dve.wait_ge(misc_for_dve, n)
                own.done(nc.vector.tensor_copy(gs[:, :], misc[:, 0:2]))
                dve.sem_inc(misc_dve, 1)
                own.done(nc.vector.scalar_tensor_tensor(out=co[:, 0:1], in0=gs[:, 0:1], scalar=gs[:, 0:1],
                                                        in1=gs[:, 1:2], op0=ALU.mult, op1=ALU.subtract))
                nc.vector.tensor_scalar(co[:, 1:2], co[:, 0:1], -1.0, EPS, ALU.mult, ALU.add).then_inc(coef_ready, 1)

            def values(n, par, c):
                dve.wait_ge(misc_for_dve, n)
                own.done(nc.vector.tensor_tensor(
                    full["v"][:, c * HALF:(c + 1) * HALF].rearrange("p (s c) -> p s c", s=HT),
                    misc[:, :].rearrange("p (s c) -> p s c", s=HT),
                    bvb[par][:, :].rearrange("p (a c) -> p a c", a=1).to_broadcast([P, HT, P]), ALU.add))
                dve.sem_inc(misc_dve, 1)
                dve.sem_inc(v_full, 1)
                if c == 1:
                    dve.sem_inc(w_used, 1)

            def output(n, c):
                dve.wait_ge(misc_for_dve, n)
                own.done(nc.vector.scalar_tensor_tensor(
                    out=y[:, c * HALF:(c + 1) * HALF], in0=misc[:, :], scalar=wo[:, P:P + 1],
                    in1=x_res[:, c * HALF:(c + 1) * HALF], op0=ALU.add, op1=ALU.add))
                dve.sem_inc(misc_dve, 1)
                dve.sem_inc(y_ready, 1)

            def maximum(n, tile):
                dve.wait_ge(s_ready, n)
                b = tile % 2
                own.done(nc.vector.tensor_reduce(nmax[:, b:b + 1], s_ps[b][:, :, :], AX.XY, ALU.max, negate=True))
                nc.vector.tensor_scalar(bias[:, b:b + 1], nmax[:, b:b + 1], SCALE, None, ALU.mult).then_inc(bias_ready, 1)

            def invert(n, tile):
                dve.wait_ge(exp_ready, n)
                b = tile % 2
                nc.vector.reciprocal(rinv[:, b:b + 1], rsum[:, b:b + 1]).then_inc(rinv_ready, 1)

            def rests(m):
                for bank in range(2):
                    dve.wait_ge(hi_ready, 2 * m + bank + 1)
                    to = (slice(None), slice(bank * HT, (bank + 1) * HT), slice(m % HT * P, (m % HT + 1) * P))
                    pt = pT[m // HT % 2]
                    nc.vector.tensor_tensor(pt[:, LO, :, :][to], t_ps[bank][:, :, :],
                                            pt[:, HI, :, :][to].bitcast(F32), ALU.subtract).then_inc(t_free, 1)

            nc.vector.memset(pT[1][:, HI, :, :].bitcast(F32), 0.0).then_inc(zeros, 1)
            nc.vector.memset(pT[1][:, LO, :, :].bitcast(F32), 0.0).then_inc(zeros, 1)
            statistics(1)
            coefficients(1)
            maximum(1, 0)
            invert(1, 0)
            maximum(2, 1)
            invert(2, 1)
            values(2, 0, 0)
            values(3, 0, 1)
            statistics(2)
            dve.sem_inc(x_dma, -32)
            dve.sem_inc(misc_for_dve, -3)
            dve.sem_inc(s_ready, -2)
            dve.sem_inc(exp_ready, -2)
            own.drain()
            with dve.Fori(0, PAIRS):
                for m in range(BODY):
                    u, tile = m // TILES, m % TILES
                    base = 5 * u
                    maximum(m + 1, m + 2)
                    if tile == AVG[0]:
                        coefficients(base + 1)
                    if tile == O0[0]:
                        output(base + 2, 0)
                    rests(m)
                    if tile == V0[0]:
                        values(base + 3, 1 - u, 0)
                    if tile == O1[0]:
                        output(base + 4, 1)
                    if tile == V1[0]:
                        values(base + 5, 1 - u, 1)
                    invert(m + 1, m + 2)
                    if tile == HT - 1:
                        statistics(u + 1)
                dve.sem_inc(x_dma, -32)
                dve.sem_inc(misc_for_dve, -10)
                dve.sem_inc(s_ready, -BODY)
                dve.sem_inc(exp_ready, -BODY)
                dve.sem_inc(hi_ready, -2 * BODY)
                own.drain()
            output(1, 0)
            output(2, 1)

        @block.scalar
        def _(act):
            own = Own(act, act_own)

            def normalise(c):
                cols = slice(c * HALF, (c + 1) * HALF)
                own.mark(nc.scalar.activation(h[:, cols], x_in[:, cols], ACT.Identity, bias=co[:, 3:4],
                                              scale=co[:, 2:3]))

            def normalised():
                normalise(0)
                normalise(1)
                own.wait()
                act.sem_inc(h_ready, 1)
                act.sem_inc(x_used, 1)

            def evacuate(n, name, c, par):
                act.wait_ge(misc_for_act, n)
                column = W_BK if name == "k" else W_BQ
                own.done(nc.scalar.activation(full[name][:, c * HALF:(c + 1) * HALF], misc[:, :], ACT.Identity,
                                              bias=wg[par][:, column:column + 1]))
                act.sem_inc(misc_act, 1)
                act.sem_inc(kq_full, 1)

            def exponentials(n, tile):
                act.wait_ge(bias_ready, n)
                b = tile % 2
                nc.scalar.activation(probs[b][:, :], s_ps[b][:, :, :], ACT.Exp, bias=bias[:, b:b + 1], scale=SCALE,
                                     accum_out=rsum[:, b:b + 1]).then_inc(exp_ready, 1)

            def divide(n, tile):
                act.wait_ge(rinv_ready, n)
                b = tile % 2
                nc.scalar.activation(probs[b][:, :], probs[b][:, :], ACT.Copy, scale=rinv[:, b:b + 1]).then_inc(p_ready, 1)

            def products(n, c):
                act.wait_ge(pv_ready, n)
                nc.scalar.copy(attn[:, c * HALF:(c + 1) * HALF], pv_ps[:, :]).then_inc(attn_ready, 1)

            act.wait_ge(scale_ready, 1)
            act.sem_inc(scale_ready, -1)
            normalised()
            evacuate(1, "k", 0, 0)
            evacuate(2, "k", 1, 0)
            evacuate(3, "q", 0, 0)
            evacuate(4, "q", 1, 0)
            act.sem_inc(misc_for_act, -4)
            exponentials(1, 0)
            divide(1, 0)
            exponentials(2, 1)
            act.sem_inc(bias_ready, -2)
            act.sem_inc(rinv_ready, -1)
            act.wait_ge(consts, CONSTS)
            own.drain()
            with act.Fori(0, PAIRS):
                for m in range(BODY):
                    u, tile = m // TILES, m % TILES
                    base = 4 * u
                    if tile % HT == 0:
                        products(m // HT + 1, 0 if tile < HT else 1)
                    if tile == K0[0] + 1:
                        evacuate(base + 1, "k", 0, 1 - u)
                    if tile == K1[0] + 1:
                        evacuate(base + 2, "k", 1, 1 - u)
                    if tile == Q0[0] + 1:
                        evacuate(base + 3, "q", 0, 1 - u)
                    if tile == Q1[0] + 1:
                        evacuate(base + 4, "q", 1, 1 - u)
                    divide(m + 1, m + 1)
                    for bank in range(2):
                        act.wait_ge(t_ready, 2 * m + bank + 1)
                        nc.scalar.copy(pT[m // HT % 2][:, HI, bank * HT:(bank + 1) * HT, m % HT * P:(m % HT + 1) * P],
                                       t_ps[bank][:, :, :]).then_inc(hi_ready, 1)
                    exponentials(m + 1, m + 2)
                    if tile == AVG[0]:
                        act.wait_ge(scale_ready, u + 1)
                        normalised()
                act.sem_inc(bias_ready, -BODY)
                act.sem_inc(rinv_ready, -BODY)
                act.sem_inc(misc_for_act, -8)
                act.sem_inc(pv_ready, -4)
                act.sem_inc(t_ready, -2 * BODY)
                act.sem_inc(scale_ready, -2)
                own.drain()
            products(1, 0)
            products(2, 1)

        @block.tensor
        def _(pe):
            def project(par, c, column):
                nc.tensor.matmul(misc[:, :], wg[par][:, column:column + P], h[:, c * HALF:(c + 1) * HALF],
                                 start=True, stop=True).then_inc(misc_for_act, 1)

            def project_values(par, c):
                for n in range(4):
                    t = 4 * c + n
                    last = nc.tensor.matmul(misc[:, n * P:(n + 1) * P], h[:, t * P:(t + 1) * P],
                                            wg[par][:, W_V:W_V + P], start=True, stop=True)
                last.then_inc(misc_for_dve, 1)

            def project_output(c):
                nc.tensor.matmul(misc[:, :], wo[:, 0:P], attn[:, c * HALF:(c + 1) * HALF],
                                 start=True, stop=True).then_inc(misc_for_dve, 1)

            def average():
                nc.tensor.matmul(misc[:, 0:2], gmat[:, :], st2[:, :], start=True, stop=True).then_inc(misc_for_dve, 1)

            def split_product(to, stationary, moving, start=True, stop=True):
                pairs = ((HI, HI), (HI, LO), (LO, HI))
                for n, (a, b) in enumerate(pairs):
                    last = nc.tensor.matmul(to, stationary(a), moving(b), start=start and n == 0,
                                            stop=stop and n == len(pairs) - 1)
                return last

            def scores(par, n):
                tile = n % TILES
                for c in range(2):
                    last = split_product(s_ps[n % 2][:, c, :],
                                         lambda part: q[par][:, part, tile * P:(tile + 1) * P],
                                         lambda part: k[par][:, part, c * HALF:(c + 1) * HALF])
                last.then_inc(s_ready, 1)

            def products(half, quarter):
                for st in (2 * quarter, 2 * quarter + 1):
                    last = split_product(pv_ps[:, :], lambda part: vT[half // 2 % 2][:, part, st, :],
                                         lambda part: pT[half % 2][:, part, st, :],
                                         start=(st == 0), stop=(st == TILES - 1))
                if quarter == 3:
                    last.then_inc(pv_ready, 1)

            pe.sem_inc(t_free, 2)
            pe.wait_ge(zeros, 2)
            pe.wait_ge(consts, CONSTS)
            pe.wait_ge(stats_ready, 1)
            average()
            pe.wait_ge(misc_dve, 1)
            pe.wait_ge(h_ready, 1)
            project(0, 0, W_K)
            pe.wait_ge(misc_act, 1)
            project(0, 1, W_K)
            pe.wait_ge(misc_act, 2)
            project(0, 0, W_Q)
            pe.wait_ge(misc_act, 3)
            project(0, 1, W_Q)
            products(3, 0)
            products(3, 1)
            products(3, 2)
            products(3, 3)
            pe.wait_ge(kq_parts, 3)
            scores(0, 0)
            scores(0, 1)
            pe.wait_ge(misc_act, 4)
            project_values(0, 0)
            pe.wait_ge(misc_dve, 2)
            project_values(0, 1)
            pe.sem_inc(kq_parts, -3)
            pe.sem_inc(stats_ready, -1)
            pe.sem_inc(misc_dve, -2)
            pe.sem_inc(h_ready, -1)
            pe.sem_inc(misc_act, -4)
            with pe.Fori(0, PAIRS):
                for m in range(BODY):
                    u, tile = m // TILES, m % TILES
                    a, d = 4 * u, 5 * u

                    def in_shared_bank(slot):
                        if slot == AVG:
                            pe.wait_ge(misc_dve, d + 1)
                            pe.wait_ge(stats_ready, u + 1)
                            average()
                        elif slot == O0:
                            pe.wait_ge(misc_dve, d + 2)
                            pe.wait_ge(o_dma, 48 * (u + 1))
                            pe.wait_ge(attn_ready, 2 * u + 1)
                            project_output(0)
                        elif slot == K0:
                            pe.wait_ge(misc_dve, d + 3)
                            pe.wait_ge(h_ready, u + 1)
                            project(1 - u, 0, W_K)
                        elif slot == K1:
                            pe.wait_ge(misc_act, a + 1)
                            project(1 - u, 1, W_K)
                        elif slot == Q0:
                            pe.wait_ge(misc_act, a + 2)
                            project(1 - u, 0, W_Q)
                        elif slot == V0:
                            pe.wait_ge(misc_act, a + 3)
                            project_values(1 - u, 0)
                        elif slot == O1:
                            pe.wait_ge(misc_dve, d + 4)
                            project_output(1)
                        elif slot == Q1:
                            pe.wait_ge(misc_dve, d + 5)
                            project(1 - u, 1, W_Q)
                        elif slot == V1:
                            pe.wait_ge(misc_act, a + 4)
                            project_values(1 - u, 1)

                    pe.wait_ge(p_ready, m + 1)
                    if tile == 2:
                        pe.wait_ge(kq_parts, a + 1)
                    if tile == TILES - 2:
                        pe.wait_ge(kq_parts, a + 4)
                    scores((m + 2) // TILES % 2, m + 2)
                    in_shared_bank((tile, 0))
                    for bank in range(2):
                        pe.wait_ge(t_free, 2 * m + bank + 1)
                        for n in range(HT):
                            st = bank * HT + n
                            last = nc.tensor.transpose(t_ps[bank][:, n, :], probs[m % 2][:, st * P:(st + 1) * P], ident[:, :])
                        last.then_inc(t_ready, 1)
                    in_shared_bank((tile, 1))
                    if m % HT == 0:
                        pe.wait_ge(attn_ready, m // HT + 1)
                    if tile == HT:
                        pe.wait_ge(v_parts, 2 * (u + 1))
                    products((m // HT + 3) % 4, m % HT)
                    in_shared_bank((tile, 2))
                pe.sem_inc(t_free, -2 * BODY)
                pe.sem_inc(attn_ready, -4)
                pe.sem_inc(o_dma, -96)
                pe.sem_inc(p_ready, -BODY)
                pe.sem_inc(kq_parts, -8)
                pe.sem_inc(v_parts, -4)
                pe.sem_inc(stats_ready, -2)
                pe.sem_inc(misc_dve, -10)
                pe.sem_inc(misc_act, -8)
                pe.sem_inc(h_ready, -2)
            pe.wait_ge(t_free, 2)
            pe.wait_ge(attn_ready, 1)
            for quarter in range(4):
                products(3, quarter)
            pe.wait_ge(misc_dve, 1)
            pe.wait_ge(o_dma, 48)
            pe.sem_inc(o_dma, -48)
            project_output(0)
            pe.wait_ge(misc_dve, 2)
            pe.wait_ge(attn_ready, 2)
            project_output(1)


def layout(inputs):
    import numpy as np

    def column(a):
        return np.asarray(a).reshape(P, 1)

    stack, rows = [], []
    for gamma, beta, qkv_w, qkv_b, proj_w, proj_b in (
        ("L0_conv_gn_w", "L0_conv_gn_b", "L0_conv_qkv_w", "L0_conv_qkv_b", "L0_conv_proj_w", "L0_conv_proj_b"),
        ("L1_conv_gamma", "L1_conv_beta", "L1_conv_w_qkv", "L1_conv_b_qkv", "L1_conv_w_proj", "L1_conv_b_proj"),
    ):
        wqkv = np.asarray(inputs[qkv_w]).reshape(HEADS, 3, CH, P)
        bqkv = np.asarray(inputs[qkv_b]).reshape(HEADS, 3, CH)
        wq, wk = (wqkv[:, n].transpose(2, 1, 0).reshape(P, P) for n in (0, 1))
        wv = wqkv[:, 2].transpose(2, 0, 1).reshape(P, P)
        bq, bk = (bqkv[:, n].transpose(1, 0).reshape(P, 1) for n in (0, 1))
        stack.append(np.concatenate([wq, wk, wv, column(inputs[gamma]), column(inputs[beta]), bq, bk,
                                     np.asarray(inputs[proj_w]).T, column(inputs[proj_b])], axis=1))
        rows.append(bqkv[:, 2].reshape(1, P))
    for names in (
        ("L2_conv_wq", "L2_conv_wk", "L2_conv_wv", "L2_conv_gn_gamma", "L2_conv_gn_beta", "L2_conv_bq", "L2_conv_bk",
         "L2_conv_wp", "L2_conv_bp", "L2_conv_bv"),
        ("L3_conv_wq", "L3_conv_wk", "L3_conv_wv", "L3_conv_gamma", "L3_conv_beta", "L3_conv_bq", "L3_conv_bk",
         "L3_conv_wo", "L3_conv_bo", "L3_conv_bv"),
    ):
        a = [np.asarray(inputs[n]) for n in names]
        stack.append(np.concatenate([m.T if m.ndim == 2 else column(m) for m in a[:-1]], axis=1))
        rows.append(a[-1].reshape(1, P))
    return np.stack(stack), np.stack(rows)


def program(nc, x, w, bv, out):
    with ExitStack() as ctx:
        many_heads(nc, ctx, x, w, bv, out)
        one_head(nc, ctx, w, bv, out)


def kernel(**inputs):
    import numpy as np
    import concourse.bacc as bacc
    from concourse.bass_utils import run_bass_kernel_spmd

    x = np.ascontiguousarray(np.asarray(inputs["x"]).reshape(B, P, T))
    w, bv = layout(inputs)
    arrays = {"x_dram": x, "w_dram": w, "bv_dram": bv}
    nc = bacc.Bacc("TRN2", target_bir_lowering=False, num_devices=1)
    args = [nc.dram_tensor(name, a.shape, F32, kind="ExternalInput").ap() for name, a in arrays.items()]
    out = nc.dram_tensor("out_dram", (B, P, T), F32, kind="ExternalOutput").ap()
    program(nc, *args, out)
    result = run_bass_kernel_spmd(nc, [arrays], core_ids=[0])
    return result.results[0]["out_dram"].reshape(np.asarray(inputs["x"]).shape)
```

```python
from contextlib import ExitStack

import concourse.bass as bass
from concourse import mybir

ALU = mybir.AluOpType
ACT = mybir.ActivationFunctionType
AX = mybir.AxisListType
F32 = mybir.dt.float32
BF16 = mybir.dt.bfloat16
F32R = mybir.dt.float32r

P = 128
T = 1024
B = 8
HALF = 512
TILES = T // P
GROUP = 4
HEADS = 8
CH = P // HEADS
QUAD = 4
TERMS = 6
KS = TERMS * CH
KM = KS + 3

W_Q, W_K, W_V, W_GAMMA, W_BETA, W_BQ, W_BK = 0, P, 2 * P, 3 * P, 3 * P + 1, 3 * P + 2, 3 * P + 3
NG = 3 * P + 4
W_P, W_BP, W_BV = NG, NG + P, NG + P + 1
NO = P + 1
NW = NG + NO + 1


def set_up_constants(nc, pool, gmat, ident, ready):
    nc.gpsimd.memset(gmat[:, :], 1.0 / GROUP).then_inc(ready, 1)
    pool.wait_ge(ready, 1)
    blocks = gmat[:, :].rearrange("p (g r) -> p g r", r=GROUP)
    nc.gpsimd.affine_select(out=blocks, in_=blocks, compare_op=ALU.is_ge, fill=0.0, base=0,
                            pattern=[[-GROUP, P // GROUP], [0, GROUP]], channel_multiplier=1).then_inc(ready, 1)
    pool.wait_ge(ready, 2)
    nc.gpsimd.affine_select(out=blocks, in_=blocks, compare_op=ALU.is_ge, fill=0.0, base=GROUP - 1,
                            pattern=[[GROUP, P // GROUP], [0, GROUP]], channel_multiplier=-1).then_inc(ready, 1)
    nc.gpsimd.memset(ident[:, :], 0.0).then_inc(ready, 1)
    pool.wait_ge(ready, 4)
    nc.gpsimd.affine_select(out=ident[:, :], in_=ident[:, :], compare_op=ALU.not_equal, fill=1.0, base=0,
                            pattern=[[-1, P]], channel_multiplier=1).then_inc(ready, 1)


def combine_weights(nc, to, wg):
    nc.tensor.matmul(to[:, P:2 * P], wg[:, W_V:W_V + P], wg[:, W_P:W_P + P], start=True, stop=True)
    nc.tensor.matmul(to[:, 2 * P:3 * P], wg[:, W_BV:W_BV + 1].to_broadcast([P, P]), wg[:, W_P:W_P + P], start=True, stop=True)


class Own:

    def __init__(self, eng, sem):
        self.eng, self.sem, self.n = eng, sem, 0

    def mark(self, instruction):
        instruction.then_inc(self.sem, 1)
        self.n += 1

    def wait(self):
        self.eng.wait_ge(self.sem, self.n)

    def done(self, instruction):
        self.mark(instruction)
        self.wait()

    def drain(self):
        self.eng.sem_inc(self.sem, -self.n)
        self.n = 0


def many_heads(nc, ctx0, kept, x, w, bv, out):
    EPS = 1e-5
    NEXT_EPS = 1e-6
    GROUPS = 2 * TILES
    UNITS = QUAD * TILES
    MH = UNITS // 2
    LEAD = 12
    AVG, K0, K1, MAX1, Q0, Q1, V0, V1, MAX0, O0, O1 = 0, 3, 4, 5, 6, 7, 8, 11, 13, 14, 15
    STATS = 8
    PAIRS = 2 * B // 2
    BANKS = 3
    STEP = 2 * UNITS
    CONSTS = 6

    def bank(n):
        return n % STEP % BANKS if n % STEP < STEP - 1 else 1

    def last_in_bank(n):
        return next(m for m in range(n - 1, n - 5, -1) if bank(m) == bank(n))

    ctx = ExitStack()
    with ctx:
        def sb(name, shape, dt=F32):
            return ctx.enter_context(nc.sbuf_tensor("h_" + name, shape, dt))

        def psum(name, shape):
            return ctx.enter_context(nc.psum_tensor("h_" + name, shape, F32))

        def sem(name):
            return ctx0.enter_context(nc.semaphore("h_" + name))

        qrep = [sb(f"qrep{i}", [P, 2, HEADS, HALF], BF16) for i in range(2)]
        krep = [sb(f"krep{i}", [P, HEADS, T], BF16) for i in range(2)]
        vT = [sb(f"vT{i}", [P, TILES, HEADS, 32]) for i in range(2)]
        probs = [sb(f"probs{i}", [P, QUAD, HALF]) for i in range(2)]
        x_in = sb("x_in", [P, T])
        wg = sb("wg", [P, NW])
        bvb = sb("bvb", [P, P])
        h = sb("h", [P, T])
        parts = {"q": sb("qp", [P, 3, T], BF16), "k": sb("kp", [P, 3, T], BF16)}
        rest = sb("rest", [P, T])
        full, av, num, den, rden, rrep, attn, x_res, wo, gmat, ident, exponent, den_dram, rden_dram = (
            kept[name] for name in ("full", "av", "num", "den", "rden", "rrep", "attn", "x_res", "wo", "gmat", "ident",
                                    "exponent", "den_dram", "rden_dram"))
        y = sb("y", [P, T])
        half_nmax = sb("half_nmax", [P, 2, UNITS])
        nmax = sb("nmax", [P, UNITS])
        nrest = sb("nrest", [P, MH])
        nparts = [sb(f"nparts{i}", [P, 3, MH], BF16) for i in range(2)]
        mrow = [sb(f"mrow{i}", [3 * MH, P], BF16) for i in range(2)]
        bst = sb("bst", [P, 2, 6])
        mv = sb("mv", [P, 2])
        st2 = sb("st2", [P, 2])
        gs = sb("gs", [P, 2])
        co = sb("co", [P, 6])

        s_ps = [psum(f"s_ps{i}", [P, HALF]) for i in range(BANKS)]
        st_ps = [psum(f"st_ps{i}", [P, HALF]) for i in range(BANKS)]
        pv_ps = psum("pv", [P, HALF])
        misc = psum("misc", [P, HALF])
        misc_bf = misc[:, :].bitcast(BF16)

        consts = sem("consts")
        ones = sem("ones")
        kq_full = sem("kq_full")
        max_done = sem("max_done")
        scores_ready = sem("scores_ready")
        st_ready = sem("st_ready")
        exp_done = sem("exp_done")
        pv_done = sem("pv_done")
        pv_free = sem("pv_free")
        misc_act = sem("misc_act")
        misc_dve = sem("misc_dve")
        misc_for_act = sem("misc_for_act")
        misc_for_dve = sem("misc_for_dve")
        stats_ready = sem("stats_ready")
        coef_ready = sem("coef_ready")
        scale_ready = sem("scale_ready")
        h_ready = sem("h_ready")
        evacuated = sem("evacuated")
        parts_ready = sem("parts_ready")
        parts_free = sem("parts_free")
        rep_ready = sem("rep_ready")
        nmax_ready = sem("nmax_ready")
        nparts_ready = sem("nparts_ready")
        mrow_dma = sem("mrow_dma")
        av_ready = sem("av_ready")
        av_free = sem("av_free")
        o_in = sem("o_in")
        den_ready = sem("den_ready")
        rden_ready = sem("rden_ready")
        attn_ready = sem("attn_ready")
        y_ready = sem("y_ready")
        g_in = sem("g_in")
        rep_dma, load_dma, av_dma, den_dma, copy_dma, store_dma = (
            sem(n) for n in ("rep_dma", "load_dma", "av_dma", "den_dma", "copy_dma", "store_dma"))
        act_own, dve_own, pool_own = sem("act_own"), sem("dve_own"), sem("pool_own")

        block = ctx.enter_context(nc.Block())

        def split_parts(engine, own, which):
            tt, whole, (lead, middle, last) = engine.tensor_tensor, full[which][:, :], (parts[which][:, p, :] for p in range(3))
            own.mark(tt(middle, whole, lead, ALU.subtract))
            own.done(tt(rest[:, :], whole, lead, ALU.subtract))
            own.done(tt(last, rest[:, :], middle, ALU.subtract))

        @block.sync
        def _(sp):
            def load_g(row, layer, columns=NG):
                sp.dma_start(x_in[:, :], row).then_inc(load_dma, 16)
                sp.dma_start(wg[:, 0:columns], w[layer, :, 0:columns]).then_inc(load_dma, 16)
                sp.dma_start(bvb[:, :], bv[layer, :, :].to_broadcast([P, P])).then_inc(load_dma, 16)

            def replicate(par, u):
                sp.wait_ge(parts_ready, 2 * u + 1)
                for term, part in enumerate((0, 1, 2, 0, 1, 0)):
                    sp.dma_start(krep[par][term * CH:(term + 1) * CH, :, :], parts["k"][:, part, :]).then_inc(rep_dma, 16)
                sp.wait_ge(parts_ready, 2 * u + 2)
                for term, part in enumerate((0, 0, 0, 1, 1, 2)):
                    for th in range(2):
                        sp.dma_start(qrep[par][term * CH:(term + 1) * CH, th, :, :],
                                     parts["q"][:, part, th * HALF:(th + 1) * HALF]).then_inc(rep_dma, 16)
                sp.wait_ge(rep_dma, 16 * 3 * TERMS)
                sp.sem_inc(rep_dma, -16 * 3 * TERMS)
                sp.sem_inc(rep_ready, 1)
                sp.sem_inc(parts_free, 1)

            load_g(x[0, :, :], 0)
            sp.wait_ge(load_dma, 48)
            sp.sem_inc(load_dma, -48)
            sp.sem_inc(g_in, 1)
            for b in range(B):
                sp.dma_start(out[b, :, :], x[b, :, :]).then_inc(copy_dma, 16)
            replicate(0, 0)
            sp.sem_inc(parts_ready, -2)
            sp.wait_ge(y_ready, 1)
            sp.sem_inc(y_ready, -1)
            load_g(x[1, :, :], 0)
            sp.wait_ge(load_dma, 48)
            sp.sem_inc(load_dma, -48)
            sp.wait_ge(copy_dma, 16 * B)
            sp.sem_inc(g_in, 1)

            def last_output(row):
                kept["gather"](sp, 1, av_dma)
                sp.dma_start(x_res[:, :], row).then_inc(load_dma, 16)
                sp.wait_ge(av_dma, 16 * 2 * (QUAD + 1))
                sp.sem_inc(av_dma, -16 * 2 * (QUAD + 1))
                sp.sem_inc(av_free, 1)
                sp.dma_start(den[:, :], den_dram.rearrange("h (p t) -> (h p) t", p=CH)).then_inc(den_dma, 16)
                sp.wait_ge(den_dma, 16)
                sp.sem_inc(den_dma, -16)
                sp.sem_inc(den_ready, 1)

            def spread():
                sp.dma_start(rden_dram.rearrange("h (p t) -> (h p) t", p=CH), rden[:, :]).then_inc(den_dma, 16)
                sp.wait_ge(den_dma, 16)
                sp.dma_start(rrep[:, :], rden_dram.rearrange("h (a t) -> h a t", a=1).to_broadcast([HEADS, CH, T])).then_inc(den_dma, 16)
                sp.wait_ge(load_dma, 16)
                sp.sem_inc(load_dma, -16)
                sp.wait_ge(den_dma, 32)
                sp.sem_inc(den_dma, -32)
                sp.sem_inc(o_in, 1)

            def body(pair, first=False, last=False):
                for u in range(2):
                    i = 2 * pair + u
                    if first and u == 0:
                        sp.sem_inc(av_ready, 1)
                        sp.sem_inc(rden_ready, 1)
                    else:
                        sp.wait_ge(av_ready, 2 * u + 1)
                        last_output(out[(i + B - 1) % B, :, :])
                        sp.wait_ge(rden_ready, u + 1)
                        spread()
                    if not (last and u == 1):
                        replicate(1 - u, u)
                    sp.wait_ge(y_ready, 2 * (u + 1))
                    if not (first and u == 0):
                        sp.dma_start(out[(i + B - 1) % B, :, :], y[:, :]).then_inc(store_dma, 16)
                        sp.wait_ge(store_dma, 16)
                        sp.sem_inc(store_dma, -16)
                    loads = 4
                    if last and u == 1:
                        loads = 1
                    else:
                        load_g(out[(i + 2) % B, :, :], (i + 2) // B, NW if last else NG)
                    sp.dma_start(wo[:, :], w[i // B, :, W_P:W_P + NO]).then_inc(load_dma, 16)
                    sp.wait_ge(load_dma, 16 * loads)
                    sp.sem_inc(load_dma, -16 * loads)
                    sp.sem_inc(g_in, 1)
                    sp.wait_ge(av_ready, 2 * u + 2)
                    kept["gather"](sp, 0, av_dma)
                if not last:
                    sp.sem_inc(parts_ready, -4)
                sp.sem_inc(av_ready, -4)
                sp.sem_inc(rden_ready, -2)
                sp.sem_inc(y_ready, -4)

            body(0, first=True)
            with sp.Fori(1, PAIRS - 1) as pair:
                body(pair)
            body(PAIRS - 1, last=True)
            sp.wait_ge(av_dma, 16 * (QUAD + 1))

        @block.gpsimd
        def _(pool):
            own = Own(pool, pool_own)
            set_up_constants(nc, pool, gmat, ident, consts)
            nc.gpsimd.memset(exponent[:, :], -0.5).then_inc(consts, 1)
            pool.wait_ge(consts, CONSTS)

            def coefficients(u):
                pool.wait_ge(coef_ready, u + 1)
                tt = nc.gpsimd.tensor_tensor
                own.done(tt(co[:, 4:5], co[:, 1:2], exponent[:, :], ALU.pow))
                own.done(tt(co[:, 2:3], co[:, 4:5], wg[:, W_GAMMA:W_GAMMA + 1], ALU.mult))
                own.done(tt(co[:, 5:6], gs[:, 0:1], co[:, 2:3], ALU.mult))
                own.done(tt(co[:, 3:4], wg[:, W_BETA:W_BETA + 1], co[:, 5:6], ALU.subtract))
                pool.sem_inc(scale_ready, 1)

            def split(n, which):
                pool.wait_ge(evacuated, n)
                split_parts(nc.gpsimd, own, which)
                pool.sem_inc(parts_ready, 1)

            def normalise(n):
                pool.wait_ge(o_in, n)
                nc.gpsimd.tensor_tensor(attn[:, :], num[:, :], rrep[:, :], ALU.mult).then_inc(attn_ready, 1)

            def split_max(n, th):
                pool.wait_ge(nmax_ready, n)
                new, to = nmax[:, th * MH:(th + 1) * MH], nparts[th]
                own.done(nc.gpsimd.tensor_scalar(to[:, 0, :], new, 1.0, None, ALU.mult))
                own.done(nc.gpsimd.tensor_tensor(nrest[:, :], new, to[:, 0, :], ALU.subtract))
                own.done(nc.gpsimd.tensor_scalar(to[:, 1, :], nrest[:, :], 1.0, None, ALU.mult))
                own.done(nc.gpsimd.tensor_tensor(to[:, 2, :], nrest[:, :], to[:, 1, :], ALU.subtract))
                pool.sem_inc(nparts_ready, 1)

            coefficients(0)
            for par in range(2):
                own.done(nc.gpsimd.memset(krep[par][KS:KM, :, :], 1.0))
                own.done(nc.gpsimd.memset(vT[par][:, :, :, CH:32], 1.0))
            pool.sem_inc(ones, 1)
            pool.sem_inc(coef_ready, -1)
            split_max(1, 0)
            pool.sem_inc(nmax_ready, -1)
            own.drain()
            def body(first=False, last=False):
                for u in range(2):
                    coefficients(u)
                    split_max(4 * u + 1, 1)
                    if not (last and u == 1):
                        split(2 * u + 1, "k")
                        split(2 * u + 2, "q")
                    if first and u == 0:
                        pool.sem_inc(o_in, 1)
                    else:
                        normalise(u + 1)
                    split_max(4 * u + 2, 0)
                    split_max(4 * u + 3, 1)
                    if not (last and u == 1):
                        split_max(4 * u + 4, 0)
                pool.sem_inc(coef_ready, -2)
                if not last:
                    pool.sem_inc(evacuated, -4)
                    pool.sem_inc(nmax_ready, -8)
                pool.sem_inc(o_in, -2)
                own.drain()

            body(first=True)
            with pool.Fori(1, PAIRS - 1):
                body()
            body(last=True)

        @block.vector
        def _(dve):
            own = Own(dve, dve_own)

            def statistics(part):
                if part < 2:
                    own.mark(nc.vector.bn_stats(bst[:, part, :], x_in[:, part * HALF:(part + 1) * HALF]))
                elif part == 2:
                    own.wait()
                    own.mark(nc.vector.bn_aggr(mv[:, :], bst[:, :, :]))
                else:
                    own.wait()
                    own.mark(nc.vector.tensor_copy(st2[:, 0:1], mv[:, 0:1]))
                    nc.vector.scalar_tensor_tensor(out=st2[:, 1:2], in0=mv[:, 0:1], scalar=mv[:, 0:1], in1=mv[:, 1:2],
                                                   op0=ALU.mult, op1=ALU.add).then_inc(stats_ready, 1)

            def coefficients(n, eps=EPS, of_next=False):
                dve.wait_ge(misc_for_dve, n)
                own.done(nc.vector.tensor_copy(gs[:, :], misc[:, 0:2]))
                if of_next:
                    own.done(nc.vector.tensor_copy(kept["value_weights"][:, :], misc[:, P:3 * P]))
                dve.sem_inc(misc_dve, 1)
                own.done(nc.vector.scalar_tensor_tensor(out=co[:, 0:1], in0=gs[:, 0:1], scalar=gs[:, 0:1],
                                                        in1=gs[:, 1:2], op0=ALU.mult, op1=ALU.subtract))
                nc.vector.tensor_scalar(co[:, 1:2], co[:, 0:1], -1.0, eps, ALU.mult, ALU.add).then_inc(coef_ready, 1)

            def values(n, par, c, of_next=False):
                dve.wait_ge(misc_for_dve, n)
                if of_next:
                    nc.vector.tensor_tensor(
                        full["v"][:, c * HALF:(c + 1) * HALF].rearrange("p (s c) -> p s c", s=4),
                        misc[:, :].rearrange("p (s c) -> p s c", s=4),
                        kept["value_weights"][:, P:2 * P].rearrange("p (a c) -> p a c", a=1).to_broadcast([P, 4, P]),
                        ALU.add).then_inc(misc_dve, 1)
                    return
                nc.vector.tensor_tensor(
                    vT[par][:, 4 * c:4 * c + 4, :, 0:CH],
                    misc[:, :].rearrange("p (s h c) -> p s h c", s=4, h=HEADS),
                    bvb[:, :].rearrange("p (a h c) -> p a h c", a=1, h=HEADS).to_broadcast([P, 4, HEADS, CH]),
                    ALU.add).then_inc(misc_dve, 1)

            def invert(n):
                dve.wait_ge(den_ready, n)
                nc.vector.reciprocal(rden[:, :], den[:, :]).then_inc(rden_ready, 1)

            def output(n, c, nothing=False):
                dve.wait_ge(misc_for_dve, n)
                if not nothing:
                    own.done(nc.vector.scalar_tensor_tensor(
                        out=y[:, c * HALF:(c + 1) * HALF], in0=misc[:, :], scalar=wo[:, P:P + 1],
                        in1=x_res[:, c * HALF:(c + 1) * HALF], op0=ALU.add, op1=ALU.add))
                dve.sem_inc(misc_dve, 1)
                dve.sem_inc(y_ready, 1)

            def maximum(n, unit, offset=0):
                for c in range(2):
                    dve.wait_ge(scores_ready, 2 * (n + offset) + c + 1)
                    reduce = nc.vector.tensor_reduce(half_nmax[:, c, unit:unit + 1], s_ps[bank(2 * n + c)][:, :],
                                                     AX.X, ALU.max, negate=True)
                    if unit % MH != MH - 1 or c == 0:
                        reduce.then_inc(max_done, 1)
                    else:
                        own.done(reduce)
                        dve.sem_inc(max_done, 1)
                        half = slice(unit + 1 - MH, unit + 1)
                        nc.vector.tensor_tensor(nmax[:, half], half_nmax[:, 0, half], half_nmax[:, 1, half],
                                                ALU.min).then_inc(nmax_ready, 1)

            dve.wait_ge(g_in, 1)
            for part in range(4):
                statistics(part)
            coefficients(1)
            for n, which in enumerate(("k", "q")):
                dve.wait_ge(kq_full, n + 1)
                split_parts(nc.vector, own, which)
                dve.sem_inc(parts_ready, 1)
            values(2, 0, 0)
            dve.wait_ge(misc_for_dve, 3)
            own.done(nc.vector.tensor_tensor(
                vT[0][:, 4:8, :, 0:CH], misc[:, :].rearrange("p (s h c) -> p s h c", s=4, h=HEADS),
                bvb[:, :].rearrange("p (a h c) -> p a h c", a=1, h=HEADS).to_broadcast([P, 4, HEADS, CH]), ALU.add))
            dve.sem_inc(misc_dve, 1)
            dve.sem_inc(y_ready, 1)
            dve.sem_inc(misc_for_dve, -3)
            for unit in range(2 * LEAD):
                maximum(unit - 2 * LEAD, unit, 2 * LEAD)
            dve.sem_inc(scores_ready, -4 * LEAD)
            dve.wait_ge(g_in, 2)
            for part in range(4):
                statistics(part)
            own.wait()
            dve.sem_inc(g_in, -2)
            own.drain()
            def body(first=False, last=False):
                for s in range(4):
                    u = s // 2
                    no_output = first and u == 0
                    for k in range(GROUPS):
                        if s % 2 == 0:
                            base = 5 * u
                            if k == AVG + 1:
                                coefficients(base + 1, *((NEXT_EPS, True) if last and u == 1 else ()))
                            if k == 5:
                                if no_output:
                                    dve.sem_inc(den_ready, 1)
                                else:
                                    invert(u + 1)
                            if k == V0 + 1:
                                values(base + 2, 1 - u, 0, last and u == 1)
                            if k == V1 + 1:
                                values(base + 3, 1 - u, 1, last and u == 1)
                            if k == O0 + 1:
                                output(base + 4, 0, no_output)
                        for unit in (2 * k, 2 * k + 1):
                            if s % 2 == 1 and unit % 2 == 1 and STATS <= k < STATS + 4 and not (last and s == 3):
                                if k == STATS:
                                    dve.wait_ge(g_in, u + 1)
                                statistics(k - STATS)
                            if not (last and s == 3 and unit + 2 * LEAD >= UNITS):
                                maximum(UNITS * s + unit, (unit + 2 * LEAD) % UNITS)
                    if s % 2 == 0:
                        output(5 * u + 5, 1, no_output)
                if last:
                    dve.sem_inc(scores_ready, 4 * LEAD)
                if not last:
                    dve.sem_inc(g_in, -2)
                dve.sem_inc(misc_for_dve, -10)
                dve.sem_inc(den_ready, -2)
                dve.sem_inc(scores_ready, -4 * STEP)
                own.drain()

            body(first=True)
            with dve.Fori(1, PAIRS - 1):
                body()
            body(last=True)

        @block.scalar
        def _(act):
            own = Own(act, act_own)

            def evacuate(n, which, c, hold=False):
                act.wait_ge(misc_for_act, n)
                bias = wg[:, W_BQ:W_BQ + 1] if which == "q" else wg[:, W_BK:W_BK + 1]
                cols = slice(c * HALF, (c + 1) * HALF)
                own.mark(nc.scalar.activation(full[which][:, cols], misc[:, :], ACT.Identity, bias=bias))

            def leading(which, c):
                cols = slice(c * HALF, (c + 1) * HALF)
                own.mark(nc.scalar.copy(parts[which][:, 0, cols], full[which][:, cols]))

            def normalise(c):
                cols = slice(c * HALF, (c + 1) * HALF)
                nc.scalar.activation(h[:, cols], x_in[:, cols], ACT.Identity, bias=co[:, 3:4],
                                     scale=co[:, 2:3]).then_inc(h_ready, 1)

            def max_rows(n, th):
                act.wait_ge(misc_for_act, n)
                own.mark(nc.scalar.copy(mrow[th][:, :], misc_bf[0:3 * MH, 0:P]))

            def send_max_rows(step, th):
                own.wait()
                act.sem_inc(misc_act, 1)
                par, quad = step // 2 % 2, step % 2
                act.dma_start(qrep[par][KS:KM, th, quad * QUAD:(quad + 1) * QUAD, :],
                              mrow[th][:, :]).then_inc(mrow_dma, 16)

            def sums(n, quad, th):
                act.wait_ge(pv_done, n + 2)
                own.mark(nc.scalar.copy(av[quad][:, th * HALF:(th + 1) * HALF], pv_ps[:, :]))

            act.wait_ge(scale_ready, 1)
            act.sem_inc(scale_ready, -1)
            normalise(0)
            normalise(1)
            for n, (which, c) in enumerate((("k", 0), ("k", 1), ("q", 0), ("q", 1))):
                evacuate(n + 1, which, c)
                own.wait()
                act.sem_inc(misc_act, 1)
                leading(which, c)
                own.wait()
                if c == 1:
                    act.sem_inc(kq_full, 1)
            max_rows(5, 0)
            send_max_rows(0, 0)
            act.sem_inc(misc_for_act, -5)
            own.drain()
            def body(first=False, last=False):
                for s in range(4):
                    u, quad = s // 2, s % 2
                    base = 8 * u + 6 * quad
                    order = [MAX1, MAX0] if quad else [K0, K1, MAX1, Q0, Q1, MAX0]
                    if last and s == 3:
                        order = [MAX1]
                    for k in range(GROUPS):
                        g = GROUPS * s + k
                        act.wait_ge(pv_done, g + 1)
                        sums_due = k % TILES == 1 and not (first and g == 1)
                        if sums_due:
                            if k > TILES and quad == 0:
                                if first and u == 0:
                                    act.sem_inc(av_free, 1)
                                act.wait_ge(av_free, u + 1)
                            sums(g - 1, quad if k > TILES else 1 - quad, 0 if k > TILES else 1)
                        for j in range(QUAD):
                            n = QUAD * g + j
                            act.wait_ge(st_ready, n + 1)
                            nc.scalar.activation(probs[g % 2][:, j, :], st_ps[bank(n)][:, :], ACT.Exp,
                                                 scale=1.0 / CH ** 0.5).then_inc(exp_done, 1)
                            if j == 0 and sums_due:
                                own.wait()
                                act.sem_inc(pv_free, 1)
                                if k < TILES:
                                    act.sem_inc(av_ready, 1)
                            if j == 0 and k - 1 in order:
                                if k - 1 == MAX1:
                                    send_max_rows(s, 1)
                                elif k - 1 == MAX0:
                                    send_max_rows(s + 1, 0)
                                else:
                                    own.wait()
                                    act.sem_inc(misc_act, 1)
                            if quad == 0 and not (last and u == 1):
                                if j == 1 and k - 1 in (K0, K1, Q0, Q1):
                                    leading("k" if k - 1 in (K0, K1) else "q", int(k - 1 in (K1, Q1)))
                                if j == 3 and k - 1 in (K1, Q1):
                                    own.wait()
                                    act.sem_inc(evacuated, 1)
                            if j % 2 == 1 and k == K0 - 1 and quad == 0:
                                if j == 1:
                                    act.wait_ge(scale_ready, u + 1)
                                normalise(j // 2)
                        if k in order:
                            n = base + order.index(k) + 1
                            if k in (MAX0, MAX1):
                                max_rows(n, 1 if k == MAX1 else 0)
                            else:
                                if k == K0:
                                    act.wait_ge(parts_free, u + 1)
                                evacuate(n, "k" if k in (K0, K1) else "q", int(k in (K1, Q1)))
                if not last:
                    act.sem_inc(misc_for_act, -16)
                act.sem_inc(pv_done, -4 * GROUPS)
                act.sem_inc(st_ready, -4 * GROUPS * QUAD)
                act.sem_inc(av_free, -2)
                act.sem_inc(scale_ready, -2)
                act.sem_inc(parts_free, -2)
                own.drain()

            body(first=True)
            with act.Fori(1, PAIRS - 1):
                body()
            body(last=True)
            act.wait_ge(pv_done, 2)
            own.done(nc.scalar.copy(av[1][:, HALF:T], pv_ps[:, :]))

        @block.tensor
        def _(pe):
            def project(c, column, ready):
                nc.tensor.matmul(misc[:, :], wg[:, column:column + P], h[:, c * HALF:(c + 1) * HALF],
                                 start=True, stop=True).then_inc(ready, 1)

            def project_values(c, of_next=False):
                weights = kept["value_weights"][:, 0:P] if of_next else wg[:, W_V:W_V + P]
                for n in range(4):
                    t = 4 * c + n
                    product = nc.tensor.matmul(misc[:, n * P:(n + 1) * P], h[:, t * P:(t + 1) * P],
                                               weights, start=True, stop=True)
                product.then_inc(misc_for_dve, 1)

            def project_output(c):
                nc.tensor.matmul(misc[:, :], wo[:, 0:P], attn[:, c * HALF:(c + 1) * HALF],
                                 start=True, stop=True).then_inc(misc_for_dve, 1)

            def average():
                nc.tensor.matmul(misc[:, 0:2], gmat[:, :], st2[:, :], start=True, stop=True).then_inc(misc_for_dve, 1)

            def transpose_max(th):
                nc.tensor.transpose(misc_bf[0:3 * MH, 0:P], nparts[th][:, :, :].rearrange("p a b -> p (a b)"),
                                    ident[:, :]).then_inc(misc_for_act, 1)

            def group_products(step, k):
                par, quad = step // 2, step % 2
                for j in range(QUAD):
                    product = nc.tensor.matmul(pv_ps[32 * j:32 * j + 32, :], vT[par][:, k % TILES, quad * QUAD + j, :],
                                               probs[k % 2][:, j, :], start=(k % TILES == 0),
                                               stop=(k % TILES == TILES - 1))
                return product

            def row_scores(n, par, quad, unit, c):
                th, head, tile = unit // MH, quad * QUAD + unit % MH // (TILES // 2), unit % (TILES // 2)
                nc.tensor.matmul(s_ps[bank(n)][:, :], qrep[par][0:KS, th, head, tile * P:(tile + 1) * P],
                                 krep[par][0:KS, head, c * HALF:(c + 1) * HALF],
                                 start=True, stop=True).then_inc(scores_ready, 1)

            pe.sem_inc(pv_done, 2)
            pe.sem_inc(exp_done, QUAD)
            pe.sem_inc(pv_free, 1)
            pe.wait_ge(consts, 3)
            pe.wait_ge(stats_ready, 1)
            average()
            pe.wait_ge(misc_dve, 1)
            pe.wait_ge(h_ready, 2)
            project(0, W_K, misc_for_act)
            pe.wait_ge(misc_act, 1)
            project(1, W_K, misc_for_act)
            pe.wait_ge(misc_act, 2)
            project(0, W_Q, misc_for_act)
            pe.wait_ge(misc_act, 3)
            project(1, W_Q, misc_for_act)
            pe.wait_ge(misc_act, 4)
            project_values(0)
            pe.wait_ge(misc_dve, 2)
            project_values(1)
            pe.wait_ge(misc_dve, 3)
            pe.wait_ge(rep_ready, 1)
            for unit in range(2 * LEAD):
                for c in range(2):
                    n = 2 * unit + c - 4 * LEAD
                    if last_in_bank(n) >= -4 * LEAD:
                        pe.wait_ge(max_done, last_in_bank(n) + 1 + 4 * LEAD)
                    row_scores(n, 0, 0, unit, c)
                if unit == MH + 3:
                    pe.wait_ge(nparts_ready, 1)
                    transpose_max(0)
            pe.wait_ge(ones, 1)
            pe.wait_ge(consts, CONSTS)
            pe.sem_inc(stats_ready, -1)
            pe.sem_inc(misc_dve, -3)
            pe.sem_inc(h_ready, -2)
            pe.sem_inc(misc_act, -4)
            pe.sem_inc(rep_ready, -1)
            pe.wait_ge(max_done, 4 * LEAD - 4)
            pe.sem_inc(max_done, -(4 * LEAD - 4))
            pe.sem_inc(nparts_ready, -1)

            def body(first=False, last=False):
                for s in range(4):
                    u, quad = s // 2, s % 2
                    par = u
                    a, d = 8 * u, 5 * u

                    def products(k):
                        g = GROUPS * s + k
                        pe.wait_ge(exp_done, QUAD * (g + 2))
                        if k % TILES == 0:
                            pe.wait_ge(pv_free, 2 * s + k // TILES + 1)
                        group_products((s if k >= 0 else s - 1) % 4, k % GROUPS).then_inc(pv_done, 1)

                    def in_shared_bank(k):
                        if k == MAX1:
                            if quad == 0:
                                pe.wait_ge(misc_act, a + 3)
                            else:
                                pe.wait_ge(misc_dve, d + 5)
                            pe.wait_ge(nparts_ready, 2 * s + 1)
                            transpose_max(1)
                        elif k == MAX0 and last and s == 3:
                            pass
                        elif k == MAX0:
                            if quad == 0:
                                pe.wait_ge(misc_dve, d + 3)
                            else:
                                pe.wait_ge(misc_act, a + 8)
                            pe.wait_ge(nparts_ready, 2 * s + 2)
                            transpose_max(0)
                        elif quad == 1:
                            pass
                        elif k == AVG:
                            pe.wait_ge(misc_act, a + 1)
                            pe.wait_ge(stats_ready, u + 1)
                            if last and u == 1:
                                combine_weights(nc, misc, wg)
                            average()
                        elif k == K0:
                            pe.wait_ge(misc_dve, d + 1)
                            pe.wait_ge(h_ready, 2 * (u + 1))
                            project(0, W_K, misc_for_act)
                        elif k == K1:
                            pe.wait_ge(misc_act, a + 2)
                            project(1, W_K, misc_for_act)
                        elif k == Q0:
                            pe.wait_ge(misc_act, a + 4)
                            project(0, W_Q, misc_for_act)
                        elif k == Q1:
                            pe.wait_ge(misc_act, a + 5)
                            project(1, W_Q, misc_for_act)
                        elif k == V0:
                            pe.wait_ge(misc_act, a + 6)
                            project_values(0, last and u == 1)
                        elif k == V1:
                            pe.wait_ge(misc_dve, d + 2)
                            project_values(1, last and u == 1)
                        elif k == O0:
                            pe.wait_ge(misc_act, a + 7)
                            if first and u == 0:
                                pe.sem_inc(attn_ready, 1)
                                pe.sem_inc(misc_for_dve, 1)
                            else:
                                pe.wait_ge(attn_ready, u + 1)
                                project_output(0)
                        elif k == O1:
                            pe.wait_ge(misc_dve, d + 4)
                            if first and u == 0:
                                pe.sem_inc(misc_for_dve, 1)
                            else:
                                project_output(1)

                    def m_unit(unit, half):
                        of_next, m = divmod(unit + 2 * LEAD, UNITS)
                        ms = s + of_next
                        if last and ms == 4:
                            return
                        n = STEP * s + 2 * unit + half
                        pe.wait_ge(max_done, last_in_bank(n) + 1 + 4)
                        if m == 0 and half == 0 and ms % 2 == 0:
                            pe.wait_ge(rep_ready, u + 1)
                        row_scores(n, ms // 2 % 2, ms % 2, m, half)

                    for k in range(GROUPS):
                        th, st = k // TILES, k % TILES
                        if st == 0:
                            pe.wait_ge(mrow_dma, 16 * (2 * s + th + 1))
                        for j in range(QUAD):
                            n = QUAD * (GROUPS * s + k) + j
                            head = quad * QUAD + j
                            pe.wait_ge(exp_done, last_in_bank(n) + 1 + QUAD)
                            nc.tensor.matmul(st_ps[bank(n)][:, :], krep[par][0:KM, head, st * P:(st + 1) * P],
                                             qrep[par][0:KM, th, head, :],
                                             start=True, stop=True).then_inc(st_ready, 1)
                            if j == 2 and not (first and n < QUAD):
                                products(k - 1)
                            m_unit(2 * k + j // 2, j % 2)
                            if j == 3:
                                in_shared_bank(k)
                if last:
                    return
                pe.sem_inc(mrow_dma, -16 * 8)
                pe.sem_inc(rep_ready, -2)
                pe.sem_inc(exp_done, -4 * GROUPS * QUAD)
                pe.sem_inc(max_done, -4 * STEP)
                pe.sem_inc(pv_free, -8)
                pe.sem_inc(stats_ready, -2)
                pe.sem_inc(misc_act, -16)
                pe.sem_inc(misc_dve, -10)
                pe.sem_inc(h_ready, -4)
                pe.sem_inc(nparts_ready, -8)
                pe.sem_inc(attn_ready, -2)
            body(first=True)
            with pe.Fori(1, PAIRS - 1):
                body()
            body(last=True)
            pe.wait_ge(exp_done, QUAD * (4 * GROUPS + 1))
            group_products(3, GROUPS - 1).then_inc(pv_done, 1)


def one_head(nc, ctx0, kept, w, out):
    EPS = 1e-6
    SCALE = float(P) ** -0.5
    HT = TILES // 2
    PAIRS = 2 * B // 2
    BODY = 2 * TILES
    STATS = 3
    PLACES = {"avg": (0, 1), "k0": (1, 2), "k1": (2, 2), "q0": (3, 2), "v0": (5, 1),
              "q1": (6, 2), "v1": (7, 1)}
    FIRST_PLACES = dict(PLACES, o0=(3, 0), o1=(4, 1))
    FOR_ACT = ("k0", "k1", "q0", "q1")
    HI, LO = 0, 1

    def shared_bank(first, last):
        places, number, before = [], {}, {}
        taken = {"act": 0, "dve": 0}
        previous = ("dve", 1)
        for u in range(2):
            chosen = FIRST_PLACES if first and u == 0 else {} if last and u == 1 else PLACES
            places.append({place: name for name, place in chosen.items()})
            for name in sorted(chosen, key=chosen.get):
                reader = "act" if name in FOR_ACT else "dve"
                taken[reader] += 1
                number[u, name] = taken[reader]
                before[u, name] = previous
                previous = (reader, taken[reader] + (reader == "dve"))
        return places, number, before, taken

    ctx = ExitStack()
    with ctx:
        def sb(name, shape, dt=F32):
            return ctx.enter_context(nc.sbuf_tensor("o_" + name, shape, dt))

        def psum(name, shape):
            return ctx.enter_context(nc.psum_tensor("o_" + name, shape, F32))

        def sem(name):
            return ctx0.enter_context(nc.semaphore("o_" + name))

        q = [sb(f"q{i}", [P, 2, T], F32R) for i in range(2)]
        k = [sb(f"k{i}", [P, 2, T], F32R) for i in range(2)]
        vT = [sb(f"vT{i}", [P, 2, TILES, P], F32R) for i in range(2)]
        full, x_res, wo, attn = kept["full"], kept["x_res"], kept["wo"], kept["attn"]
        probs = [sb(f"probs{i}", [P, T]) for i in range(2)]
        pT = [sb(f"pT{i}", [P, 2, TILES, HALF], F32R) for i in range(2)]
        x_in = sb("x_in", [P, T])
        wg = [sb(f"wg{i}", [P, NW]) for i in range(2)]
        value_weights = kept["value_weights"]
        h = sb("h", [P, T])
        y = sb("y", [P, T])
        ident = sb("ident", [P, P])
        bst = sb("bst", [P, 2, 6])
        mv = sb("mv", [P, 2])
        st2 = sb("st2", [P, 2])
        gs = sb("gs", [P, 2])
        co = sb("co", [P, 6])
        gmat, exponent = kept["gmat"], kept["exponent"]
        nmax = sb("nmax", [P, 2])
        bias = sb("bias", [P, 2])
        rsum = sb("rsum", [P, 2])
        rinv = sb("rinv", [P, 2])

        s_ps = [psum(f"s{i}", [P, 2, HALF]) for i in range(2)]
        t_ps = [psum(f"t{i}", [P, HT, P]) for i in range(2)]
        pv_ps = psum("pv", [P, HALF])
        misc = psum("misc", [P, HALF])

        consts = sem("consts")
        hi_of_first = sem("hi_of_first")
        rows_dma = sem("rows_dma")
        den_ready = sem("den_ready")
        rden_ready = sem("rden_ready")
        rrep_ready = sem("rrep_ready")
        store_dma = sem("store_dma")
        s_ready = sem("s_ready")
        bias_ready = sem("bias_ready")
        exp_ready = sem("exp_ready")
        rinv_ready = sem("rinv_ready")
        p_ready = sem("p_ready")
        t_ready = sem("t_ready")
        hi_ready = sem("hi_ready")
        t_free = sem("t_free")
        pv_ready = sem("pv_ready")
        pv_free = sem("pv_free")
        half_ready = sem("half_ready")
        attn_ready = sem("attn_ready")
        misc_act = sem("misc_act")
        misc_dve = sem("misc_dve")
        misc_for_act = sem("misc_for_act")
        misc_for_dve = sem("misc_for_dve")
        kq_full = sem("kq_full")
        v_full = sem("v_full")
        kq_parts = sem("kq_parts")
        v_parts = sem("v_parts")
        stats_ready = sem("stats_ready")
        coef_ready = sem("coef_ready")
        scale_ready = sem("scale_ready")
        h_ready = sem("h_ready")
        x_dma = sem("x_dma")
        w_dma = [sem(f"w_dma{i}") for i in range(2)]
        o_dma = sem("o_dma")
        x_used = sem("x_used")
        w_used = sem("w_used")
        y_ready = sem("y_ready")
        act_own, dve_own, pool_own = sem("act_own"), sem("dve_own"), sem("pool_own")

        block = ctx.enter_context(nc.Block())

        @block.sync
        def _(sp):
            def load_weights(par, layer):
                sp.dma_start(wg[par][:, :], w[layer, :, :]).then_inc(w_dma[par], 16)

            sp.dma_start(x_in[:, :], out[1, :, :]).then_inc(x_dma, 16)
            kept["gather"](sp, 1, rows_dma)
            load_weights(1, 2)
            sp.dma_start(x_res[:, :], out[B - 1, :, :]).then_inc(o_dma, 48)
            sp.wait_ge(rows_dma, 16 * (QUAD + 1))
            sp.dma_start(kept["den"][:, :], kept["den_dram"].rearrange("h (p t) -> (h p) t", p=CH)).then_inc(rows_dma, 16)
            sp.wait_ge(rows_dma, 16 * (QUAD + 2))
            sp.sem_inc(den_ready, 1)
            sp.wait_ge(rden_ready, 1)
            sp.dma_start(kept["rden_dram"].rearrange("h (p t) -> (h p) t", p=CH), kept["rden"][:, :]).then_inc(rows_dma, 16)
            sp.wait_ge(rows_dma, 16 * (QUAD + 3))
            sp.dma_start(kept["rrep"][:, :], kept["rden_dram"].rearrange("h (a t) -> h a t", a=1).to_broadcast([HEADS, CH, T])).then_inc(rows_dma, 16)
            sp.wait_ge(rows_dma, 16 * (QUAD + 4))
            sp.sem_inc(rrep_ready, 1)
            sp.sem_inc(w_used, 1)

            def body(pair, last=False):
                for u in range(2):
                    i = 2 * pair + u
                    if not last:
                        sp.wait_ge(w_used, u + 1)
                        load_weights(u, ((i + 2) // B + 2) % 4)
                        sp.wait_ge(x_used, u + 1)
                        sp.dma_start(x_in[:, :], out[(i + 2) % B, :, :]).then_inc(x_dma, 16)
                    sp.wait_ge(y_ready, 2 * (u + 1))
                    sp.dma_start(out[(i + B - 1) % B, :, :], y[:, :]).then_inc(o_dma, 16)
                    sp.dma_start(x_res[:, :], out[i % B, :, :]).then_inc(o_dma, 16)
                    sp.dma_start(wo[:, :], w[i // B + 2, :, W_P:W_P + NO]).then_inc(o_dma, 16)
                if not last:
                    sp.sem_inc(w_used, -2)
                    sp.sem_inc(x_used, -2)
                sp.sem_inc(y_ready, -4)

            with sp.Fori(0, PAIRS - 1) as pair:
                body(pair)
            body(PAIRS - 1, last=True)
            for c in range(2):
                sp.wait_ge(y_ready, c + 1)
                cols = slice(c * HALF, (c + 1) * HALF)
                sp.dma_start(out[B - 1, :, cols], y[:, cols]).then_inc(store_dma, 16)
            sp.wait_ge(store_dma, 32)

        @block.gpsimd
        def _(pool):
            own = Own(pool, pool_own)
            nc.gpsimd.tensor_scalar(ident[:, :], kept["ident"][:, :], 1.0, None, ALU.mult).then_inc(consts, 1)

            def coefficients(n, par):
                pool.wait_ge(coef_ready, n)
                tt = nc.gpsimd.tensor_tensor
                own.done(tt(co[:, 4:5], co[:, 1:2], exponent[:, :], ALU.pow))
                own.done(tt(co[:, 2:3], co[:, 4:5], wg[par][:, W_GAMMA:W_GAMMA + 1], ALU.mult))
                own.done(tt(co[:, 5:6], gs[:, 0:1], co[:, 2:3], ALU.mult))
                tt(co[:, 3:4], wg[par][:, W_BETA:W_BETA + 1], co[:, 5:6], ALU.subtract).then_inc(scale_ready, 1)

            def split(source, hi, lo, ready):
                own.done(nc.gpsimd.tensor_copy(hi, source))
                nc.gpsimd.tensor_tensor(lo, source, hi.bitcast(F32), ALU.subtract).then_inc(ready, 1)

            def split_kq(n, operand, name, c):
                pool.wait_ge(kq_full, n)
                cols = slice(c * HALF, (c + 1) * HALF)
                split(full[name][:, cols], operand[:, HI, cols], operand[:, LO, cols], kq_parts)

            def split_v(par, c):
                tiles = slice(c * HT, (c + 1) * HT)
                split(full["v"][:, c * HALF:(c + 1) * HALF].rearrange("p (s c) -> p s c", s=HT),
                      vT[par][:, HI, tiles, :], vT[par][:, LO, tiles, :], v_parts)

            def stage_g(u, par, finish=False):
                coefficients(u + 1, par)
                if finish:
                    pool.wait_ge(rrep_ready, 1)
                    own.done(nc.gpsimd.tensor_tensor(attn[:, :], kept["num"][:, :], kept["rrep"][:, :], ALU.mult))
                    pool.sem_inc(attn_ready, 1)
                split_kq(4 * u + 1, k[par], "k", 0)
                split_kq(4 * u + 2, k[par], "k", 1)
                split_kq(4 * u + 3, q[par], "q", 0)
                pool.wait_ge(v_full, 2 * u + 1)
                split_v(par, 0)
                split_kq(4 * u + 4, q[par], "q", 1)
                pool.wait_ge(v_full, 2 * u + 2)
                split_v(par, 1)

            split_v(0, 0)
            split_v(0, 1)
            own.drain()

            def body(first=False, last=False):
                for u in range(2 - last):
                    stage_g(u, 1 - u, finish=first and u == 0)
                if not last:
                    pool.sem_inc(coef_ready, -2)
                    pool.sem_inc(kq_full, -8)
                    pool.sem_inc(v_full, -4)
                own.drain()

            body(first=True)
            with pool.Fori(1, PAIRS - 1):
                body()
            body(last=True)

        @block.vector
        def _(dve):
            own = Own(dve, dve_own)

            def statistics(part):
                if part < 2:
                    own.mark(nc.vector.bn_stats(bst[:, part, :], x_in[:, part * HALF:(part + 1) * HALF]))
                    return
                own.wait()
                if part == 2:
                    own.mark(nc.vector.bn_aggr(mv[:, :], bst[:, :, :]))
                else:
                    own.done(nc.vector.tensor_copy(st2[:, 0:1], mv[:, 0:1]))
                    nc.vector.scalar_tensor_tensor(out=st2[:, 1:2], in0=mv[:, 0:1], scalar=mv[:, 0:1], in1=mv[:, 1:2],
                                                   op0=ALU.mult, op1=ALU.add).then_inc(stats_ready, 1)

            def coefficients(n):
                dve.wait_ge(misc_for_dve, n)
                own.done(nc.vector.tensor_copy(gs[:, :], misc[:, 0:2]))
                own.done(nc.vector.scalar_tensor_tensor(out=co[:, 0:1], in0=gs[:, 0:1], scalar=gs[:, 0:1],
                                                        in1=gs[:, 1:2], op0=ALU.mult, op1=ALU.subtract))
                nc.vector.tensor_scalar(co[:, 1:2], co[:, 0:1], -1.0, EPS, ALU.mult, ALU.add).then_inc(coef_ready, 1)
                own.done(nc.vector.tensor_copy(value_weights[:, :], misc[:, P:3 * P]))
                dve.sem_inc(misc_dve, 1)

            def values(n, c):
                dve.wait_ge(misc_for_dve, n)
                own.done(nc.vector.tensor_tensor(
                    full["v"][:, c * HALF:(c + 1) * HALF].rearrange("p (s c) -> p s c", s=HT),
                    misc[:, :].rearrange("p (s c) -> p s c", s=HT),
                    value_weights[:, P:2 * P].rearrange("p (a c) -> p a c", a=1).to_broadcast([P, HT, P]), ALU.add))
                dve.sem_inc(misc_dve, 1)
                dve.sem_inc(v_full, 1)
                if c == 1:
                    dve.sem_inc(w_used, 1)

            def output(source, c):
                own.done(nc.vector.scalar_tensor_tensor(
                    out=y[:, c * HALF:(c + 1) * HALF], in0=source, scalar=wo[:, P:P + 1],
                    in1=x_res[:, c * HALF:(c + 1) * HALF], op0=ALU.add, op1=ALU.add))
                dve.sem_inc(y_ready, 1)

            def layer_1_output(n, c):
                dve.wait_ge(misc_for_dve, n)
                output(misc[:, :], c)
                dve.sem_inc(misc_dve, 1)

            def finish(n, c):
                dve.wait_ge(half_ready, n)
                output(attn[:, c * HALF:(c + 1) * HALF], c)

            def maximum(n, tile):
                dve.wait_ge(s_ready, n)
                b = tile % 2
                own.done(nc.vector.tensor_reduce(nmax[:, b:b + 1], s_ps[b][:, :, :], AX.XY, ALU.max, negate=True))
                nc.vector.tensor_scalar(bias[:, b:b + 1], nmax[:, b:b + 1], SCALE, None, ALU.mult).then_inc(bias_ready, 1)

            def invert(n, tile):
                dve.wait_ge(exp_ready, n)
                b = tile % 2
                nc.vector.reciprocal(rinv[:, b:b + 1], rsum[:, b:b + 1]).then_inc(rinv_ready, 1)

            def rests(m):
                for bank in range(2):
                    dve.wait_ge(hi_ready, 2 * m + bank + 1)
                    to = (slice(None), slice(bank * HT, (bank + 1) * HT), slice(m % HT * P, (m % HT + 1) * P))
                    pt = pT[m // HT % 2]
                    nc.vector.tensor_tensor(pt[:, LO, :, :][to], t_ps[bank][:, :, :],
                                            pt[:, HI, :, :][to].bitcast(F32), ALU.subtract).then_inc(t_free, 1)

            def split_rest(n, operand, name):
                dve.wait_ge(hi_of_first, n)
                nc.vector.tensor_tensor(operand[:, LO, :], full[name][:, :], operand[:, HI, :].bitcast(F32),
                                        ALU.subtract).then_inc(kq_parts, 2)

            dve.sem_inc(half_ready, 2)
            split_rest(1, k[0], "k")
            split_rest(2, q[0], "q")
            maximum(1, 0)
            invert(1, 0)
            maximum(2, 1)
            invert(2, 1)
            dve.wait_ge(x_dma, 16)
            for part in range(4):
                statistics(part)
            dve.wait_ge(den_ready, 1)
            nc.vector.reciprocal(kept["rden"][:, :], kept["den"][:, :]).then_inc(rden_ready, 1)
            dve.sem_inc(x_dma, -16)
            dve.sem_inc(s_ready, -2)
            dve.sem_inc(exp_ready, -2)
            own.drain()

            def body(first=False, last=False):
                _, number, _, taken = shared_bank(first, last)
                for m in range(BODY):
                    u, tile = m // TILES, m % TILES
                    last_it = last and u == 1
                    first_it = first and u == 0
                    more = not (last and m >= BODY - 2)
                    if more:
                        maximum(m + 1, m + 2)
                    if tile == PLACES["avg"][0] and not last_it:
                        coefficients(number[u, "avg"])
                    if tile == FIRST_PLACES["o0"][0] and first_it:
                        layer_1_output(number[u, "o0"], 0)
                    rests(m)
                    if tile == 1:
                        dve.wait_ge(o_dma, 48 * (u + 1))
                    if tile % HT == 2 and not first_it:
                        finish(m // HT + 1, 0 if tile < HT else 1)
                    if tile == PLACES["v0"][0] and not last_it:
                        values(number[u, "v0"], 0)
                    if tile == FIRST_PLACES["o1"][0] and first_it:
                        layer_1_output(number[u, "o1"], 1)
                    if tile == PLACES["v1"][0] and not last_it:
                        values(number[u, "v1"], 1)
                    if more:
                        invert(m + 1, m + 2)
                    if STATS <= tile < STATS + 4 and not last:
                        if tile == STATS:
                            dve.wait_ge(x_dma, 16 * (u + 1))
                        statistics(tile - STATS)
                dve.sem_inc(misc_for_dve, -taken["dve"])
                dve.sem_inc(o_dma, -96)
                dve.sem_inc(half_ready, -4)
                if not last:
                    dve.sem_inc(x_dma, -32)
                    dve.sem_inc(s_ready, -BODY)
                    dve.sem_inc(exp_ready, -BODY)
                dve.sem_inc(hi_ready, -2 * BODY)
                own.drain()

            body(first=True)
            with dve.Fori(1, PAIRS - 1):
                body()
            body(last=True)
            dve.wait_ge(o_dma, 48)
            finish(1, 0)
            finish(2, 1)

        @block.scalar
        def _(act):
            own = Own(act, act_own)

            def normalise(c):
                cols = slice(c * HALF, (c + 1) * HALF)
                own.mark(nc.scalar.activation(h[:, cols], x_in[:, cols], ACT.Identity, bias=co[:, 3:4],
                                              scale=co[:, 2:3]))

            def normalised():
                normalise(0)
                normalise(1)
                own.wait()
                act.sem_inc(h_ready, 1)
                act.sem_inc(x_used, 1)

            def evacuate(n, name, c, par):
                act.wait_ge(misc_for_act, n)
                column = W_BK if name == "k" else W_BQ
                own.done(nc.scalar.activation(full[name][:, c * HALF:(c + 1) * HALF], misc[:, :], ACT.Identity,
                                              bias=wg[par][:, column:column + 1]))
                act.sem_inc(misc_act, 1)
                act.sem_inc(kq_full, 1)

            def exponentials(n, tile):
                act.wait_ge(bias_ready, n)
                b = tile % 2
                nc.scalar.activation(probs[b][:, :], s_ps[b][:, :, :], ACT.Exp, bias=bias[:, b:b + 1], scale=SCALE,
                                     accum_out=rsum[:, b:b + 1]).then_inc(exp_ready, 1)

            def divide(n, tile):
                act.wait_ge(rinv_ready, n)
                b = tile % 2
                nc.scalar.activation(probs[b][:, :], probs[b][:, :], ACT.Copy, scale=rinv[:, b:b + 1]).then_inc(p_ready, 1)

            def products(n, c):
                act.wait_ge(pv_ready, n)
                own.done(nc.scalar.copy(attn[:, c * HALF:(c + 1) * HALF], pv_ps[:, :]))
                act.sem_inc(pv_free, 1)
                act.sem_inc(half_ready, 1)

            for operand, name in ((k[0], "k"), (q[0], "q")):
                nc.scalar.copy(operand[:, HI, :], full[name][:, :]).then_inc(hi_of_first, 1)
            exponentials(1, 0)
            divide(1, 0)
            exponentials(2, 1)
            act.sem_inc(bias_ready, -2)
            act.sem_inc(rinv_ready, -1)
            act.sem_inc(pv_ready, 2)

            def body(first=False, last=False):
                _, number, _, taken = shared_bank(first, last)
                for m in range(BODY):
                    u, tile = m // TILES, m % TILES
                    if tile % HT == 0 and not (first and u == 0):
                        products(m // HT + 1, 0 if tile < HT else 1)
                    for name in FOR_ACT:
                        if tile == PLACES[name][0] + 1 and not (last and u == 1):
                            evacuate(number[u, name], name[0], int(name[1]), 1 - u)
                    if not (last and m == BODY - 1):
                        divide(m + 1, m + 1)
                    for bank in range(2):
                        act.wait_ge(t_ready, 2 * m + bank + 1)
                        nc.scalar.copy(pT[m // HT % 2][:, HI, bank * HT:(bank + 1) * HT, m % HT * P:(m % HT + 1) * P],
                                       t_ps[bank][:, :, :]).then_inc(hi_ready, 1)
                    if not (last and m >= BODY - 2):
                        exponentials(m + 1, m + 2)
                    if tile == PLACES["avg"][0] and not (last and u == 1):
                        act.wait_ge(scale_ready, u + 1)
                        normalised()
                if not last:
                    act.sem_inc(bias_ready, -BODY)
                    act.sem_inc(rinv_ready, -BODY)
                    act.sem_inc(scale_ready, -2)
                act.sem_inc(misc_for_act, -taken["act"])
                act.sem_inc(t_ready, -2 * BODY)
                act.sem_inc(pv_ready, -4)
                own.drain()

            body(first=True)
            with act.Fori(1, PAIRS - 1):
                body()
            body(last=True)
            products(1, 0)
            products(2, 1)

        @block.tensor
        def _(pe):
            def project(par, c, column):
                nc.tensor.matmul(misc[:, :], wg[par][:, column:column + P], h[:, c * HALF:(c + 1) * HALF],
                                 start=True, stop=True).then_inc(misc_for_act, 1)

            def project_values(c):
                for n in range(4):
                    t = 4 * c + n
                    last = nc.tensor.matmul(misc[:, n * P:(n + 1) * P], h[:, t * P:(t + 1) * P],
                                            value_weights[:, 0:P], start=True, stop=True)
                last.then_inc(misc_for_dve, 1)

            def project_output(c):
                nc.tensor.matmul(misc[:, :], wo[:, 0:P], attn[:, c * HALF:(c + 1) * HALF],
                                 start=True, stop=True).then_inc(misc_for_dve, 1)

            def average():
                nc.tensor.matmul(misc[:, 0:2], gmat[:, :], st2[:, :], start=True, stop=True).then_inc(misc_for_dve, 1)

            def split_product(to, stationary, moving, start=True, stop=True):
                pairs = ((HI, HI), (HI, LO), (LO, HI))
                for n, (a, b) in enumerate(pairs):
                    last = nc.tensor.matmul(to, stationary(a), moving(b), start=start and n == 0,
                                            stop=stop and n == len(pairs) - 1)
                return last

            def scores(par, n):
                tile = n % TILES
                for c in range(2):
                    last = split_product(s_ps[n % 2][:, c, :],
                                         lambda part: q[par][:, part, tile * P:(tile + 1) * P],
                                         lambda part: k[par][:, part, c * HALF:(c + 1) * HALF])
                last.then_inc(s_ready, 1)

            def products(half, quarter):
                for st in (2 * quarter, 2 * quarter + 1):
                    last = split_product(pv_ps[:, :], lambda part: vT[half // 2 % 2][:, part, st, :],
                                         lambda part: pT[half % 2][:, part, st, :],
                                         start=(st == 0), stop=(st == TILES - 1))
                if quarter == 3:
                    last.then_inc(pv_ready, 1)

            pe.sem_inc(t_free, 2)
            pe.sem_inc(misc_dve, 1)
            pe.sem_inc(pv_free, 2)
            pe.wait_ge(kq_parts, 4)
            scores(0, 0)
            scores(0, 1)
            pe.sem_inc(kq_parts, -3)
            pe.wait_ge(consts, 1)

            def body(first=False, last=False):
                places, _, before, taken = shared_bank(first, last)
                for m in range(BODY):
                    u, tile = m // TILES, m % TILES

                    def in_shared_bank(place):
                        name = places[u].get((tile, place))
                        if name is None:
                            return
                        reader, count = before[u, name]
                        pe.wait_ge(misc_act if reader == "act" else misc_dve, count)
                        if name == "avg":
                            pe.wait_ge(stats_ready, u + 1)
                            pe.wait_ge(w_dma[1 - u], 16)
                            combine_weights(nc, misc, wg[1 - u])
                            average()
                        elif name == "o0":
                            pe.wait_ge(attn_ready, 1)
                            project_output(0)
                        elif name == "o1":
                            project_output(1)
                        elif name[0] == "v":
                            project_values(int(name[1]))
                        else:
                            if name == "k0":
                                pe.wait_ge(h_ready, u + 1)
                            project(1 - u, int(name[1]), W_K if name[0] == "k" else W_Q)

                    pe.wait_ge(p_ready, m + 1)
                    if tile == 2:
                        pe.wait_ge(kq_parts, 4 * u + 1)
                    if tile == TILES - 2 and not (last and u == 1):
                        pe.wait_ge(kq_parts, 4 * u + 4)
                    if not (last and m >= BODY - 2):
                        scores((m + 2) // TILES % 2, m + 2)
                    in_shared_bank(0)
                    for bank in range(2):
                        pe.wait_ge(t_free, 2 * m + bank + 1)
                        for n in range(HT):
                            st = bank * HT + n
                            transposed = nc.tensor.transpose(t_ps[bank][:, n, :], probs[m % 2][:, st * P:(st + 1) * P], ident[:, :])
                        transposed.then_inc(t_ready, 1)
                    in_shared_bank(1)
                    if m >= HT or not first:
                        if m % HT == 0:
                            pe.wait_ge(pv_free, m // HT + 1)
                        if tile == HT:
                            pe.wait_ge(v_parts, 2 * (u + 1))
                        products((m // HT + 3) % 4, m % HT)
                    in_shared_bank(2)
                pe.sem_inc(t_free, -2 * BODY)
                pe.sem_inc(pv_free, -4)
                pe.sem_inc(misc_dve, -taken["dve"])
                pe.sem_inc(misc_act, -taken["act"])
                if not last:
                    pe.sem_inc(p_ready, -BODY)
                    pe.sem_inc(kq_parts, -8)
                    pe.sem_inc(v_parts, -4)
                    pe.sem_inc(stats_ready, -2)
                    pe.sem_inc(h_ready, -2)
                    pe.sem_inc(w_dma[0], -16)
                    pe.sem_inc(w_dma[1], -16)

            body(first=True)
            with pe.Fori(1, PAIRS - 1):
                body()
            body(last=True)
            pe.wait_ge(t_free, 2)
            pe.wait_ge(pv_free, 1)
            for quarter in range(4):
                products(3, quarter)


def layout(inputs):
    import numpy as np

    def column(a):
        return np.asarray(a).reshape(P, 1)

    stack, rows = [], []
    for gamma, beta, qkv_w, qkv_b, proj_w, proj_b in (
        ("L0_conv_gn_w", "L0_conv_gn_b", "L0_conv_qkv_w", "L0_conv_qkv_b", "L0_conv_proj_w", "L0_conv_proj_b"),
        ("L1_conv_gamma", "L1_conv_beta", "L1_conv_w_qkv", "L1_conv_b_qkv", "L1_conv_w_proj", "L1_conv_b_proj"),
    ):
        wqkv = np.asarray(inputs[qkv_w]).reshape(HEADS, 3, CH, P)
        bqkv = np.asarray(inputs[qkv_b]).reshape(HEADS, 3, CH)
        wq, wk = (wqkv[:, n].transpose(2, 1, 0).reshape(P, P) for n in (0, 1))
        wv = wqkv[:, 2].transpose(2, 0, 1).reshape(P, P)
        bq, bk = (bqkv[:, n].transpose(1, 0).reshape(P, 1) for n in (0, 1))
        stack.append(np.concatenate([wq, wk, wv, column(inputs[gamma]), column(inputs[beta]), bq, bk,
                                     np.asarray(inputs[proj_w]).T, column(inputs[proj_b]),
                                     bqkv[:, 2].reshape(P, 1)], axis=1))
        rows.append(bqkv[:, 2].reshape(1, P))
    for names in (
        ("L2_conv_wq", "L2_conv_wk", "L2_conv_wv", "L2_conv_gn_gamma", "L2_conv_gn_beta", "L2_conv_bq", "L2_conv_bk",
         "L2_conv_wp", "L2_conv_bp", "L2_conv_bv"),
        ("L3_conv_wq", "L3_conv_wk", "L3_conv_wv", "L3_conv_gamma", "L3_conv_beta", "L3_conv_bq", "L3_conv_bk",
         "L3_conv_wo", "L3_conv_bo", "L3_conv_bv"),
    ):
        a = [np.asarray(inputs[n]) for n in names]
        a[2] = a[2].T
        stack.append(np.concatenate([m.T if m.ndim == 2 else column(m) for m in a], axis=1))
        rows.append(a[-1].reshape(1, P))
    return np.stack(stack), np.stack(rows)


def keep(nc, ctx):
    def sb(name, shape, dt=F32):
        return ctx.enter_context(nc.sbuf_tensor(name, shape, dt))

    kept = {
        "full": {name: sb(f"full_{name}", [P, T]) for name in ("q", "k", "v")},
        "av": [sb(f"av{i}", [P, T]) for i in range(2)],
        "num": sb("num", [P, T]),
        "den": sb("den", [P, HEADS * T // P]),
        "rden": sb("rden", [P, HEADS * T // P]),
        "rrep": sb("rrep", [P, T]),
        "attn": sb("attn", [P, T]),
        "x_res": sb("x_res", [P, T]),
        "wo": sb("wo", [P, NO]),
        "value_weights": sb("value_weights", [P, 2 * P]),
        "gmat": sb("gmat", [P, P]),
        "ident": sb("ident", [P, P], BF16),
        "exponent": sb("exponent", [P, 1]),
        "den_dram": nc.dram_tensor("den_dram", (HEADS, T), F32).ap(),
        "rden_dram": nc.dram_tensor("rden_dram", (HEADS, T), F32).ap(),
    }

    def gather(sp, quad, done):
        rows = kept["av"][quad]
        sp.dma_start(kept["den_dram"][quad * QUAD:(quad + 1) * QUAD, :], rows[CH:P:32, :]).then_inc(done, 16)
        for j in range(QUAD):
            to = (quad * QUAD + j) * CH
            sp.dma_start(kept["num"][to:to + CH, :], rows[32 * j:32 * j + CH, :]).then_inc(done, 16)

    kept["gather"] = gather
    return kept


def program(nc, x, w, bv, out):
    with ExitStack() as ctx:
        kept = keep(nc, ctx)
        many_heads(nc, ctx, kept, x, w, bv, out)
        one_head(nc, ctx, kept, w, out)


def kernel(**inputs):
    import numpy as np
    import concourse.bacc as bacc
    from concourse.bass_utils import run_bass_kernel_spmd

    x = np.ascontiguousarray(np.asarray(inputs["x"]).reshape(B, P, T))
    w, bv = layout(inputs)
    arrays = {"x_dram": x, "w_dram": w, "bv_dram": bv}
    nc = bacc.Bacc("TRN2", target_bir_lowering=False, num_devices=1)
    args = [nc.dram_tensor(name, a.shape, F32, kind="ExternalInput").ap() for name, a in arrays.items()]
    out = nc.dram_tensor("out_dram", (B, P, T), F32, kind="ExternalOutput").ap()
    program(nc, *args, out)
    result = run_bass_kernel_spmd(nc, [arrays], core_ids=[0])
    return result.results[0]["out_dram"].reshape(np.asarray(inputs["x"]).shape)
```
